# Optimizing a Trainium2 kernel written in Bass

```python
import numpy as np
import jax
import jax.numpy as jnp

def _softmax(x, axis=-1):
    return jax.nn.softmax(x, axis=axis)

def _gelu(x):
    return jax.nn.gelu(x, approximate=True)

def _silu(x):
    return jax.nn.silu(x)

def _sigmoid(x):
    return jax.nn.sigmoid(x)

def _layernorm(x, axis=-1, eps=1e-05):
    m = jnp.mean(x, axis=axis, keepdims=True)
    v = jnp.var(x, axis=axis, keepdims=True)
    return (x - m) / jnp.sqrt(v + eps)

def _scatter_add(tgt, idx, src, axis=0):
    return tgt.at[idx].add(src)

def _segment_sum(src, seg, n):
    return jax.ops.segment_sum(src, seg, n)
kernel_name = 'mk_xattn_ffn_d2_seqx_r8_34f4f8'

def setup_inputs(seed: int=0):
    np.random.seed(seed)
    _w = jnp.asarray

    def _rec_inputs():
        import jax
        import jax.numpy as jnp
        _rk = jax.random.key(seed)
        x = 7.22e-05 + 1 * jax.random.normal(jax.random.fold_in(_rk, 1), (64, 64, 256), jnp.float32)
        _lenS = 64 - jax.random.randint(jax.random.fold_in(_rk, 7), (64,), 0, max(1, 64 // 4) + 1, jnp.int32)
        _lenS2 = 64 - jax.random.randint(jax.random.fold_in(_rk, 8), (64,), 0, max(1, 64 // 4) + 1, jnp.int32)
        _ctx_2048P = jax.random.normal(jax.random.fold_in(_rk, 11), (64, 16, 256), jnp.float32)
        _ctx_2048c = jax.random.dirichlet(jax.random.fold_in(_rk, 511), 0.3 * jnp.ones((16,), jnp.float32), (64, 64))
        _ctx_2048t = jnp.einsum('bsk,bkd->bsd', _ctx_2048c, _ctx_2048P)
        _ctx_2048t = _ctx_2048t * jax.lax.rsqrt(jnp.mean(jnp.square(_ctx_2048t)) + 1e-12) * 0.953939
        ctx_2048 = 4.13588e-05 + 0.999923 * (_ctx_2048t + 0.3 * jax.random.normal(jax.random.fold_in(_rk, 611), (64, 64, 256), jnp.float32))
        return (x, ctx_2048)
    x, ctx_2048 = _rec_inputs()

    def _L0_xattn_setup():
        import jax, jax.numpy as jnp
        import numpy as np
        N, E, T, H = (8, 64, 256, 8)
        key = jax.random.key(seed)
        ks = jax.random.split(key, 6)
        s = 1.0 / np.sqrt(E)
        return {'mask': jax.random.normal(ks[0], (N, E, T), jnp.float32), 'encodings': jax.random.normal(ks[1], (N, E, T), jnp.float32), 'w_in': jax.random.normal(ks[2], (3 * E, E), jnp.float32) * s, 'b_in': jnp.zeros((3 * E,), jnp.float32), 'w_out': jax.random.normal(ks[3], (E, E), jnp.float32) * s, 'b_out': jnp.zeros((E,), jnp.float32), 'w_ct': jax.random.normal(ks[4], (E, E), jnp.float32) * s, 'b_ct': jnp.zeros((E,), jnp.float32), 'local_size': 64}
    _L0_xattn_all = _L0_xattn_setup()
    _L0_xattn_in = {k: v for k, v in _L0_xattn_all.items() if k in ('w_in', 'b_in', 'w_out', 'b_out', 'w_ct', 'b_ct')}
    del _L0_xattn_all

    def _L0_ffn_setup():
        import jax, jax.numpy as jnp
        import numpy as np
        EPS = 1e-07
        CURVATURE = 1.0
        MAX_NORM_RATIO = 0.99
        B, L, N, K = (4, 256, 256, 256)

        def _ternary_init(key, n, k):
            rand = jax.random.normal(key, (n, k), dtype=jnp.float32)
            threshold = 0.5 * jnp.mean(jnp.abs(rand))
            return jnp.where(rand > threshold, 1.0, jnp.where(rand < -threshold, -1.0, 0.0)).astype(jnp.float32)
        key = jax.random.key(seed)
        kx, kw = jax.random.split(key)
        x = jax.random.normal(kx, (B, L, N), dtype=jnp.float32)
        weight = _ternary_init(kw, N, K)
        scale = jnp.full((K,), 1.0 / np.sqrt(N), dtype=jnp.float32)
        return {'x': x, 'weight': weight, 'scale': scale}
    _L0_ffn_all = _L0_ffn_setup()
    _L0_ffn_in = {k: v for k, v in _L0_ffn_all.items() if k in ('weight', 'scale')}
    del _L0_ffn_all

    def _L1_xattn_setup():
        import math
        import jax, jax.numpy as jnp
        import numpy as np
        N_HEADS = 8
        CHANNELS = 64
        K_CH = CHANNELS // N_HEADS
        THETA = 10000.0

        def _rope_freqs(length, dim):
            inv_freq = 1.0 / THETA ** (jnp.arange(0, dim, 2, dtype=jnp.float32) / dim)
            f = jnp.arange(length, dtype=jnp.float32)[:, None] * inv_freq[None, :]
            return jnp.concatenate([f, f], axis=-1)

        def _apply_rotary(pos, t):
            half = t.shape[-1] // 2
            rot = jnp.concatenate([-t[..., half:], t[..., :half]], axis=-1)
            return t * jnp.cos(pos) + rot * jnp.sin(pos)

        def _proj(inp, W, b):
            return jnp.einsum('oc,bct->bot', W, inp) + b[None, :, None]
        key = jax.random.key(seed)
        ks = jax.random.split(key, 10)
        B, C, T = (4, CHANNELS, 256)
        bound = math.sqrt(6.0 / (C + C))

        def w(k):
            return jax.random.uniform(k, (C, C), jnp.float32, -bound, bound)
        return {'x': jax.random.normal(ks[0], (B, C, T), jnp.float32), 'c': jax.random.normal(ks[1], (B, C, T), jnp.float32), 'Wq': w(ks[2]), 'bq': jnp.zeros((C,), jnp.float32), 'Wk': w(ks[3]), 'bk': jnp.zeros((C,), jnp.float32), 'Wv': w(ks[4]), 'bv': jnp.zeros((C,), jnp.float32), 'Wo': w(ks[5]), 'bo': jnp.zeros((C,), jnp.float32)}
    _L1_xattn_all = _L1_xattn_setup()
    _L1_xattn_in = {k: v for k, v in _L1_xattn_all.items() if k in ('Wq', 'bq', 'Wk', 'bk', 'Wv', 'bv', 'Wo', 'bo')}
    del _L1_xattn_all

    def _L1_ffn_setup():
        import jax, jax.numpy as jnp
        import numpy as np
        BLOCK = 64

        def dequant4bit(q, scale):
            return (q.astype(jnp.float32) - 7.5) * jnp.repeat(scale, BLOCK, axis=1)
        key = jax.random.key(seed)
        ks = jax.random.split(key, 11)
        B, S, D, H, R = (4, 256, 256, 1024, 16)
        return {'x1': jax.random.normal(ks[0], (B, S, D), jnp.float32), 'w_up_q': jax.random.randint(ks[1], (H, D), 0, 16, dtype=jnp.int32), 'w_up_scale': jax.random.uniform(ks[2], (H, D // BLOCK), jnp.float32) * 0.02, 'b_up': jax.random.normal(ks[3], (H,), jnp.float32) * 0.01, 'w_up_lora_a': jax.random.normal(ks[4], (D, R), jnp.float32) * 0.02, 'w_up_lora_b': jax.random.normal(ks[5], (R, H), jnp.float32) * 0.02, 'w_down_q': jax.random.randint(ks[6], (D, H), 0, 16, dtype=jnp.int32), 'w_down_scale': jax.random.uniform(ks[7], (D, H // BLOCK), jnp.float32) * 0.02, 'b_down': jax.random.normal(ks[8], (D,), jnp.float32) * 0.01, 'w_down_lora_a': jax.random.normal(ks[9], (H, R), jnp.float32) * 0.02, 'w_down_lora_b': jax.random.normal(ks[10], (R, D), jnp.float32) * 0.02}
    _L1_ffn_all = _L1_ffn_setup()
    _L1_ffn_in = {k: v for k, v in _L1_ffn_all.items() if k in ('w_up_q', 'w_up_scale', 'b_up', 'w_up_lora_a', 'w_up_lora_b', 'w_down_q', 'w_down_scale', 'b_down', 'w_down_lora_a', 'w_down_lora_b')}
    del _L1_ffn_all
    return {'x': x, 'ctx_2048': ctx_2048, 'L0_xattn_w_in': _L0_xattn_in['w_in'], 'L0_xattn_b_in': _L0_xattn_in['b_in'], 'L0_xattn_w_out': _L0_xattn_in['w_out'], 'L0_xattn_b_out': _L0_xattn_in['b_out'], 'L0_xattn_w_ct': _L0_xattn_in['w_ct'], 'L0_xattn_b_ct': _L0_xattn_in['b_ct'], 'L0_ffn_weight': _L0_ffn_in['weight'], 'L0_ffn_scale': _L0_ffn_in['scale'], 'L1_xattn_Wq': _L1_xattn_in['Wq'], 'L1_xattn_bq': _L1_xattn_in['bq'], 'L1_xattn_Wk': _L1_xattn_in['Wk'], 'L1_xattn_bk': _L1_xattn_in['bk'], 'L1_xattn_Wv': _L1_xattn_in['Wv'], 'L1_xattn_bv': _L1_xattn_in['bv'], 'L1_xattn_Wo': _L1_xattn_in['Wo'], 'L1_xattn_bo': _L1_xattn_in['bo'], 'L1_ffn_w_up_q': _L1_ffn_in['w_up_q'], 'L1_ffn_w_up_scale': _L1_ffn_in['w_up_scale'], 'L1_ffn_b_up': _L1_ffn_in['b_up'], 'L1_ffn_w_up_lora_a': _L1_ffn_in['w_up_lora_a'], 'L1_ffn_w_up_lora_b': _L1_ffn_in['w_up_lora_b'], 'L1_ffn_w_down_q': _L1_ffn_in['w_down_q'], 'L1_ffn_w_down_scale': _L1_ffn_in['w_down_scale'], 'L1_ffn_b_down': _L1_ffn_in['b_down'], 'L1_ffn_w_down_lora_a': _L1_ffn_in['w_down_lora_a'], 'L1_ffn_w_down_lora_b': _L1_ffn_in['w_down_lora_b']}

def reference(x, ctx_2048, L0_xattn_w_in, L0_xattn_b_in, L0_xattn_w_out, L0_xattn_b_out, L0_xattn_w_ct, L0_xattn_b_ct, L0_ffn_weight, L0_ffn_scale, L1_xattn_Wq, L1_xattn_bq, L1_xattn_Wk, L1_xattn_bk, L1_xattn_Wv, L1_xattn_bv, L1_xattn_Wo, L1_xattn_bo, L1_ffn_w_up_q, L1_ffn_w_up_scale, L1_ffn_b_up, L1_ffn_w_up_lora_a, L1_ffn_w_up_lora_b, L1_ffn_w_down_q, L1_ffn_w_down_scale, L1_ffn_b_down, L1_ffn_w_down_lora_a, L1_ffn_w_down_lora_b):
    import jax
    import jax.numpy as jnp

    def _L0_xattn_ref(mask, encodings, w_in, b_in, w_out, b_out, w_ct, b_ct, local_size):
        import jax, jax.numpy as jnp
        import numpy as np
        N, E, T, H = (8, 64, 256, 8)
        n, e, t = mask.shape
        d = e // H
        x = jnp.transpose(mask, (0, 2, 1))
        qkv = x @ w_in.T + b_in
        q, k, v = jnp.split(qkv, 3, axis=-1)
        q = q.reshape(n, t, H, d)
        k = k.reshape(n, t, H, d)
        v = v.reshape(n, t, H, d)
        scores = jnp.einsum('bqhd,bkhd->bhqk', q, k) / jnp.sqrt(jnp.asarray(d, q.dtype))
        idx = jnp.arange(t)
        band = jnp.abs(idx[:, None] - idx[None, :]) <= local_size
        neg = jnp.asarray(jnp.finfo(scores.dtype).min, scores.dtype)
        scores = jnp.where(band[None, None], scores, neg)
        attn = jax.nn.softmax(scores, axis=-1)
        o = jnp.einsum('bhqk,bkhd->bqhd', attn, v).reshape(n, t, e)
        o = o @ w_out.T + b_out
        o = jnp.transpose(o, (0, 2, 1))
        y = jax.nn.relu(o) * encodings
        out = jnp.einsum('nit,io->not', y, w_ct) + b_ct[None, :, None]
        return out

    def _L0_ffn_ref(x, weight, scale):
        import jax, jax.numpy as jnp
        import numpy as np
        EPS = 1e-07
        CURVATURE = 1.0
        MAX_NORM_RATIO = 0.99
        B, L, N, K = (4, 256, 256, 256)

        def _ternary_init(key, n, k):
            rand = jax.random.normal(key, (n, k), dtype=jnp.float32)
            threshold = 0.5 * jnp.mean(jnp.abs(rand))
            return jnp.where(rand > threshold, 1.0, jnp.where(rand < -threshold, -1.0, 0.0)).astype(jnp.float32)
        sqrt_c = jnp.sqrt(jnp.float32(CURVATURE))
        out = jnp.einsum('bln,nk->blk', x, weight) * scale
        v_norm = jnp.maximum(jnp.linalg.norm(out, axis=-1, keepdims=True), EPS)
        scaled_norm = sqrt_c * v_norm
        out = out * (jnp.tanh(scaled_norm) / (scaled_norm + EPS))
        max_norm = MAX_NORM_RATIO / sqrt_c
        o_norm = jnp.maximum(jnp.linalg.norm(out, axis=-1, keepdims=True), EPS)
        out = out * jnp.minimum(max_norm / o_norm, 1.0)
        return out.astype(x.dtype)

    def _L1_xattn_ref(x, c, Wq, bq, Wk, bk, Wv, bv, Wo, bo):
        import math
        import jax, jax.numpy as jnp
        import numpy as np
        N_HEADS = 8
        CHANNELS = 64
        K_CH = CHANNELS // N_HEADS
        THETA = 10000.0

        def _rope_freqs(length, dim):
            inv_freq = 1.0 / THETA ** (jnp.arange(0, dim, 2, dtype=jnp.float32) / dim)
            f = jnp.arange(length, dtype=jnp.float32)[:, None] * inv_freq[None, :]
            return jnp.concatenate([f, f], axis=-1)

        def _apply_rotary(pos, t):
            half = t.shape[-1] // 2
            rot = jnp.concatenate([-t[..., half:], t[..., :half]], axis=-1)
            return t * jnp.cos(pos) + rot * jnp.sin(pos)

        def _proj(inp, W, b):
            return jnp.einsum('oc,bct->bot', W, inp) + b[None, :, None]
        b, _, t_t = x.shape
        t_s = c.shape[2]
        q_emb = _rope_freqs(t_t, K_CH)
        k_emb = _rope_freqs(t_s, K_CH)

        def split_heads(t):
            return t.reshape(b, N_HEADS, K_CH, t.shape[2]).transpose(0, 1, 3, 2)
        q = split_heads(_proj(x, Wq, bq))
        k = split_heads(_proj(c, Wk, bk))
        v = split_heads(_proj(c, Wv, bv))
        q = _apply_rotary(q_emb, q)
        k = _apply_rotary(k_emb, k)
        scores = jnp.einsum('bhtc,bhsc->bhts', q, k) / math.sqrt(K_CH)
        p_attn = jax.nn.softmax(scores, axis=-1)
        out = jnp.einsum('bhts,bhsc->bhtc', p_attn, v)
        out = out.transpose(0, 1, 3, 2).reshape(b, N_HEADS * K_CH, t_t)
        return _proj(out, Wo, bo)

    def _L1_ffn_ref(x1, w_up_q, w_up_scale, b_up, w_up_lora_a, w_up_lora_b, w_down_q, w_down_scale, b_down, w_down_lora_a, w_down_lora_b):
        import jax, jax.numpy as jnp
        import numpy as np
        BLOCK = 64

        def dequant4bit(q, scale):
            return (q.astype(jnp.float32) - 7.5) * jnp.repeat(scale, BLOCK, axis=1)
        w_up = dequant4bit(w_up_q, w_up_scale).T
        y1 = x1 @ w_up + b_up + x1 @ w_up_lora_a @ w_up_lora_b
        x2 = jax.nn.relu(y1)
        w_down = dequant4bit(w_down_q, w_down_scale).T
        y2 = x2 @ w_down + b_down + x2 @ w_down_lora_a @ w_down_lora_b
        return y2
    x = x + _L0_xattn_ref(_layernorm(x, axis=-1), ctx_2048, L0_xattn_w_in, L0_xattn_b_in, L0_xattn_w_out, L0_xattn_b_out, L0_xattn_w_ct, L0_xattn_b_ct, 64)
    x = x + _L0_ffn_ref(_layernorm(x, axis=-1), L0_ffn_weight, L0_ffn_scale)
    x = x + _L1_xattn_ref(_layernorm(x, axis=-1), ctx_2048, L1_xattn_Wq, L1_xattn_bq, L1_xattn_Wk, L1_xattn_bk, L1_xattn_Wv, L1_xattn_bv, L1_xattn_Wo, L1_xattn_bo)
    x = x + _L1_ffn_ref(_layernorm(x, axis=-1), L1_ffn_w_up_q, L1_ffn_w_up_scale, L1_ffn_b_up, L1_ffn_w_up_lora_a, L1_ffn_w_up_lora_b, L1_ffn_w_down_q, L1_ffn_w_down_scale, L1_ffn_b_down, L1_ffn_w_down_lora_a, L1_ffn_w_down_lora_b)
    return x

_drawn_inputs = setup_inputs


def setup_inputs(seed=0):
    import zlib

    import numpy as np

    out = dict(_drawn_inputs(seed))
    spreads = {'L0_xattn_b_in': (0.0, 0.1),
     'L0_xattn_b_out': (0.0, 0.1),
     'L0_xattn_b_ct': (0.0, 0.1),
     'L0_ffn_scale': (0.0625, 0.6),
     'L1_xattn_bq': (0.0, 0.402),
     'L1_xattn_bk': (0.0, 0.752),
     'L1_xattn_bv': (0.0, 0.1),
     'L1_xattn_bo': (0.0, 0.1)}
    factors = {'L1_ffn_b_up': 7.69,
     'L1_ffn_w_up_lora_a': 2.753,
     'L1_ffn_w_up_lora_b': 2.75,
     'L1_ffn_b_down': 8.0,
     'L1_ffn_w_down_lora_a': 2.802,
     'L1_ffn_w_down_lora_b': 2.882}
    for name, (base, spread) in spreads.items():
        noise = np.random.default_rng([zlib.crc32(name.encode()), seed]).standard_normal(out[name].shape)
        drawn = base * np.exp(spread * noise) if base else spread * noise
        out[name] = jnp.asarray(drawn.astype(out[name].dtype))
    for name, factor in factors.items():
        out[name] = (out[name] * factor).astype(out[name].dtype)
    return out
```

```python
import concourse.bass as bass
from concourse import mybir
from contextlib import ExitStack

BATCH = 64
CH = 64
T = 256
HEADS = 8
HD = CH // HEADS
BAND = 64
FF = 1024
RANK = 16
QBLOCK = 64
P = 128
PAIRS = BATCH // 2
HPP = 2 * HEADS
PARTS = 3
SPLIT_ROWS = PARTS * PARTS * HD
SHIFT_ROW = 96
LN_EPS = 1e-5
FFN_EPS = 1e-7
MAX_NORM = 0.99
OUTSIDE = -1.0e30
WIN = T // 2 + BAND
RING = 3
VALUES_AT = (3, 2)
AHEAD = 3
COPY_ROW = 72


def at(r, k, ring=RING):
    i, u = r
    t = u + k
    return (i + t // ring, t % ring)


def num(r, ring=RING):
    return r[0] * ring + r[1]


def active(r, ring=RING):
    return not isinstance(r[0], int) or 0 <= num(r, ring) < PAIRS


JOBS = {
    "A": [("q", AHEAD), ("heads1", -1), ("v", 2), ("max0", 1), ("heads0", 0)],
    "B": [("max1", 0), ("k", AHEAD), ("back", -1), ("out", -1), ("mix", -1)],
}
FIRST_FULL, LAST_FULL = 1, PAIRS - 1 - AHEAD


def job_order(layer, bank, name, pair):
    jobs = [j for j in JOBS[bank] if layer == 0 or j[0] != "mix"]
    place = [j[0] for j in jobs].index(name)
    r = at(pair, -jobs[place][1])
    if isinstance(r[0], int):
        if not active(pair):
            return None
        n = sum(0 <= q + d < PAIRS for q in range(-AHEAD, num(r)) for _, d in jobs)
        return n + sum(0 <= num(r) + d < PAIRS for _, d in jobs[:place])
    before = sum(0 <= q + d < PAIRS for q in range(-AHEAD, FIRST_FULL) for _, d in jobs)
    return num(r) * len(jobs) + (before - FIRST_FULL * len(jobs) + place)


def build(nc, a, out):
    fp32 = mybir.dt.float32
    bf16 = mybir.dt.bfloat16
    i32 = mybir.dt.int32
    ALU = mybir.AluOpType
    ACT = mybir.ActivationFunctionType
    AX = mybir.AxisListType

    x_dram = a["x"].rearrange("(n b) c t -> (b c) n t", b=2)
    ctx_dram = a["ctx"].rearrange("(n b) c t -> n (b c) t", b=2)
    out_dram = out.rearrange("(n b) c t -> (b c) n t", b=2)

    stack = ExitStack()
    with stack:
        def sb(name, shape, dt=fp32):
            return stack.enter_context(nc.sbuf_tensor(name, shape, dt))

        def sem(name):
            return stack.enter_context(nc.semaphore(name))

        X = sb("X", [P, PAIRS, T])
        ident = sb("ident", [P, P])
        ident16 = sb("ident16", [P, P], bf16)
        band16 = sb("band16", [P, 2 * WIN], bf16)
        rope = sb("rope", [P, 2, T])
        att_w = [sb("att_w0", [P, 5, P]), sb("att_w1", [P, 6, P])]
        att_b = [sb("att_b0", [P, 5]), sb("att_b1", [P, 6])]
        out_bias = sb("out_bias", [P, 2])
        ff0_w = sb("ff0_w", [P, 2, T])
        ff0_scale = sb("ff0_scale", [P, T])
        up_w = sb("up_w", [P, 2, FF])
        down_w = sb("down_w", [P, FF // P, T])
        up_b = sb("up_b", [P, FF // P])
        down_b = sb("down_b", [P, T])
        up_scale = sb("up_scale", [P, FF // P, T // QBLOCK])
        down_scale = sb("down_scale", [P, 2, FF // QBLOCK])
        stats = sb("stats", [P, PAIRS, 6])
        mean = sb("mean", [P, PAIRS])
        var = sb("var", [P, PAIRS])
        rstd = sb("rstd", [P, PAIRS])
        tmp = sb("tmp", [P, 4, PAIRS])
        sumsq = sb("sumsq", [P, PAIRS])
        gain = sb("gain", [P, PAIRS])
        Qs = sb("Qs", [P, RING, HPP, T], bf16)
        Ks = sb("Ks", [P, RING, HPP, T], bf16)
        probs = sb("probs", [P, 8, 2 * T])
        V = sb("V", [P, RING, 2, HPP, 32])
        xn = sb("xn", [P, RING, T])
        side = sb("side", [P, RING, T])
        Qp = sb("Qp", [P, RING, PARTS, T], bf16)
        Kp = sb("Kp", [P, RING, PARTS, T], bf16)
        q_rest = sb("q_rest", [P, RING, T])
        k_rest = sb("k_rest", [P, RING, T])
        rot = sb("rot", [P, 4, T])
        row_max = sb("row_max", [P, RING, HPP, 2])
        max_parts = sb("max_parts", [P, 2, PARTS, HPP], bf16)
        max_rest = sb("max_rest", [P, 2, HPP])
        max_rows = sb("max_rows", [PARTS * HPP, 2, P], bf16)
        heads_sb = sb("heads_sb", [P, 2, 2 * T])
        rcp = sb("rcp", [P, 2, HPP])
        normed = sb("normed", [P, RING, 2, P])
        mixed_in = sb("mixed_in", [P, T])
        relu_out = rot[:, 0, :]
        gated = rot[:, 1, :]
        band_raw = rot[:, :, :].rearrange("p a t -> p (a t)")[:, 0:2 * WIN]
        ff = sb("ff", [P, PAIRS, T])
        junk = rot[:, 2:4, :]
        ff0_xT = heads_sb
        xT = (Ks[:, 0:2, :, :].rearrange("p a h t -> p (a h t)").bitcast(fp32)[:, 0:4 * T * 2]
              .rearrange("p (a b t) -> p a b t", a=2, b=2))
        up_raw = ff[:, 0:FF // P, :].bitcast(i32)
        down_raw = ff[:, FF // P:2 * FF // P, :].rearrange("p (a b) t -> p a (b t)", a=2).bitcast(i32)
        lora = probs[0:RANK, :, :].rearrange("p h t -> p (h t)")
        lora_in = lora[:, 0:T + FF]
        lora_out = lora[:, T + FF:2 * (T + FF)]
        up_f = ff[:, 2 * FF // P:3 * FF // P, :]
        down_f = ff[:, 3 * FF // P:4 * FF // P, :].rearrange("p (a b) t -> p a (b t)", a=2)
        hidden = [probs, Qs[:, 0:2, :, :].rearrange("p a h t -> p (a h t)").bitcast(fp32)
                  .rearrange("p (h t) -> p h t", h=FF // P)]

        bank = [stack.enter_context(nc.psum_tensor(f"bank{n}", [P, 512], fp32)) for n in range(8)]
        score_bank, exp_bank, pv_bank = bank[0:2], bank[2:4], bank[4:6]
        job_bank = {"A": bank[6], "B": bank[7]}
        max_bank = {b: job_bank[b][0:PARTS * HPP, 0:P // 2].bitcast(bf16) for b in "AB"}

        passed = sem("passed")
        consts_in = sem("consts_in")
        rounded = sem("rounded")
        x_in = sem("x_in")
        ffn_in = sem("ffn_in")
        stored = sem("stored")
        cleared = sem("cleared")
        prep_ps = sem("prep_ps")
        prep_read = sem("prep_read")
        dequant = sem("dequant")
        ln_vec = sem("ln_vec")
        ln_var = sem("ln_var")
        ln_std = sem("ln_std")
        ln_ready = sem("ln_ready")
        L = []
        for l in range(2):
            L.append({n: sem(f"L{l}_{n}") for n in (
                "xn_ready", "side_in0", "side_in1", "side_in2", "A_filled", "A_read", "B_filled", "B_read", "q_high", "k_high",
                "q_mid", "k_mid", "q_parts", "k_parts", "rot_mul", "rot_sum", "q_in0", "q_in1", "q_in2", "k_in0", "k_in1", "k_in2",
                "stack_in0", "stack_in1", "stack_in2", "scored", "maxed", "max_step0", "max_step1", "max_parts0", "max_parts1", "max_in0", "max_in1", "shifted", "exped",
                "masked", "mask_step", "pv_done", "heads_out", "rcp_done", "mixed", "relued", "gated")})
        f_xn = sem("f_xn")
        f_xT = sem("f_xT")
        f_xTs = sem("f_xTs")
        f_mm = sem("f_mm")
        f_sq = sem("f_sq")
        f_keep = sem("f_keep")
        f_norm = sem("f_norm")
        f_root = sem("f_root")
        f_tanh = sem("f_tanh")
        f_step = sem("f_step")
        f_upd = sem("f_upd")
        g_xn = sem("g_xn")
        g_xT = sem("g_xT")
        g_xTs = sem("g_xTs")
        g_bias = sem("g_bias")
        g_up = sem("g_up")
        g_relu = sem("g_relu")
        g_down = sem("g_down")
        g_upd = sem("g_upd")

        SCALE = float(HD) ** -0.5
        win_of = [WIN, T]
        start_of = [lambda blk: blk * BAND, lambda blk: 0]
        STACK_IN = PARTS * 16
        CONSTS = 7
        JOBS_B = (len(JOBS["B"]) * PAIRS, (len(JOBS["B"]) - 1) * PAIRS)
        CHUNK = 4
        HB = FF // P

        def iterations(e, body):
            for r in range(-AHEAD, RING):
                body((r // RING, r % RING))
            with e.Fori(1, (LAST_FULL + 1) // RING) as i:
                for u in range(RING):
                    body((i, u))
            for r in range((LAST_FULL + 1) // RING * RING, PAIRS + 1):
                body((r // RING, r % RING))

        def wait_job(e, s, l, b, name, pair, what):
            n = job_order(l, b, name, pair)
            if n is not None:
                e.wait_ge(s[f"{b}_{what}"], n + 1)

        def wait_bank(e, s, l, b, name, pair):
            n = job_order(l, b, name, pair)
            if not (isinstance(n, int) and n == 0):
                e.wait_ge(s[f"{b}_read"], n)

        def wait_some(e, s, value):
            if not (isinstance(value, int) and value <= 0):
                e.wait_ge(s, value)

        def wait_apart(e, *waits):
            for w, v in waits:
                if v is not None and not (isinstance(v, int) and v <= 0):
                    e.wait_ge(w, v)
                    if not isinstance(v, int):
                        e.sem_inc(passed, 1)

        def job_wait(s, l, b, name, pair, what):
            n = job_order(l, b, name, pair)
            return s[f"{b}_{what}"], None if n is None else n + 1

        block = stack.enter_context(nc.Block())

        def sync_attention(e, l):
            s = L[l]
            q_stack, k_stack = Qs[:, :, :, :].tensor, Ks[:, :, :, :].tensor

            def load_side(pair):
                if not active(pair):
                    return
                if l == 0:
                    wait_apart(e, (s["gated"], num(pair) - RING + 1))
                else:
                    wait_apart(e, job_wait(s, l, "A", "v", at(pair, -RING), "filled"))
                e.dma_start(side[:, pair[1], :], ctx_dram[num(pair)]).then_inc(s[f"side_in{pair[1]}"], 16)

            n, slot = PARTS * HD, HPP * T
            row = RING * slot

            def lay_out(pair):
                if not active(pair):
                    return
                u = pair[1]
                first = u * slot
                wait_apart(e, (s["q_parts"], num(pair) + 1), (s["shifted"], (num(pair) - RING + 1) * HPP))
                for j in range(PARTS):
                    dst = bass.AP(q_stack, first + j * row, [[PARTS * row, HD], [T, HPP], [1, T]])
                    e.dma_start(dst, Qp[:, u, j, :]).then_inc(s[f"q_in{u}"], 16)
                e.wait_ge(s["k_parts"], num(pair) + 1)
                for i in range(PARTS):
                    e.dma_start(Ks[COPY_ROW + i * HD:COPY_ROW + (i + 1) * HD, u, :, :],
                                Kp[:, u, i, :]).then_inc(s[f"k_in{u}"], 16)

            def replicate(pair):
                if not active(pair):
                    return
                u = pair[1]
                first = u * slot
                e.wait_ge(s[f"q_in{u}"], (pair[0] + 1) * PARTS * 16)
                for i in range(1, PARTS):
                    e.dma_start(Qs[i * n:(i + 1) * n, u, :, :], Qs[0:n, u, :, :]).then_inc(s[f"stack_in{u}"], 16)
                e.wait_ge(s[f"k_in{u}"], (pair[0] + 1) * PARTS * 16)
                e.dma_start(bass.AP(k_stack, first, [[row, SPLIT_ROWS], [1, slot]]),
                            bass.AP(k_stack, first + COPY_ROW * row, [[row, n], [0, PARTS], [1, slot]])
                            ).then_inc(s[f"stack_in{u}"], 16)

            def shift_rows(pair, half):
                if not active(pair):
                    return
                wait_job(e, s, l, *(("A", "max0"), ("B", "max1"))[half], pair, "read")
                e.dma_start(Qs[SHIFT_ROW:SHIFT_ROW + PARTS, pair[1], half * HEADS:(half + 1) * HEADS, :],
                            max_rows[:, half, :]).then_inc(s[f"max_in{half}"], 16)

            def iteration(r):
                load_side(at(r, AHEAD + 1 if l else 0))
                lay_out(at(r, 2))
                shift_rows(r, 1)
                replicate(at(r, 2))
                shift_rows(at(r, 1), 0)

            if l:
                load_side((0, 0))
            iterations(e, iteration)

        @block.sync
        def _(e):
            for dst, src in ((ident, "ident"), (att_w[0], "att_w0"), (att_b[0], "att_b0"), (band_raw, "band"),
                             (att_w[1], "att_w1"), (att_b[1], "att_b1"), (rope, "rope")):
                full = tuple(slice(None) for _ in dst.shape)
                e.dma_start(dst[full], a[src]).then_inc(consts_in, 16)
            for n in range(4):
                e.dma_start(X[:, n * 8:n * 8 + 8, :], x_dram[:, n * 8:n * 8 + 8, :]).then_inc(x_in, 16)
            e.dma_start(ff0_w[:, :, :], a["ff0_w"].rearrange("(b p) n -> p b n", p=P)).then_inc(ffn_in, 16)
            e.dma_start(ff0_scale[:, :], a["ff0_scale"].partition_broadcast(P)).then_inc(ffn_in, 16)
            e.dma_start(down_b[:, :], a["down_b"].partition_broadcast(P)).then_inc(ffn_in, 16)
            e.dma_start(up_b[:, :], a["up_b"]).then_inc(ffn_in, 16)
            e.dma_start(up_raw, a["up_q"].rearrange("(b p) n -> p b n", p=P)).then_inc(ffn_in, 16)
            e.dma_start(up_scale[:, :, :], a["up_scale"].rearrange("(b p) n -> p b n", p=P)).then_inc(ffn_in, 16)
            e.dma_start(down_raw, a["down_q"].rearrange("(b p) n -> p b n", p=P)).then_inc(ffn_in, 16)
            e.dma_start(down_scale[:, :, :],
                        a["down_scale"].rearrange("(b p) n -> p b n", p=P)).then_inc(ffn_in, 16)
            e.dma_start(lora_in, a["lora_in"]).then_inc(ffn_in, 16)
            e.dma_start(lora_out, a["lora_out"]).then_inc(ffn_in, 16)
            e.wait_ge(cleared, 7)
            sync_attention(e, 0)
            e.wait_ge(L[0]["B_read"], JOBS_B[0])
            sync_attention(e, 1)
            with e.Fori(0, PAIRS // CHUNK) as c:
                e.wait_ge(g_upd, c * CHUNK + CHUNK)
                e.dma_start(out_dram[:, bass.ds(c * CHUNK, CHUNK), :],
                            X[:, bass.ds(c * CHUNK, CHUNK), :]).then_inc(stored, 16)
            e.wait_ge(stored, PAIRS // CHUNK * 16)

        def tensor_attention(e, l):
            s = L[l]
            w = att_w[l]
            WQ, WK, WV, WO = (0, 1, 2, 3) if l == 0 else (0, 2, 4, 5)
            win, start = win_of[l], start_of[l]

            def score_head(pair, h):
                if not active(pair):
                    return
                n = num(pair) * HPP + h
                if h == 0:
                    e.wait_ge(s[f"stack_in{pair[1]}"], (pair[0] + 1) * STACK_IN)
                wait_some(e, s["maxed"], n - 1)
                dst = score_bank[h % 2]
                if l == 0:
                    nc.tensor.matmul(dst[:, 0:2 * win], ident16[:, :], band16[:, :], start=True, stop=False)
                for blk in range(2):
                    last = nc.tensor.matmul(dst[:, blk * win:(blk + 1) * win],
                                            Qs[0:SHIFT_ROW, pair[1], h, blk * P:(blk + 1) * P],
                                            Ks[0:SHIFT_ROW, pair[1], h, start(blk):start(blk) + win],
                                            start=(l == 1), stop=(l == 1 or blk == 1))
                last.then_inc(s["scored"], 1)

            def shifted_head(pair, h):
                if not active(pair):
                    return
                n = num(pair) * HPP + h
                if h % HEADS == 0:
                    e.wait_ge(s[f"max_in{h // HEADS}"], (num(pair) + 1) * 16)
                wait_some(e, s["exped"], n - 1)
                dst = exp_bank[h % 2]
                for blk in range(2):
                    last = nc.tensor.matmul(dst[:, blk * win:(blk + 1) * win],
                                            Ks[:, pair[1], h, blk * P:(blk + 1) * P],
                                            Qs[:, pair[1], h, start(blk):start(blk) + win],
                                            start=True, stop=True)
                last.then_inc(s["shifted"], 1)

            def values_group(pair, g):
                if not active(pair):
                    return
                if l == 0:
                    e.wait_ge(s["masked"], num(pair) * 4 + g + 1)
                else:
                    e.wait_ge(s["exped"], num(pair) * HPP + 4 * g + 4)
                if g == 0:
                    wait_job(e, s, l, "A", "v", pair, "read")
                if g % 2 == 0:
                    wait_some(e, s["heads_out"], num(pair) * 2 + g // 2 - 1)
                dst = pv_bank[g // 2]
                for blk in range(2):
                    for j in range(4):
                        head = 4 * g + j
                        first = (g % 2) * T + start(blk)
                        last = nc.tensor.matmul(dst[32 * j:32 * j + 32, first:first + win],
                                                V[:, pair[1], blk, head, :],
                                                probs[:, head % 8, blk * win:(blk + 1) * win],
                                                start=(blk == 0), stop=(blk == 1), skip_group_check=True)
                last.then_inc(s["pv_done"], 1)

            def project(b, name, pair, weights, source, wait):
                if not active(pair):
                    return
                wait()
                wait_bank(e, s, l, b, name, pair)
                for n, k in enumerate(weights):
                    last = nc.tensor.matmul(job_bank[b][:, n * T:(n + 1) * T], w[:, k, :], source,
                                            start=True, stop=True)
                last.then_inc(s[f"{b}_filled"], 1)

            def project_v(pair):
                if not active(pair):
                    return
                src = side if l else xn
                wait_bank(e, s, l, "A", "v", pair)
                for blk in range(2):
                    last = nc.tensor.matmul(job_bank["A"][:, blk * P:(blk + 1) * P],
                                            src[:, pair[1], blk * P:(blk + 1) * P], w[:, WV, :],
                                            start=True, stop=True)
                last.then_inc(s["A_filled"], 1)

            def turn_max(b, pair, half):
                if not active(pair):
                    return
                wait_apart(e, (s[f"{b}_read"], job_order(l, b, f"max{half}", pair)),
                        (s[f"max_parts{half}"], num(pair) + 1))
                nc.tensor.transpose(max_bank[b], max_parts[:, half, :, :].rearrange("p n h -> p (n h)"),
                                    ident16[:, :]).then_inc(s[f"{b}_filled"], 1)

            def turn_heads(pair, half):
                if not active(pair):
                    return
                wait_bank(e, s, l, "A", f"heads{half}", pair)
                e.wait_ge(s["heads_out"], num(pair) * 2 + half + 1)
                for blk in range(2):
                    for g in range(2):
                        last = nc.tensor.transpose(job_bank["A"][:, (blk * 2 + g) * P:(blk * 2 + g + 1) * P],
                                                   heads_sb[:, half, g * T + blk * P:g * T + (blk + 1) * P],
                                                   ident[:, :])
                last.then_inc(s["A_filled"], 1)

            def turn_back(pair):
                if not active(pair):
                    return
                wait_bank(e, s, l, "B", "back", pair)
                wait_job(e, s, l, "A", "heads1", pair, "read")
                for blk in range(2):
                    last = nc.tensor.transpose(job_bank["B"][:, blk * P:(blk + 1) * P],
                                               normed[:, pair[1], blk, :], ident[:, :])
                last.then_inc(s["B_filled"], 1)

            def iteration(r):
                p1, p2, p3, m1 = at(r, 1), at(r, 2), at(r, AHEAD), at(r, -1)
                for h in range(HPP):
                    if h == 3:
                        turn_max("B", r, 1)
                    if h == 2:
                        project("A", "q", p3, [WQ] if l == 0 else [WQ, WQ + 1], xn[:, p3[1], :],
                                lambda: e.wait_ge(s["xn_ready"], num(p3) + 1))
                    if h == 4:
                        project("B", "k", p3, [WK] if l == 0 else [WK, WK + 1],
                                (side if l else xn)[:, p3[1], :],
                                lambda: l and e.wait_ge(s[f"side_in{p3[1]}"], (p3[0] + 1) * 16))
                    if h == 5:
                        turn_heads(m1, 1)
                    if h == 7:
                        turn_back(m1)
                    if h == 8:
                        project_v(p2)
                    if h == 10:
                        project("B", "out", m1, [WO], mixed_in[:, :],
                                lambda: wait_job(e, s, l, "B", "back", m1, "read"))
                    if h == 11:
                        turn_max("A", p1, 0)
                    if h == 13 and l == 0:
                        project("B", "mix", m1, [4], gated,
                                lambda: e.wait_ge(s["gated"], num(m1) + 1))
                    if h == 14:
                        turn_heads(r, 0)
                    score_head(p1, h)
                    shifted_head(r, h)
                    if h % 4 == VALUES_AT[l]:
                        values_group(m1 if h < 4 else r, (h // 4 - 1) % 4)

            iterations(e, iteration)

        @block.tensor
        def _(e):
            e.wait_ge(consts_in, CONSTS * 16)
            e.wait_ge(ffn_in, 10 * 16)
            e.wait_ge(dequant, 4)
            n = 0
            for blk in range(2):
                for hb in range(HB):
                    wait_some(e, prep_read, n - 7)
                    dst = bank[n % 8][:, 0:P]
                    nc.tensor.matmul(dst, up_f[:, hb, blk * P:(blk + 1) * P], ident[:, :], start=True, stop=False)
                    nc.tensor.matmul(dst, lora_in[:, blk * P:(blk + 1) * P], lora_out[:, hb * P:(hb + 1) * P],
                                     start=False, stop=True).then_inc(prep_ps, 1)
                    n += 1
            for hb in range(HB):
                for blk in range(2):
                    wait_some(e, prep_read, n - 7)
                    dst = bank[n % 8][:, 0:P]
                    nc.tensor.matmul(dst, down_f[:, blk, hb * P:(hb + 1) * P], ident[:, :], start=True, stop=False)
                    nc.tensor.matmul(dst, lora_in[:, T + hb * P:T + (hb + 1) * P],
                                     lora_out[:, FF + blk * P:FF + (blk + 1) * P],
                                     start=False, stop=True).then_inc(prep_ps, 1)
                    n += 1
            for l in range(2):
                wait_some(e, prep_read, n - 7)
                nc.tensor.matmul(bank[n % 8][:, 0:1], att_w[l][:, 3 if l == 0 else 5, :],
                                 att_b[l][:, 2 if l == 0 else 4:(2 if l == 0 else 4) + 1],
                                 start=True, stop=True).then_inc(prep_ps, 1)
                n += 1
            e.wait_ge(prep_read, n)
            e.wait_ge(rounded, 2)
            tensor_attention(e, 0)

            def ff0(pair):
                n, u = num(pair, 2), pair[1]
                if active(pair, 2):
                    e.wait_ge(f_xn, n + 1)
                    wait_some(e, f_xTs, n - 1)
                    for blk in range(2):
                        last = nc.tensor.transpose(bank[u][:, blk * P:(blk + 1) * P],
                                                   xn[:, u, blk * P:(blk + 1) * P], ident[:, :])
                    last.then_inc(f_xT, 1)
                m1 = at(pair, -1, 2)
                if active(m1, 2):
                    e.wait_ge(f_xTs, num(m1, 2) + 1)
                    wait_some(e, f_keep, num(m1, 2) - 1)
                    for blk in range(2):
                        last = nc.tensor.matmul(bank[2 + m1[1]][:, 0:T], ff0_xT[:, m1[1], blk * P:(blk + 1) * P],
                                                ff0_w[:, blk, :], start=(blk == 0), stop=(blk == 1))
                    last.then_inc(f_mm, 1)

            e.wait_ge(L[0]["B_read"], JOBS_B[0])
            for pair in range(4):
                ff0((pair // 2, pair % 2))
            with e.Fori(2, PAIRS // 2) as i:
                ff0((i, 0))
                ff0((i, 1))
            ff0((PAIRS // 2, 0))
            e.wait_ge(f_keep, PAIRS)
            tensor_attention(e, 1)

            def turn_chunk(c, cu):
                for j in range(CHUNK):
                    e.wait_ge(g_xn, c * CHUNK + j + 1)
                    if j == 0:
                        wait_some(e, g_xTs, 2 * c)
                    for blk in range(2):
                        last = nc.tensor.transpose(bank[blk][:, j * P:(j + 1) * P],
                                                   xn[:, j % 2, blk * P:(blk + 1) * P], ident[:, :])
                    last.then_inc(g_xT, 1)

            def up_chunk(c, cu):
                e.wait_ge(g_xTs, 2 * c + 2)
                for hb in range(HB):
                    wait_some(e, g_relu, HB * c + hb - 1)
                    for blk in range(2):
                        last = nc.tensor.matmul(bank[2 + hb % 2][:, :], up_w[:, blk, hb * P:(hb + 1) * P],
                                                xT[:, cu, blk, :], start=(blk == 0), stop=(blk == 1))
                    last.then_inc(g_up, 1)

            def down_chunk(c, cu):
                e.wait_ge(g_relu, HB * c + HB)
                for j in range(CHUNK):
                    wait_some(e, g_upd, CHUNK * c + j - 1)
                    for hb in range(HB):
                        last = nc.tensor.matmul(bank[4 + j % 2][:, 0:T],
                                                hidden[cu][:, hb, j * P:(j + 1) * P], down_w[:, hb, :],
                                                start=(hb == 0), stop=(hb == HB - 1))
                    last.then_inc(g_down, 1)

            e.wait_ge(L[1]["B_read"], JOBS_B[1])
            turn_chunk(0, 0)
            up_chunk(0, 0)
            turn_chunk(1, 1)
            down_chunk(0, 0)
            up_chunk(1, 1)
            with e.Fori(1, PAIRS // CHUNK // 2) as i:
                turn_chunk(i * 2, 0)
                down_chunk(i * 2 - 1, 1)
                up_chunk(i * 2, 0)
                turn_chunk(i * 2 + 1, 1)
                down_chunk(i * 2, 0)
                up_chunk(i * 2 + 1, 1)
            down_chunk(PAIRS // CHUNK - 1, 1)

        def scalar_attention(e, l):
            s = L[l]
            b = att_b[l]
            win, start = win_of[l], start_of[l]

            def exp_head(pair, h):
                if not active(pair):
                    return
                n = num(pair) * HPP + h
                e.wait_ge(s["shifted"], n + 1)
                if h % 4 == 0:
                    wait_some(e, s["pv_done"], num(pair) * 4 + h // 4 - 1)
                nc.scalar.activation(probs[:, h % 8, 0:2 * win], exp_bank[h % 2][:, 0:2 * win], ACT.Exp,
                                     scale=SCALE).then_inc(s["exped"], 1)

            def high_part(bk, name, pair, parts, column):
                if not active(pair):
                    return
                u = pair[1]
                wait_some(e, s[f"{name}_in{u}"], pair[0] * PARTS * 16)
                if l == 0:
                    wait_job(e, s, l, bk, name, pair, "filled")
                    nc.scalar.activation(parts[:, u, 0, :], job_bank[bk][:, 0:T], ACT.Identity,
                                         bias=b[:, column:column + 1]).then_inc(s[f"{name}_high"], 1)
                else:
                    e.wait_ge(s["rot_sum"], num(pair) * 2 + (1 if name == "q" else 2))
                    rest = q_rest if name == "q" else k_rest
                    nc.scalar.activation(parts[:, u, 0, :], rest[:, u, :],
                                         ACT.Copy).then_inc(s[f"{name}_high"], 1)

            def values_out(pair):
                if not active(pair):
                    return
                wait_job(e, s, l, "A", "v", pair, "filled")
                wait_some(e, s["pv_done"], (num(pair) - RING + 1) * 4)
                nc.scalar.activation(V[:, pair[1], :, :, 0:HD].rearrange("p b h d -> p (b h) d"),
                                     job_bank["A"][:, 0:2 * P].rearrange("p (n d) -> p n d", d=HD),
                                     ACT.Copy).then_inc(s["A_read"], 1)

            def heads_out(pair, half):
                if not active(pair):
                    return
                e.wait_ge(s["pv_done"], num(pair) * 4 + 2 * half + 2)
                wait_job(e, s, l, "A", f"heads{half}", at(pair, -1), "filled")
                nc.scalar.activation(heads_sb[:, half, :], pv_bank[half][:, :],
                                     ACT.Copy).then_inc(s["heads_out"], 1)

            def max_out(bk, pair, half):
                if not active(pair):
                    return
                wait_job(e, s, l, bk, f"max{half}", pair, "filled")
                wait_some(e, s[f"max_in{half}"], num(pair) * 16)
                nc.scalar.activation(max_rows[:, half, :], max_bank[bk], ACT.Copy).then_inc(s[f"{bk}_read"], 1)

            def back_out(pair):
                if not active(pair):
                    return
                wait_job(e, s, l, "B", "back", pair, "filled")
                nc.scalar.activation(mixed_in[:, :], job_bank["B"][:, 0:T], ACT.Copy).then_inc(s["B_read"], 1)

            def relu(pair):
                if not active(pair):
                    return
                wait_job(e, s, l, "B", "out", pair, "filled")
                wait_some(e, s["gated"], num(pair))
                nc.scalar.activation(relu_out, job_bank["B"][:, 0:T], ACT.Relu,
                                     bias=out_bias[:, 0:1]).then_inc(s["B_read"], 1)

            def iteration(r):
                p1, p2, p3, m1 = at(r, 1), at(r, 2), at(r, AHEAD), at(r, -1)
                for h in range(HPP):
                    if h == 2 and l == 0:
                        high_part("A", "q", p3, Qp, 0)
                    if h == 3:
                        max_out("B", r, 1)
                    if h == VALUES_AT[l] + 1:
                        heads_out(m1, 1)
                    if h == 4 and l == 0:
                        high_part("B", "k", p3, Kp, 1)
                    if h == 5 and l == 1:
                        high_part("A", "q", p3, Qp, 0)
                    if h == 7:
                        back_out(m1)
                    if h == 7 and l == 1:
                        high_part("B", "k", p3, Kp, 1)
                    if h == 8:
                        values_out(p2)
                    if h == 10 and l == 0:
                        relu(m1)
                    if h == 11:
                        max_out("A", p1, 0)
                    if h == VALUES_AT[l] + 9:
                        heads_out(r, 0)
                    exp_head(r, h)

            iterations(e, iteration)

        def scalar_sqrt(n):
            nc.scalar.activation(rstd[:, :], var[:, :], ACT.Sqrt).then_inc(ln_std, 1)

        @block.scalar
        def _(e):
            e.wait_ge(consts_in, CONSTS * 16)
            nc.scalar.activation(ident16[:, :], ident[:, :], ACT.Copy).then_inc(rounded, 1)
            nc.scalar.activation(band16[:, :], band_raw, ACT.Copy).then_inc(rounded, 1)
            e.wait_ge(ln_var, 1)
            scalar_sqrt(0)
            scalar_attention(e, 0)
            e.wait_ge(ln_var, 2)
            scalar_sqrt(1)

            def ff0(pair):
                n, u = num(pair, 2), pair[1]
                if active(pair, 2):
                    e.wait_ge(f_xT, n + 1)
                    wait_some(e, f_mm, n - 1)
                    nc.scalar.activation(ff0_xT[:, u, 0:T], bank[u][:, 0:T], ACT.Copy).then_inc(f_xTs, 1)
                m1 = at(pair, -1, 2)
                if active(m1, 2):
                    e.wait_ge(f_mm, num(m1, 2) + 1)
                    wait_some(e, f_sq, num(m1, 2) - 1)
                    nc.scalar.activation(junk[:, m1[1], :], bank[2 + m1[1]][:, 0:T], ACT.Square,
                                         accum_out=sumsq[:, bass.ds(num(m1, 2), 1)]).then_inc(f_sq, 1)

            for pair in range(4):
                ff0((pair // 2, pair % 2))
            with e.Fori(2, PAIRS // 2) as i:
                ff0((i, 0))
                ff0((i, 1))
            ff0((PAIRS // 2, 0))
            e.wait_ge(f_sq, PAIRS)
            nc.scalar.activation(tmp[:, 0, :], sumsq[:, :], ACT.Sqrt).then_inc(f_root, 1)
            e.wait_ge(f_norm, 1)
            nc.scalar.activation(tmp[:, 2, :], tmp[:, 1, :], ACT.Tanh).then_inc(f_tanh, 1)
            e.wait_ge(ln_var, 3)
            scalar_sqrt(2)
            scalar_attention(e, 1)
            e.wait_ge(ln_var, 4)
            scalar_sqrt(3)

            def turn_out(c, cu):
                e.wait_ge(g_xT, CHUNK * c + CHUNK)
                wait_some(e, g_up, HB * c - HB)
                for blk in range(2):
                    nc.scalar.activation(xT[:, cu, blk, :], bank[blk][:, :], ACT.Copy).then_inc(g_xTs, 1)

            def relu_chunk(c, cu):
                wait_some(e, g_down, CHUNK * c - CHUNK)
                for hb in range(HB):
                    e.wait_ge(g_up, HB * c + hb + 1)
                    nc.scalar.activation(hidden[cu][:, hb, :], bank[2 + hb % 2][:, :], ACT.Relu,
                                         bias=up_b[:, hb:hb + 1]).then_inc(g_relu, 1)

            turn_out(0, 0)
            relu_chunk(0, 0)
            turn_out(1, 1)
            relu_chunk(1, 1)
            with e.Fori(1, PAIRS // CHUNK // 2) as i:
                turn_out(i * 2, 0)
                relu_chunk(i * 2, 0)
                turn_out(i * 2 + 1, 1)
                relu_chunk(i * 2 + 1, 1)

        def split_max(e, engine, s, l, pair, half):
            if not active(pair):
                return
            wait_apart(e, (s["maxed"], num(pair) * HPP + HEADS * (half + 1)),
                    job_wait(s, l, *(("A", "max0"), ("B", "max1"))[half], at(pair, -1), "filled"))
            src = row_max[:, pair[1], half * HEADS:(half + 1) * HEADS, :].rearrange("p h b -> p (h b)")
            step, done = s[f"max_step{half}"], num(pair) * PARTS
            parts, rest = max_parts[:, half, :, :], max_rest[:, half, :]
            engine.tensor_scalar(parts[:, 0, :], src, 1.0, None, ALU.mult).then_inc(step, 1)
            e.wait_ge(step, done + 1)
            engine.tensor_tensor(rest, src, parts[:, 0, :], ALU.subtract).then_inc(step, 1)
            wait_apart(e, (step, done + 2))
            engine.tensor_scalar(parts[:, 1, :], rest, 1.0, None, ALU.mult).then_inc(step, 1)
            e.wait_ge(step, done + 3)
            engine.tensor_tensor(parts[:, 2, :], rest, parts[:, 1, :],
                                 ALU.subtract).then_inc(s[f"max_parts{half}"], 1)

        def vector_stats(e, pair_value):
            nc.vector.bn_stats(stats[:, pair_value, :], X[:, pair_value, :]).then_inc(ln_vec, 1)

        def vector_norm(e, round_):
            base = round_ * (PAIRS + 6) + PAIRS
            e.wait_ge(ln_vec, base)
            me, mo = stats[:, :, 1], stats[:, :, 4]
            nc.vector.tensor_tensor(tmp[:, 0, :], me, mo, ALU.add).then_inc(ln_vec, 1)
            nc.vector.tensor_tensor(tmp[:, 1, :], me, mo, ALU.subtract).then_inc(ln_vec, 1)
            nc.vector.tensor_tensor(tmp[:, 2, :], stats[:, :, 2], stats[:, :, 5], ALU.add).then_inc(ln_vec, 1)
            e.wait_ge(ln_vec, base + 3)
            nc.vector.tensor_scalar(mean[:, :], tmp[:, 0, :], 0.5, None, ALU.mult).then_inc(ln_vec, 1)
            nc.vector.scalar_tensor_tensor(out=tmp[:, 3, :], in0=tmp[:, 1, :], scalar=0.25, in1=tmp[:, 1, :],
                                           op0=ALU.mult, op1=ALU.mult).then_inc(ln_vec, 1)
            nc.vector.tensor_scalar(tmp[:, 2, :], tmp[:, 2, :], 1.0 / T, LN_EPS, ALU.mult,
                                    ALU.add).then_inc(ln_vec, 1)
            e.wait_ge(ln_vec, base + 6)
            nc.vector.tensor_tensor(var[:, :], tmp[:, 2, :], tmp[:, 3, :], ALU.add).then_inc(ln_var, 1)
            e.wait_ge(ln_std, round_ + 1)
            nc.vector.reciprocal(rstd[:, :], rstd[:, :]).then_inc(ln_ready, 1)
            e.wait_ge(ln_ready, round_ + 1)

        def vector_apply(pair_value, dst, signal):
            nc.vector.tensor_scalar(dst, X[:, pair_value, :], mean[:, bass.ds(pair_value, 1)],
                                    rstd[:, bass.ds(pair_value, 1)], ALU.subtract, ALU.mult).then_inc(signal, 1)

        def vector_attention(e, l):
            s = L[l]
            b = att_b[l]
            win = win_of[l]

            def apply(pair):
                if not active(pair):
                    return
                if l == 0:
                    wait_job(e, s, l, "A", "v", at(pair, -RING), "filled")
                else:
                    wait_job(e, s, l, "A", "q", at(pair, -RING), "filled")
                vector_apply(num(pair), xn[:, pair[1], :], s["xn_ready"])

            def maximum(pair, h):
                if not active(pair):
                    return
                if h % HEADS == 0:
                    wait_job(e, s, l, *(("A", "max0"), ("B", "max1"))[h // HEADS], at(pair, -RING), "filled")
                e.wait_ge(s["scored"], num(pair) * HPP + h + 1)
                nc.vector.tensor_reduce(row_max[:, pair[1], h, :],
                                        score_bank[h % 2][:, 0:2 * win].rearrange("p (b k) -> p b k", b=2),
                                        AX.X, ALU.max).then_inc(s["maxed"], 1)

            def rest_of(bk, name, pair, parts, rest, column):
                if not active(pair):
                    return
                e.wait_ge(s[f"{name}_high"], num(pair) + 1)
                wait_some(e, s[f"{name}_parts"], num(pair) - RING + 1)
                nc.vector.scalar_tensor_tensor(out=rest[:, pair[1], :], in0=job_bank[bk][:, 0:T],
                                               scalar=b[:, column:column + 1], in1=parts[:, pair[1], 0, :],
                                               op0=ALU.add, op1=ALU.subtract).then_inc(s[f"{bk}_read"], 1)

            def rotate(bk, name, pair, n, column):
                if not active(pair):
                    return
                wait_job(e, s, l, bk, name, pair, "filled")
                wait_some(e, s["rot_sum"], num(pair) * 2 - 1 + n)
                nc.vector.scalar_tensor_tensor(out=rot[:, 2 * n, :], in0=job_bank[bk][:, 0:T],
                                               scalar=b[:, column:column + 1], in1=rope[:, 0, :],
                                               op0=ALU.add, op1=ALU.mult).then_inc(s["rot_mul"], 1)
                nc.vector.scalar_tensor_tensor(out=rot[:, 2 * n + 1, :], in0=job_bank[bk][:, T:2 * T],
                                               scalar=b[:, column + 1:column + 2], in1=rope[:, 1, :],
                                               op0=ALU.add, op1=ALU.mult).then_inc(s[f"{bk}_read"], 1)

            def normalise(pair, half):
                if not active(pair):
                    return
                wait_job(e, s, l, "A", f"heads{half}", pair, "filled")
                turned = job_bank["A"][:, :].rearrange("p (n c) -> p n c", c=32)
                nc.vector.reciprocal(rcp[:, half, :], turned[:, :, HD]).then_inc(s["rcp_done"], 1)
                e.wait_ge(s["rcp_done"], num(pair) * 2 + half + 1)
                wait_job(e, s, l, "B", "back", at(pair, -RING), "filled")
                nc.vector.tensor_tensor(
                    normed[:, pair[1], :, half * CH:(half + 1) * CH].rearrange("p b (h d) -> p b h d", d=HD),
                    turned[:, :, 0:HD].rearrange("p (b h) d -> p b h d", b=2),
                    rcp[:, half, :].rearrange("p (b h) -> p b h", b=2).unsqueeze(3)
                    .broadcast_to([P, 2, HEADS, HD]),
                    ALU.mult).then_inc(s["A_read"], 1)

            def update(pair):
                if not active(pair):
                    return
                last = "mix" if l == 0 else "out"
                wait_job(e, s, l, "B", last, pair, "filled")
                bias = b[:, 4:5] if l == 0 else out_bias[:, 1:2]
                nc.vector.scalar_tensor_tensor(out=X[:, num(pair), :], in0=job_bank["B"][:, 0:T], scalar=bias,
                                               in1=X[:, num(pair), :], op0=ALU.add,
                                               op1=ALU.add).then_inc(s["B_read"], 1)
                wait_job(e, s, l, "B", last, pair, "read")
                vector_stats(e, num(pair))

            def iteration(r):
                p1, p3, m1 = at(r, 1), at(r, AHEAD), at(r, -1)
                for h in range(HPP):
                    if h == 2 and l == 1:
                        rotate("A", "q", p3, 0, 0)
                    if h == 4 and l == 1:
                        rotate("B", "k", p3, 1, 2)
                    if h == 5:
                        normalise(m1, 1)
                    if h == 6:
                        apply(at(r, AHEAD + 1))
                    if h == (13, 10)[l]:
                        update(m1)
                    if h == 14:
                        normalise(r, 0)
                    maximum(p1, h)
                    if h == 2 and l == 0:
                        rest_of("A", "q", p3, Qp, q_rest, 0)
                    if h == 4 and l == 0:
                        rest_of("B", "k", p3, Kp, k_rest, 1)
                    if l == 0 and h in (HEADS - 1, HPP - 1):
                        split_max(e, nc.vector, s, l, p1, h // HEADS)

            apply((0, 0))
            iterations(e, iteration)

        @block.vector
        def _(e):
            nc.vector.memset(Qs[:, :, :, :].rearrange("p a h t -> p (a h t)").bitcast(i32), 0).then_inc(cleared, 1)
            nc.vector.memset(Ks[:, :, :, :].rearrange("p a h t -> p (a h t)").bitcast(i32), 0).then_inc(cleared, 1)
            nc.vector.memset(V[:, :, :, :, :], 0.0).then_inc(cleared, 1)
            e.wait_ge(cleared, 3)
            nc.vector.memset(Ks[SHIFT_ROW:SHIFT_ROW + PARTS, :, :, :], -1.0).then_inc(cleared, 1)
            nc.vector.memset(V[:, :, :, :, HD:HD + 1], 1.0).then_inc(cleared, 1)
            e.wait_ge(ffn_in, 10 * 16)
            for n, (dst, raw, sc, cols) in enumerate(((up_f, up_raw, up_scale, HB * T // QBLOCK),
                                                      (down_f, down_raw, down_scale, 2 * FF // QBLOCK))):
                nc.vector.tensor_scalar(dst, raw, 7.5, None, ALU.subtract).then_inc(dequant, 1)
                e.wait_ge(dequant, 2 * n + 1)
                flat = dst.rearrange("p a b -> p (a b)").rearrange("p (s q) -> p s q", q=QBLOCK)
                nc.vector.tensor_tensor(flat, flat, sc[:, :, :].rearrange("p a s -> p (a s)").unsqueeze(2)
                                        .broadcast_to([P, cols, QBLOCK]), ALU.mult).then_inc(dequant, 1)
            for blk in range(2):
                last = nc.vector.tensor_tensor(ff0_w[:, blk, :], ff0_w[:, blk, :], ff0_scale[:, :], ALU.mult)
                last.then_inc(cleared, 1)
            n = 0
            for blk in range(2):
                for hb in range(HB):
                    e.wait_ge(prep_ps, n + 1)
                    nc.vector.tensor_copy(up_w[:, blk, hb * P:(hb + 1) * P],
                                          bank[n % 8][:, 0:P]).then_inc(prep_read, 1)
                    n += 1
            for hb in range(HB):
                for blk in range(2):
                    e.wait_ge(prep_ps, n + 1)
                    nc.vector.tensor_copy(down_w[:, hb, blk * P:(blk + 1) * P],
                                          bank[n % 8][:, 0:P]).then_inc(prep_read, 1)
                    n += 1
            e.wait_ge(consts_in, CONSTS * 16)
            for l in range(2):
                e.wait_ge(prep_ps, n + 1)
                col = 3 if l == 0 else 5
                nc.vector.tensor_tensor(out_bias[:, l:l + 1], bank[n % 8][:, 0:1], att_b[l][:, col:col + 1],
                                        ALU.add).then_inc(prep_read, 1)
                n += 1
            e.wait_ge(prep_read, n)
            e.wait_ge(x_in, 4 * 16)
            with e.Fori(0, PAIRS) as i:
                vector_stats(e, i)
            vector_norm(e, 0)
            vector_attention(e, 0)
            vector_norm(e, 1)

            def ff0(pair):
                n, u = num(pair, 2), pair[1]
                if active(pair, 2):
                    wait_some(e, f_xT, n - 1)
                    vector_apply(n, xn[:, u, :], f_xn)
                m1 = at(pair, -1, 2)
                if active(m1, 2):
                    e.wait_ge(f_sq, num(m1, 2) + 1)
                    nc.vector.tensor_copy(ff[:, num(m1, 2), :], bank[2 + m1[1]][:, 0:T]).then_inc(f_keep, 1)

            for pair in range(4):
                ff0((pair // 2, pair % 2))
            with e.Fori(2, PAIRS // 2) as i:
                ff0((i, 0))
                ff0((i, 1))
            ff0((PAIRS // 2, 0))
            e.wait_ge(f_root, 1)
            nc.vector.tensor_scalar(tmp[:, 1, :], tmp[:, 0, :], FFN_EPS, None, ALU.max).then_inc(f_norm, 1)
            e.wait_ge(f_norm, 1)
            nc.vector.tensor_scalar(tmp[:, 3, :], tmp[:, 1, :], FFN_EPS, None, ALU.add).then_inc(f_step, 1)
            e.wait_ge(f_step, 1)
            nc.vector.reciprocal(tmp[:, 3, :], tmp[:, 3, :]).then_inc(f_step, 1)
            e.wait_ge(f_step, 2)
            e.wait_ge(f_tanh, 1)
            nc.vector.tensor_tensor(gain[:, :], tmp[:, 2, :], tmp[:, 3, :], ALU.mult).then_inc(f_step, 1)
            e.wait_ge(f_step, 3)
            nc.vector.tensor_tensor(tmp[:, 1, :], gain[:, :], tmp[:, 0, :], ALU.mult).then_inc(f_step, 1)
            e.wait_ge(f_step, 4)
            nc.vector.tensor_scalar(tmp[:, 1, :], tmp[:, 1, :], FFN_EPS, None, ALU.max).then_inc(f_step, 1)
            e.wait_ge(f_step, 5)
            nc.vector.reciprocal(tmp[:, 3, :], tmp[:, 1, :]).then_inc(f_step, 1)
            e.wait_ge(f_step, 6)
            nc.vector.tensor_scalar(tmp[:, 3, :], tmp[:, 3, :], MAX_NORM, 1.0, ALU.mult, ALU.min).then_inc(f_step, 1)
            e.wait_ge(f_step, 7)
            nc.vector.tensor_tensor(gain[:, :], gain[:, :], tmp[:, 3, :], ALU.mult).then_inc(f_step, 1)
            e.wait_ge(f_step, 8)
            e.wait_ge(f_keep, PAIRS)
            with e.Fori(0, PAIRS) as i:
                nc.vector.scalar_tensor_tensor(out=X[:, i, :], in0=ff[:, i, :], scalar=gain[:, bass.ds(i, 1)],
                                               in1=X[:, i, :], op0=ALU.mult, op1=ALU.add).then_inc(f_upd, 1)
                e.wait_ge(f_upd, i + 1)
                vector_stats(e, i)
            vector_norm(e, 2)
            vector_attention(e, 1)
            vector_norm(e, 3)

            def norm_chunk(c):
                for j in range(CHUNK):
                    wait_some(e, g_xT, c * CHUNK + j - 1)
                    vector_apply(c * CHUNK + j, xn[:, j % 2, :], g_xn)

            def update_chunk(c):
                for j in range(CHUNK):
                    e.wait_ge(g_down, c * CHUNK + j + 1)
                    e.wait_ge(g_bias, c * CHUNK + j + 1)
                    nc.vector.tensor_tensor(X[:, c * CHUNK + j, :], bank[4 + j % 2][:, 0:T],
                                            X[:, c * CHUNK + j, :], ALU.add).then_inc(g_upd, 1)

            norm_chunk(0)
            norm_chunk(1)
            with e.Fori(0, PAIRS // CHUNK - 2) as c:
                update_chunk(c)
                norm_chunk(c + 2)
            update_chunk(PAIRS // CHUNK - 2)
            update_chunk(PAIRS // CHUNK - 1)

        def pool_attention(e, l):
            s = L[l]

            def split(name, pair, parts, rest, mid, done):
                if not active(pair):
                    return
                u = pair[1]
                bk = "A" if name == "q" else "B"
                if l == 0:
                    wait_apart(e, job_wait(s, l, bk, name, pair, "read"))
                    n, total = num(pair), 1
                else:
                    e.wait_ge(s[f"{name}_high"], num(pair) + 1)
                    nc.gpsimd.tensor_tensor(rest[:, u, :], rest[:, u, :], parts[:, u, 0, :],
                                            ALU.subtract).then_inc(s[mid], 1)
                    wait_apart(e, (s[mid], num(pair) * 2 + 1))
                    n, total = num(pair), 2
                nc.gpsimd.tensor_scalar(parts[:, u, 1, :], rest[:, u, :], 1.0, None,
                                        ALU.mult).then_inc(s[mid], 1)
                e.wait_ge(s[mid], (n + 1) * total)
                nc.gpsimd.tensor_tensor(parts[:, u, 2, :], rest[:, u, :], parts[:, u, 1, :],
                                        ALU.subtract).then_inc(s[done], 1)

            def rot_sum(bk, name, pair, n, rest):
                if not active(pair):
                    return
                wait_job(e, s, l, bk, name, pair, "read")
                e.wait_ge(s["rot_mul"], num(pair) * 2 + n + 1)
                wait_some(e, s[f"{name}_parts"], num(pair) - RING + 1)
                nc.gpsimd.tensor_tensor(rest[:, pair[1], :], rot[:, 2 * n, :], rot[:, 2 * n + 1, :],
                                        ALU.add).then_inc(s["rot_sum"], 1)

            def mask_group(pair, g):
                if not active(pair):
                    return
                wait_apart(e, (s["exped"], num(pair) * HPP + 4 * g + 4))
                first = (g % 2) * 4
                half = P // 2

                def keep(blk, lo, width, base, sign):
                    part = probs[:, first:first + 4, blk * WIN + lo:blk * WIN + lo + width]
                    return nc.gpsimd.affine_select(out=part, in_=part, compare_op=ALU.is_ge, fill=0.0, base=base,
                                                   pattern=[[0, 4], [-sign, width]], channel_multiplier=sign)

                keep(0, 0, half, BAND, -1).then_inc(s["mask_step"], 1)
                keep(0, half, P, BAND - half, 1).then_inc(s["mask_step"], 1)
                keep(1, 0, P, BAND - (P - BAND), -1).then_inc(s["mask_step"], 1)
                wait_apart(e, (s["mask_step"], (num(pair) * 4 + g + 1) * 3))
                keep(1, P, half, P + BAND - BAND - P + 0, 1).then_inc(s["masked"], 1)

            def gate(pair):
                if not active(pair):
                    return
                wait_job(e, s, l, "B", "out", pair, "read")
                e.wait_ge(s[f"side_in{pair[1]}"], (pair[0] + 1) * 16)
                wait_job(e, s, l, "B", "mix", at(pair, -1), "filled")
                nc.gpsimd.tensor_tensor(gated, relu_out, side[:, pair[1], :],
                                        ALU.mult).then_inc(s["gated"], 1)

            def iteration(r):
                p1, p3, m1 = at(r, 1), at(r, AHEAD), at(r, -1)
                if l == 0:
                    mask_group(m1, 3)
                    split("q", p3, Qp, q_rest, "q_mid", "q_parts")
                    mask_group(r, 0)
                    split("k", p3, Kp, k_rest, "k_mid", "k_parts")
                    mask_group(r, 1)
                    gate(m1)
                    mask_group(r, 2)
                else:
                    rot_sum("A", "q", p3, 0, q_rest)
                    rot_sum("B", "k", p3, 1, k_rest)
                    split("q", p3, Qp, q_rest, "q_mid", "q_parts")
                    split_max(e, nc.gpsimd, s, l, p1, 0)
                    split("k", p3, Kp, k_rest, "k_mid", "k_parts")
                    split_max(e, nc.gpsimd, s, l, p1, 1)

            iterations(e, iteration)

        @block.gpsimd
        def _(e):
            pool_attention(e, 0)
            pool_attention(e, 1)

            def add_bias(c):
                for j in range(CHUNK):
                    e.wait_ge(g_xn, c * CHUNK + j + 1)
                    nc.gpsimd.tensor_tensor(X[:, c * CHUNK + j, :], X[:, c * CHUNK + j, :], down_b[:, :],
                                            ALU.add).then_inc(g_bias, 1)

            with e.Fori(0, PAIRS // CHUNK) as c:
                add_bias(c)


def _bd(m):
    import numpy as np
    z = np.zeros_like(m)
    return np.block([[m, z], [z, m]])


def _layouts(i):
    import numpy as np
    f = {k: np.asarray(v) for k, v in i.items()}
    dh = np.arange(CH).reshape(HEADS, HD).T.reshape(-1)
    turned = np.roll(dh.reshape(HD, HEADS), HD // 2, axis=0).reshape(-1)
    w_in, b_in = f["L0_xattn_w_in"], f["L0_xattn_b_in"]
    wq, wk, wv = w_in[0:CH], w_in[CH:2 * CH], w_in[2 * CH:3 * CH]
    bq, bk, bv = b_in[0:CH], b_in[CH:2 * CH], b_in[2 * CH:3 * CH]
    w0 = [wq[dh].T, wk[dh].T, wv.T, f["L0_xattn_w_out"].T, f["L0_xattn_w_ct"]]
    b0 = [bq[dh], bk[dh], bv, f["L0_xattn_b_out"], f["L0_xattn_b_ct"]]
    wq, wk, bq, bk = f["L1_xattn_Wq"], f["L1_xattn_Wk"], f["L1_xattn_bq"], f["L1_xattn_bk"]
    w1 = [wq[dh].T, wq[turned].T, wk[dh].T, wk[turned].T, f["L1_xattn_Wv"].T, f["L1_xattn_Wo"].T]
    b1 = [bq[dh], bq[turned], bk[dh], bk[turned], f["L1_xattn_bv"], f["L1_xattn_bo"]]
    inv = (1.0 / 10000.0 ** (np.arange(0, HD, 2, dtype=np.float32) / HD)).astype(np.float32)
    ang = np.arange(T, dtype=np.float32)[None, :] * np.concatenate([inv, inv])[:, None]
    sign = np.where(np.arange(HD) < HD // 2, -1.0, 1.0)[:, None]
    cs = np.stack([np.cos(ang), np.sin(ang) * sign], 1).astype(np.float32)
    rope = np.tile(np.repeat(cs, HEADS, axis=0), (2, 1, 1))
    q = np.arange(P)[:, None]
    k = np.arange(WIN)[None, :]
    band = np.concatenate([np.where(abs((q + b * P) - (k + b * BAND)) <= BAND, 0.0, OUTSIDE) for b in range(2)], 1)
    c = np.ascontiguousarray

    def spread(per_sequence):
        m = per_sequence.reshape(2, HD, HEADS, *per_sequence.shape[1:])
        return m.swapaxes(0, 1).reshape(P, *per_sequence.shape[1:])

    w0 = [spread(_bd(w).T).T if n < 2 else _bd(w) for n, w in enumerate(w0)]
    w1 = [spread(_bd(w).T).T if n < 4 else _bd(w) for n, w in enumerate(w1)]
    b0 = [spread(np.tile(b, 2)) if n < 2 else np.tile(b, 2) for n, b in enumerate(b0)]
    b1 = [spread(np.tile(b, 2)) if n < 4 else np.tile(b, 2) for n, b in enumerate(b1)]
    rope = spread(rope)
    return {
        "x": f["x"], "ctx": f["ctx_2048"],
        "ident": np.eye(P, dtype=np.float32), "band": band.astype(np.float32),
        "rope": rope,
        "att_w0": c(np.stack(w0, 1)), "att_w1": c(np.stack(w1, 1)),
        "att_b0": c(np.stack(b0, 1)), "att_b1": c(np.stack(b1, 1)),
        "ff0_w": f["L0_ffn_weight"], "ff0_scale": f["L0_ffn_scale"],
        "down_b": f["L1_ffn_b_down"], "up_b": c(f["L1_ffn_b_up"].reshape(FF // P, P).T),
        "up_q": f["L1_ffn_w_up_q"], "up_scale": f["L1_ffn_w_up_scale"],
        "down_q": f["L1_ffn_w_down_q"], "down_scale": f["L1_ffn_w_down_scale"],
        "lora_in": c(np.concatenate([f["L1_ffn_w_up_lora_a"].T, f["L1_ffn_w_down_lora_a"].T], 1)),
        "lora_out": c(np.concatenate([f["L1_ffn_w_up_lora_b"], f["L1_ffn_w_down_lora_b"]], 1)),
    }


def kernel(**inputs):
    import numpy as np
    import concourse.bacc as bacc
    from concourse.bass_utils import run_bass_kernel_spmd

    nc = bacc.Bacc("TRN2", target_bir_lowering=False, num_devices=1)
    arrays, aps = {}, {}
    for name, value in _layouts(inputs).items():
        value = np.ascontiguousarray(value)
        arrays[f"in_{name}"] = value
        aps[name] = nc.dram_tensor(f"in_{name}", value.shape, mybir.dt.from_np(value.dtype),
                                   kind="ExternalInput").ap()
    out = nc.dram_tensor("out", (BATCH, CH, T), mybir.dt.float32, kind="ExternalOutput").ap()
    build(nc, aps, out)
    result = run_bass_kernel_spmd(nc, [arrays], core_ids=[0])
    return result.results[0]["out"]
```

```python
import concourse.bass as bass
from concourse import mybir
from contextlib import ExitStack

BATCH = 64
CH = 64
T = 256
HEADS = 8
HD = CH // HEADS
BAND = 64
FF = 1024
RANK = 16
QBLOCK = 64
P = 128
PAIRS = BATCH // 2
HPP = 2 * HEADS
PARTS = 3
SPLIT_ROWS = PARTS * PARTS * HD
SHIFT_ROW = 96
LN_EPS = 1e-5
FFN_EPS = 1e-7
MAX_NORM = 0.99
OUTSIDE = -1.0e30
WIN = T // 2 + BAND
RING = 3
VALUES_AT = (3, 2)
X_CHUNKS = 4
X_PAIRS = PAIRS // X_CHUNKS
FF0_RING = 4
FF0_LAG = (2, 2, 4)
SCORE_BANKS = 3
AHEAD = 3
MINUS_ONES = -(1.0 + 383 / 2 ** 16)
COPY_ROW = 72


def at(r, k, ring=RING):
    i, u = r
    t = u + k
    return (i + t // ring, t % ring)


def num(r, ring=RING):
    return r[0] * ring + r[1]


def active(r, ring=RING):
    return not isinstance(r[0], int) or 0 <= num(r, ring) < PAIRS


JOBS = {
    "A": [("q", AHEAD), ("heads1", -1), ("v", 2), ("max0", 1), ("heads0", 0)],
    "B": [("max1", 0), ("k", AHEAD), ("back", -1), ("out", -1), ("mix", -1)],
}
FIRST_FULL, LAST_FULL = 1, PAIRS - 1 - AHEAD


def job_order(layer, bank, name, pair):
    jobs = [j for j in JOBS[bank] if layer == 0 or j[0] != "mix"]
    place = [j[0] for j in jobs].index(name)
    r = at(pair, -jobs[place][1])
    if isinstance(r[0], int):
        if not active(pair):
            return None
        n = sum(0 <= q + d < PAIRS for q in range(-AHEAD, num(r)) for _, d in jobs)
        return n + sum(0 <= num(r) + d < PAIRS for _, d in jobs[:place])
    before = sum(0 <= q + d < PAIRS for q in range(-AHEAD, FIRST_FULL) for _, d in jobs)
    return num(r) * len(jobs) + (before - FIRST_FULL * len(jobs) + place)


def build(nc, a, out):
    fp32 = mybir.dt.float32
    bf16 = mybir.dt.bfloat16
    i32 = mybir.dt.int32
    ALU = mybir.AluOpType
    ACT = mybir.ActivationFunctionType
    AX = mybir.AxisListType

    x_dram = a["x"].rearrange("(n b) c t -> (b c) n t", b=2)
    ctx_dram = a["ctx"].rearrange("(n b) c t -> n (b c) t", b=2)
    out_dram = out.rearrange("(n b) c t -> (b c) n t", b=2)

    stack = ExitStack()
    with stack:
        def sb(name, shape, dt=fp32):
            return stack.enter_context(nc.sbuf_tensor(name, shape, dt))

        def sem(name):
            return stack.enter_context(nc.semaphore(name))

        X = sb("X", [P, PAIRS, T])
        ident = sb("ident", [P, P])
        ident16 = sb("ident16", [P, P], bf16)
        band16 = sb("band16", [P, 2 * WIN], bf16)
        rope = sb("rope", [P, 2, T])
        att_w = [sb("att_w0", [P, 5, P]), sb("att_w1", [P, 6, P])]
        att_b = [sb("att_b0", [P, 5]), sb("att_b1", [P, 6])]
        out_bias = sb("out_bias", [P, 2])
        ff0_w = sb("ff0_w", [P, 2, T])
        ff0_scale = sb("ff0_scale", [P, T])
        up_w = sb("up_w", [P, 2, FF])
        down_w = sb("down_w", [P, FF // P, T])
        up_b = sb("up_b", [P, FF // P])
        down_b = sb("down_b", [P, T])
        up_scale = sb("up_scale", [P, FF // P, T // QBLOCK])
        down_scale = sb("down_scale", [P, 2, FF // QBLOCK])
        stats = sb("stats", [P, PAIRS, 6])
        mean = sb("mean", [P, PAIRS])
        var = sb("var", [P, PAIRS])
        rstd = sb("rstd", [P, PAIRS])
        tmp = sb("tmp", [P, 4, PAIRS])
        sumsq = sb("sumsq", [P, PAIRS])
        gain = sb("gain", [P, PAIRS])
        Qs = sb("Qs", [P, RING, HPP, T], bf16)
        Ks = sb("Ks", [P, RING, HPP, T], bf16)
        probs = sb("probs", [P, 8, 2 * T])
        V = sb("V", [P, RING, 2, HPP, 32])
        xn = sb("xn", [P, RING, T])
        side = sb("side", [P, RING, T])
        Qp = sb("Qp", [P, RING, PARTS, T], bf16)
        Kp = sb("Kp", [P, RING, PARTS, T], bf16)
        q_rest = sb("q_rest", [P, RING, T])
        k_rest = sb("k_rest", [P, RING, T])
        rot = sb("rot", [P, 4, T])
        row_max = sb("row_max", [P, RING, HPP, 2])
        max_parts = sb("max_parts", [P, 2, PARTS, HPP], bf16)
        max_rest = sb("max_rest", [P, 2, HPP])
        max_rows = sb("max_rows", [PARTS * HPP, 2, P], bf16)
        heads_sb = sb("heads_sb", [P, 2, 2 * T])
        rcp = sb("rcp", [P, 2, HPP])
        normed = sb("normed", [P, RING, 2, P])
        mixed_in = sb("mixed_in", [P, T])
        relu_out = rot[:, 0, :]
        gated = rot[:, 1, :]
        band_raw = rot[:, :, :].rearrange("p a t -> p (a t)")[:, 0:2 * WIN]
        ff = sb("ff", [P, PAIRS, T])
        junk = k_rest
        ff0_xT = heads_sb[:, :, :].rearrange("p h (n t) -> p (h n) t", t=T)
        ff0_xn = rot
        xT = (Ks[:, 0:2, :, :].rearrange("p a h t -> p (a h t)").bitcast(fp32)[:, 0:4 * T * 2]
              .rearrange("p (a b t) -> p a b t", a=2, b=2))
        up_raw = ff[:, 0:FF // P, :].bitcast(i32)
        down_raw = ff[:, FF // P:2 * FF // P, :].rearrange("p (a b) t -> p a (b t)", a=2).bitcast(i32)
        lora = probs[0:RANK, :, :].rearrange("p h t -> p (h t)")
        lora_in = lora[:, 0:T + FF]
        lora_out = lora[:, T + FF:2 * (T + FF)]
        up_f = ff[:, 2 * FF // P:3 * FF // P, :]
        down_f = ff[:, 3 * FF // P:4 * FF // P, :].rearrange("p (a b) t -> p a (b t)", a=2)
        hidden = [probs, Qs[:, 0:2, :, :].rearrange("p a h t -> p (a h t)").bitcast(fp32)
                  .rearrange("p (h t) -> p h t", h=FF // P)]

        bank = [stack.enter_context(nc.psum_tensor(f"bank{n}", [P, 512], fp32)) for n in range(8)]
        exp_bank, pv_bank = bank[2:4], bank[4]
        score_bank = [bank[0], bank[1], bank[5]]
        job_bank = {"A": bank[6], "B": bank[7]}
        max_bank = {b: job_bank[b][0:PARTS * HPP, 0:P // 2].bitcast(bf16) for b in "AB"}

        passed = sem("passed")
        weights0_in = sem("weights0_in")
        consts_in = sem("consts_in")
        rounded = sem("rounded")
        x_in = [sem(f"x_in{c}") for c in range(X_CHUNKS)]
        ffn_in = sem("ffn_in")
        stored = sem("stored")
        cleared_q = sem("cleared_q")
        cleared_k = sem("cleared_k")
        x_vec = sem("x_vec")
        prep_ps = sem("prep_ps")
        prep_read = sem("prep_read")
        dequant_up = sem("dequant_up")
        dequant_down = sem("dequant_down")
        ff0_scaled = sem("ff0_scaled")
        ln_vec = sem("ln_vec")
        ln_var = sem("ln_var")
        ln_std = sem("ln_std")
        ln_ready = sem("ln_ready")
        L = []
        for l in range(2):
            L.append({n: sem(f"L{l}_{n}") for n in (
                "xn_ready", "side_in0", "side_in1", "side_in2", "A_filled", "A_read", "B_filled", "B_read", "q_high", "k_high",
                "q_mid", "k_mid", "q_parts", "k_parts", "rot_mul", "rot_sum", "q_in0", "q_in1", "q_in2", "k_in0", "k_in1", "k_in2",
                "stack_in0", "stack_in1", "stack_in2", "scored", "maxed", "max_step0", "max_step1", "max_parts0", "max_parts1", "max_in0", "max_in1", "shifted", "exped",
                "masked", "mask_step", "pv_done", "heads_out", "rcp_done", "mixed", "relued", "gated")})
        f_xn = sem("f_xn")
        f_xT = sem("f_xT")
        f_xTs = sem("f_xTs")
        f_mm = sem("f_mm")
        f_sq = sem("f_sq")
        f_keep = sem("f_keep")
        f_norm = sem("f_norm")
        f_root = sem("f_root")
        f_tanh = sem("f_tanh")
        f_step = sem("f_step")
        f_upd = sem("f_upd")
        g_xn = sem("g_xn")
        g_xT = sem("g_xT")
        g_xTs = sem("g_xTs")
        g_bias = sem("g_bias")
        g_up = sem("g_up")
        g_relu = sem("g_relu")
        g_down = sem("g_down")
        g_upd = sem("g_upd")

        SCALE = float(HD) ** -0.5
        win_of = [WIN, T]
        start_of = [lambda blk: blk * BAND, lambda blk: 0]
        STACK_IN = PARTS * 16
        CONSTS = 5
        PREP_READS = FF // P + 2
        PREP_BANKS = bank[2:5]
        JOBS_B = (len(JOBS["B"]) * PAIRS, (len(JOBS["B"]) - 1) * PAIRS)
        FFN_LOADS = 10
        NORM_STEPS = 6
        CHUNK = 4
        HB = FF // P

        def bank_of(pair, h):
            return score_bank[(HPP * pair[1] + h) % SCORE_BANKS]

        def iterations(e, body, extra=None):
            for n in range(-AHEAD, RING):
                body((n // RING, n % RING))
                if extra:
                    extra(n)
            with e.Fori(1, (LAST_FULL + 1) // RING) as i:
                for u in range(RING):
                    body((i, u))
            for n in range((LAST_FULL + 1) // RING * RING, PAIRS + 1):
                body((n // RING, n % RING))

        def ff0_steps(e, step):
            for n in range(2 * FF0_RING):
                step((n // FF0_RING, n % FF0_RING))
            with e.Fori(2, PAIRS // FF0_RING) as i:
                for u in range(FF0_RING):
                    step((i, u))
            for n in range(PAIRS, PAIRS + max(FF0_LAG)):
                step((n // FF0_RING, n % FF0_RING))

        def wait_job(e, s, l, b, name, pair, what):
            n = job_order(l, b, name, pair)
            if n is not None:
                e.wait_ge(s[f"{b}_{what}"], n + 1)

        def wait_bank(e, s, l, b, name, pair):
            n = job_order(l, b, name, pair)
            if not (isinstance(n, int) and n == 0):
                e.wait_ge(s[f"{b}_read"], n)

        def wait_some(e, s, value):
            if not (isinstance(value, int) and value <= 0):
                e.wait_ge(s, value)

        def wait_apart(e, *waits):
            for w, v in waits:
                if v is not None and not (isinstance(v, int) and v <= 0):
                    e.wait_ge(w, v)
                    if not isinstance(v, int):
                        e.sem_inc(passed, 1)

        def job_wait(s, l, b, name, pair, what):
            n = job_order(l, b, name, pair)
            return s[f"{b}_{what}"], None if n is None else n + 1

        block = stack.enter_context(nc.Block())

        def sync_attention(e, l):
            s = L[l]
            q_stack, k_stack = Qs[:, :, :, :].tensor, Ks[:, :, :, :].tensor

            def load_side(pair):
                if not active(pair):
                    return
                if l == 0:
                    wait_apart(e, (s["gated"], num(pair) - RING + 1))
                else:
                    wait_apart(e, job_wait(s, l, "A", "v", at(pair, -RING), "filled"))
                e.dma_start(side[:, pair[1], :], ctx_dram[num(pair)]).then_inc(s[f"side_in{pair[1]}"], 16)

            n, slot = PARTS * HD, HPP * T
            row = RING * slot

            def lay_out(pair):
                if not active(pair):
                    return
                u = pair[1]
                first = u * slot
                wait_apart(e, (s["q_parts"], num(pair) + 1), (s["shifted"], (num(pair) - RING + 1) * HPP))
                for j in range(PARTS):
                    dst = bass.AP(q_stack, first + j * row, [[PARTS * row, HD], [T, HPP], [1, T]])
                    e.dma_start(dst, Qp[:, u, j, :]).then_inc(s[f"q_in{u}"], 16)
                e.wait_ge(s["k_parts"], num(pair) + 1)
                for i in range(PARTS):
                    e.dma_start(Ks[COPY_ROW + i * HD:COPY_ROW + (i + 1) * HD, u, :, :],
                                Kp[:, u, i, :]).then_inc(s[f"k_in{u}"], 16)

            def replicate(pair):
                if not active(pair):
                    return
                u = pair[1]
                first = u * slot
                e.wait_ge(s[f"q_in{u}"], (pair[0] + 1) * PARTS * 16)
                for i in range(1, PARTS):
                    e.dma_start(Qs[i * n:(i + 1) * n, u, :, :], Qs[0:n, u, :, :]).then_inc(s[f"stack_in{u}"], 16)
                e.wait_ge(s[f"k_in{u}"], (pair[0] + 1) * PARTS * 16)
                e.dma_start(bass.AP(k_stack, first, [[row, SPLIT_ROWS], [1, slot]]),
                            bass.AP(k_stack, first + COPY_ROW * row, [[row, n], [0, PARTS], [1, slot]])
                            ).then_inc(s[f"stack_in{u}"], 16)

            def shift_rows(pair, half):
                if not active(pair):
                    return
                wait_job(e, s, l, *(("A", "max0"), ("B", "max1"))[half], pair, "read")
                e.dma_start(Qs[SHIFT_ROW:SHIFT_ROW + PARTS, pair[1], half * HEADS:(half + 1) * HEADS, :],
                            max_rows[:, half, :]).then_inc(s[f"max_in{half}"], 16)

            def iteration(r):
                load_side(at(r, AHEAD + 1 if l else 0))
                lay_out(at(r, 2))
                shift_rows(r, 1)
                replicate(at(r, 2))
                shift_rows(at(r, 1), 0)

            if l:
                load_side((0, 0))
            iterations(e, iteration)

        @block.sync
        def _(e):
            e.dma_start(att_w[0][:, :, :], a["att_w0"]).then_inc(weights0_in, 16)
            e.dma_start(att_b[0][:, :], a["att_b0"]).then_inc(weights0_in, 16)
            e.dma_start(ident[:, :], a["ident"]).then_inc(consts_in, 16)
            e.dma_start(band_raw, a["band"]).then_inc(consts_in, 16)
            e.dma_start(att_w[1][:, :, :], a["att_w1"]).then_inc(consts_in, 16)
            e.dma_start(att_b[1][:, :], a["att_b1"]).then_inc(consts_in, 16)
            e.dma_start(rope[:, :, :], a["rope"]).then_inc(consts_in, 16)
            e.wait_ge(cleared_q, 3)
            e.wait_ge(cleared_k, 2)
            sync_attention(e, 0)
            e.wait_ge(L[0]["B_read"], JOBS_B[0])
            sync_attention(e, 1)
            with e.Fori(0, PAIRS // CHUNK) as c:
                e.wait_ge(g_upd, c * CHUNK + CHUNK)
                e.dma_start(out_dram[:, bass.ds(c * CHUNK, CHUNK), :],
                            X[:, bass.ds(c * CHUNK, CHUNK), :]).then_inc(stored, 16)
            e.wait_ge(stored, PAIRS // CHUNK * 16)

        def tensor_attention(e, l, extra=None):
            s = L[l]
            w = att_w[l]
            WQ, WK, WV, WO = (0, 1, 2, 3) if l == 0 else (0, 2, 4, 5)
            win, start = win_of[l], start_of[l]

            def score_head(pair, h):
                if not active(pair):
                    return
                n = num(pair) * HPP + h
                if h == 0:
                    e.wait_ge(s[f"stack_in{pair[1]}"], (pair[0] + 1) * STACK_IN)
                wait_some(e, s["maxed"], n - SCORE_BANKS + 1)
                dst = bank_of(pair, h)
                if l == 0:
                    nc.tensor.matmul(dst[:, 0:2 * win], ident16[:, :], band16[:, :], start=True, stop=False)
                for blk in range(2):
                    last = nc.tensor.matmul(dst[:, blk * win:(blk + 1) * win],
                                            Qs[0:SHIFT_ROW, pair[1], h, blk * P:(blk + 1) * P],
                                            Ks[0:SHIFT_ROW, pair[1], h, start(blk):start(blk) + win],
                                            start=(l == 1), stop=(l == 1 or blk == 1))
                last.then_inc(s["scored"], 1)

            def shifted_head(pair, h):
                if not active(pair):
                    return
                n = num(pair) * HPP + h
                if h % HEADS == 0:
                    e.wait_ge(s[f"max_in{h // HEADS}"], (num(pair) + 1) * 16)
                wait_some(e, s["exped"], n - 1)
                dst = exp_bank[h % 2]
                for blk in range(2):
                    last = nc.tensor.matmul(dst[:, blk * win:(blk + 1) * win],
                                            Ks[:, pair[1], h, blk * P:(blk + 1) * P],
                                            Qs[:, pair[1], h, start(blk):start(blk) + win],
                                            start=True, stop=True)
                last.then_inc(s["shifted"], 1)

            def values_group(pair, g):
                if not active(pair):
                    return
                if l == 0:
                    e.wait_ge(s["masked"], num(pair) * 4 + g + 1)
                else:
                    e.wait_ge(s["exped"], num(pair) * HPP + 4 * g + 4)
                if g == 0:
                    wait_job(e, s, l, "A", "v", pair, "read")
                if g % 2 == 0:
                    wait_some(e, s["heads_out"], num(pair) * 2 + g // 2)
                dst = pv_bank
                for blk in range(2):
                    for j in range(4):
                        head = 4 * g + j
                        first = (g % 2) * T + start(blk)
                        last = nc.tensor.matmul(dst[32 * j:32 * j + 32, first:first + win],
                                                V[:, pair[1], blk, head, :],
                                                probs[:, head % 8, blk * win:(blk + 1) * win],
                                                start=(blk == 0), stop=(blk == 1), skip_group_check=True)
                last.then_inc(s["pv_done"], 1)

            def project(b, name, pair, weights, source, wait):
                if not active(pair):
                    return
                wait()
                wait_bank(e, s, l, b, name, pair)
                for n, k in enumerate(weights):
                    last = nc.tensor.matmul(job_bank[b][:, n * T:(n + 1) * T], w[:, k, :], source,
                                            start=True, stop=True)
                last.then_inc(s[f"{b}_filled"], 1)

            def project_v(pair):
                if not active(pair):
                    return
                src = side if l else xn
                wait_bank(e, s, l, "A", "v", pair)
                for blk in range(2):
                    last = nc.tensor.matmul(job_bank["A"][:, blk * P:(blk + 1) * P],
                                            src[:, pair[1], blk * P:(blk + 1) * P], w[:, WV, :],
                                            start=True, stop=True)
                last.then_inc(s["A_filled"], 1)

            def turn_max(b, pair, half):
                if not active(pair):
                    return
                wait_apart(e, (s[f"{b}_read"], job_order(l, b, f"max{half}", pair)),
                        (s[f"max_parts{half}"], num(pair) + 1))
                nc.tensor.transpose(max_bank[b], max_parts[:, half, :, :].rearrange("p n h -> p (n h)"),
                                    ident16[:, :]).then_inc(s[f"{b}_filled"], 1)

            def turn_heads(pair, half):
                if not active(pair):
                    return
                wait_bank(e, s, l, "A", f"heads{half}", pair)
                e.wait_ge(s["heads_out"], num(pair) * 2 + half + 1)
                for blk in range(2):
                    for g in range(2):
                        last = nc.tensor.transpose(job_bank["A"][:, (blk * 2 + g) * P:(blk * 2 + g + 1) * P],
                                                   heads_sb[:, half, g * T + blk * P:g * T + (blk + 1) * P],
                                                   ident[:, :])
                last.then_inc(s["A_filled"], 1)

            def turn_back(pair):
                if not active(pair):
                    return
                wait_bank(e, s, l, "B", "back", pair)
                wait_job(e, s, l, "A", "heads1", pair, "read")
                for blk in range(2):
                    last = nc.tensor.transpose(job_bank["B"][:, blk * P:(blk + 1) * P],
                                               normed[:, pair[1], blk, :], ident[:, :])
                last.then_inc(s["B_filled"], 1)

            def iteration(r):
                p1, p2, p3, m1 = at(r, 1), at(r, 2), at(r, AHEAD), at(r, -1)
                for h in range(HPP):
                    if h == 3:
                        turn_max("B", r, 1)
                    if h == 2:
                        project("A", "q", p3, [WQ] if l == 0 else [WQ, WQ + 1], xn[:, p3[1], :],
                                lambda: e.wait_ge(s["xn_ready"], num(p3) + 1))
                    if h == 4:
                        project("B", "k", p3, [WK] if l == 0 else [WK, WK + 1],
                                (side if l else xn)[:, p3[1], :],
                                lambda: l and e.wait_ge(s[f"side_in{p3[1]}"], (p3[0] + 1) * 16))
                    if h == 5:
                        turn_heads(m1, 1)
                    if h == 7:
                        turn_back(m1)
                    if h == 8:
                        project_v(p2)
                    if h == 10:
                        project("B", "out", m1, [WO], mixed_in[:, :],
                                lambda: wait_job(e, s, l, "B", "back", m1, "read"))
                    if h == 12:
                        turn_max("A", p1, 0)
                    if h == 13 and l == 0:
                        project("B", "mix", m1, [4], gated,
                                lambda: e.wait_ge(s["gated"], num(m1) + 1))
                    if h == 14:
                        turn_heads(r, 0)
                    score_head(p1, h)
                    shifted_head(r, h)
                    if h % 4 == VALUES_AT[l]:
                        values_group(m1 if h < 4 else r, (h // 4 - 1) % 4)

            iterations(e, iteration, extra and (lambda n: extra(e, n)))

        def tensor_prepare(e, n):
            if n == -2:
                e.wait_ge(consts_in, CONSTS * 16)
                e.wait_ge(rounded, 2)
            if n != -1:
                return
            e.wait_ge(ffn_in, FFN_LOADS * 16)
            e.wait_ge(dequant_up, 2)
            e.wait_ge(dequant_down, 2)
            job = 0
            for blk in range(2):
                for hb in range(HB):
                    if job % 4 == 0:
                        wait_some(e, prep_read, job // 4 - 2)
                    dst = PREP_BANKS[job // 4 % 3][:, job % 4 * P:(job % 4 + 1) * P]
                    nc.tensor.matmul(dst, up_f[:, hb, blk * P:(blk + 1) * P], ident[:, :], start=True, stop=False)
                    nc.tensor.matmul(dst, lora_in[:, blk * P:(blk + 1) * P], lora_out[:, hb * P:(hb + 1) * P],
                                     start=False, stop=True).then_inc(prep_ps, 1)
                    job += 1
            for hb in range(HB):
                for blk in range(2):
                    if job % 4 == 0:
                        wait_some(e, prep_read, job // 4 - 2)
                    dst = PREP_BANKS[job // 4 % 3][:, job % 4 * P:(job % 4 + 1) * P]
                    nc.tensor.matmul(dst, down_f[:, blk, hb * P:(hb + 1) * P], ident[:, :], start=True, stop=False)
                    nc.tensor.matmul(dst, lora_in[:, T + hb * P:T + (hb + 1) * P],
                                     lora_out[:, FF + blk * P:FF + (blk + 1) * P],
                                     start=False, stop=True).then_inc(prep_ps, 1)
                    job += 1
            wait_some(e, prep_read, job // 4 - 2)
            for l in range(2):
                nc.tensor.matmul(PREP_BANKS[job // 4 % 3][:, l:l + 1], att_w[l][:, 3 if l == 0 else 5, :],
                                 att_b[l][:, 2 if l == 0 else 4:(2 if l == 0 else 4) + 1],
                                 start=True, stop=True).then_inc(prep_ps, 1)
            e.wait_ge(prep_read, PREP_READS)

        @block.tensor
        def _(e):
            e.wait_ge(weights0_in, 2 * 16)
            tensor_attention(e, 0, tensor_prepare)

            def ff0(pair):
                n, u = num(pair, FF0_RING), pair[1]
                if active(pair, FF0_RING):
                    e.wait_ge(f_xn, n + 1)
                    wait_some(e, f_xTs, n - FF0_RING + 1)
                    for blk in range(2):
                        last = nc.tensor.transpose(bank[u][:, blk * P:(blk + 1) * P],
                                                   ff0_xn[:, u, blk * P:(blk + 1) * P], ident[:, :])
                    last.then_inc(f_xT, 1)
                late = at(pair, -FF0_LAG[0], FF0_RING)
                n, u = num(late, FF0_RING), late[1]
                if active(late, FF0_RING):
                    e.wait_ge(f_xTs, n + 1)
                    wait_some(e, f_keep, n - FF0_RING + 1)
                    for blk in range(2):
                        last = nc.tensor.matmul(bank[4 + u][:, 0:T], ff0_xT[:, u, blk * P:(blk + 1) * P],
                                                ff0_w[:, blk, :], start=(blk == 0), stop=(blk == 1))
                    last.then_inc(f_mm, 1)

            e.wait_ge(L[0]["B_read"], JOBS_B[0])
            e.wait_ge(ff0_scaled, 2)
            ff0_steps(e, ff0)
            e.wait_ge(f_keep, PAIRS)
            tensor_attention(e, 1)

            def turn_chunk(c, cu):
                for j in range(CHUNK):
                    e.wait_ge(g_xn, c * CHUNK + j + 1)
                    if j == 0:
                        wait_some(e, g_xTs, 2 * c)
                    for blk in range(2):
                        last = nc.tensor.transpose(bank[blk][:, j * P:(j + 1) * P],
                                                   xn[:, j % 2, blk * P:(blk + 1) * P], ident[:, :])
                    last.then_inc(g_xT, 1)

            def up_chunk(c, cu):
                e.wait_ge(g_xTs, 2 * c + 2)
                for hb in range(HB):
                    wait_some(e, g_relu, HB * c + hb - 1)
                    for blk in range(2):
                        last = nc.tensor.matmul(bank[2 + hb % 2][:, :], up_w[:, blk, hb * P:(hb + 1) * P],
                                                xT[:, cu, blk, :], start=(blk == 0), stop=(blk == 1))
                    last.then_inc(g_up, 1)

            def down_chunk(c, cu):
                e.wait_ge(g_relu, HB * c + HB)
                for j in range(CHUNK):
                    wait_some(e, g_upd, CHUNK * c + j - 1)
                    for hb in range(HB):
                        last = nc.tensor.matmul(bank[4 + j % 2][:, 0:T],
                                                hidden[cu][:, hb, j * P:(j + 1) * P], down_w[:, hb, :],
                                                start=(hb == 0), stop=(hb == HB - 1))
                    last.then_inc(g_down, 1)

            e.wait_ge(L[1]["B_read"], JOBS_B[1])
            turn_chunk(0, 0)
            up_chunk(0, 0)
            turn_chunk(1, 1)
            down_chunk(0, 0)
            up_chunk(1, 1)
            with e.Fori(1, PAIRS // CHUNK // 2) as i:
                turn_chunk(i * 2, 0)
                down_chunk(i * 2 - 1, 1)
                up_chunk(i * 2, 0)
                turn_chunk(i * 2 + 1, 1)
                down_chunk(i * 2, 0)
                up_chunk(i * 2 + 1, 1)
            down_chunk(PAIRS // CHUNK - 1, 1)

        def scalar_attention(e, l, extra=None):
            s = L[l]
            b = att_b[l]
            win, start = win_of[l], start_of[l]

            def exp_head(pair, h):
                if not active(pair):
                    return
                n = num(pair) * HPP + h
                e.wait_ge(s["shifted"], n + 1)
                if h % 4 == 0:
                    wait_some(e, s["pv_done"], num(pair) * 4 + h // 4 - 1)
                nc.scalar.activation(probs[:, h % 8, 0:2 * win], exp_bank[h % 2][:, 0:2 * win], ACT.Exp,
                                     scale=SCALE).then_inc(s["exped"], 1)

            def high_part(bk, name, pair, parts, column):
                if not active(pair):
                    return
                u = pair[1]
                wait_some(e, s[f"{name}_in{u}"], pair[0] * PARTS * 16)
                if l == 0:
                    wait_job(e, s, l, bk, name, pair, "filled")
                    nc.scalar.activation(parts[:, u, 0, :], job_bank[bk][:, 0:T], ACT.Identity,
                                         bias=b[:, column:column + 1]).then_inc(s[f"{name}_high"], 1)
                else:
                    e.wait_ge(s["rot_sum"], num(pair) * 2 + (1 if name == "q" else 2))
                    rest = q_rest if name == "q" else k_rest
                    nc.scalar.activation(parts[:, u, 0, :], rest[:, u, :],
                                         ACT.Copy).then_inc(s[f"{name}_high"], 1)

            def values_out(pair):
                if not active(pair):
                    return
                wait_job(e, s, l, "A", "v", pair, "filled")
                wait_some(e, s["pv_done"], (num(pair) - RING + 1) * 4)
                nc.scalar.activation(V[:, pair[1], :, :, 0:HD].rearrange("p b h d -> p (b h) d"),
                                     job_bank["A"][:, 0:2 * P].rearrange("p (n d) -> p n d", d=HD),
                                     ACT.Copy).then_inc(s["A_read"], 1)

            def heads_out(pair, half):
                if not active(pair):
                    return
                e.wait_ge(s["pv_done"], num(pair) * 4 + 2 * half + 2)
                wait_job(e, s, l, "A", f"heads{half}", at(pair, -1), "filled")
                nc.scalar.activation(heads_sb[:, half, :], pv_bank[:, :],
                                     ACT.Copy).then_inc(s["heads_out"], 1)

            def max_out(bk, pair, half):
                if not active(pair):
                    return
                wait_job(e, s, l, bk, f"max{half}", pair, "filled")
                wait_some(e, s[f"max_in{half}"], num(pair) * 16)
                nc.scalar.activation(max_rows[:, half, :], max_bank[bk], ACT.Copy).then_inc(s[f"{bk}_read"], 1)

            def back_out(pair):
                if not active(pair):
                    return
                wait_job(e, s, l, "B", "back", pair, "filled")
                nc.scalar.activation(mixed_in[:, :], job_bank["B"][:, 0:T], ACT.Copy).then_inc(s["B_read"], 1)

            def relu(pair):
                if not active(pair):
                    return
                wait_job(e, s, l, "B", "out", pair, "filled")
                wait_some(e, s["gated"], num(pair))
                nc.scalar.activation(relu_out, job_bank["B"][:, 0:T], ACT.Relu,
                                     bias=out_bias[:, 0:1]).then_inc(s["B_read"], 1)

            def iteration(r):
                p1, p2, p3, m1 = at(r, 1), at(r, 2), at(r, AHEAD), at(r, -1)
                for h in range(HPP):
                    if h == 2 and l == 0:
                        high_part("A", "q", p3, Qp, 0)
                    if h == 3:
                        max_out("B", r, 1)
                    if h == VALUES_AT[l] + 1:
                        heads_out(m1, 1)
                    if h == 4 and l == 0:
                        high_part("B", "k", p3, Kp, 1)
                    if h == 5 and l == 1:
                        high_part("A", "q", p3, Qp, 0)
                    if h == 7:
                        back_out(m1)
                    if h == 7 and l == 1:
                        high_part("B", "k", p3, Kp, 1)
                    if h == 8:
                        values_out(p2)
                    if h == 10 and l == 0:
                        relu(m1)
                    if h == 12:
                        max_out("A", p1, 0)
                    if h == VALUES_AT[l] + 9:
                        heads_out(r, 0)
                    exp_head(r, h)

            iterations(e, iteration, extra and (lambda n: extra(e, n)))

        def scalar_sqrt(first, end):
            nc.scalar.activation(rstd[:, first:end], var[:, first:end], ACT.Sqrt).then_inc(ln_std, 1)

        def scalar_loads(e):
            e.dma_start(ff0_w[:, :, :], a["ff0_w"].rearrange("(b p) n -> p b n", p=P)).then_inc(ffn_in, 16)
            e.dma_start(ff0_scale[:, :], a["ff0_scale"].partition_broadcast(P)).then_inc(ffn_in, 16)
            e.dma_start(down_b[:, :], a["down_b"].partition_broadcast(P)).then_inc(ffn_in, 16)
            e.dma_start(up_b[:, :], a["up_b"]).then_inc(ffn_in, 16)
            e.dma_start(up_raw, a["up_q"].rearrange("(b p) n -> p b n", p=P)).then_inc(ffn_in, 16)
            e.dma_start(up_scale[:, :, :], a["up_scale"].rearrange("(b p) n -> p b n", p=P)).then_inc(ffn_in, 16)
            e.dma_start(down_raw, a["down_q"].rearrange("(b p) n -> p b n", p=P)).then_inc(ffn_in, 16)
            e.dma_start(down_scale[:, :, :],
                        a["down_scale"].rearrange("(b p) n -> p b n", p=P)).then_inc(ffn_in, 16)
            e.dma_start(lora_in, a["lora_in"]).then_inc(ffn_in, 16)
            e.dma_start(lora_out, a["lora_out"]).then_inc(ffn_in, 16)

        def scalar_prepare(e, n):
            if n == -AHEAD:
                e.wait_ge(consts_in, CONSTS * 16)
                nc.scalar.activation(ident16[:, :], ident[:, :], ACT.Copy).then_inc(rounded, 1)
                nc.scalar.activation(band16[:, :], band_raw, ACT.Copy).then_inc(rounded, 1)
            if n == -1:
                for b in range(HB):
                    e.wait_ge(prep_ps, 4 * b + 4)
                    if b < HB // 2:
                        dst = up_w[:, b // 2, b % 2 * 4 * P:(b % 2 + 1) * 4 * P]
                    else:
                        dst = down_w[:, 2 * b - HB:2 * b - HB + 2, :].rearrange("p h t -> p (h t)")
                    nc.scalar.activation(dst, PREP_BANKS[b % 3][:, :], ACT.Copy).then_inc(prep_read, 1)
                e.wait_ge(prep_ps, 4 * HB + 2)
                for l in range(2):
                    col = 3 if l == 0 else 5
                    nc.scalar.activation(out_bias[:, l:l + 1], PREP_BANKS[HB % 3][:, l:l + 1], ACT.Identity,
                                         bias=att_b[l][:, col:col + 1]).then_inc(prep_read, 1)
            if n == 0:
                e.wait_ge(ln_var, 2)
                scalar_sqrt(X_PAIRS, PAIRS)

        @block.scalar
        def _(e):
            for c in range(X_CHUNKS):
                e.dma_start(X[:, c * X_PAIRS:(c + 1) * X_PAIRS, :],
                            x_dram[:, c * X_PAIRS:(c + 1) * X_PAIRS, :]).then_inc(x_in[c], 16)
                if c == 0:
                    scalar_loads(e)
            e.wait_ge(ln_var, 1)
            scalar_sqrt(0, X_PAIRS)
            e.wait_ge(weights0_in, 2 * 16)
            e.wait_ge(cleared_q, 3)
            scalar_attention(e, 0, scalar_prepare)
            e.wait_ge(ln_var, 3)
            scalar_sqrt(0, PAIRS)

            def ff0(pair):
                n, u = num(pair, FF0_RING), pair[1]
                if active(pair, FF0_RING):
                    e.wait_ge(f_xT, n + 1)
                    wait_some(e, f_mm, n - FF0_RING + 1)
                    nc.scalar.activation(ff0_xT[:, u, :], bank[u][:, 0:T], ACT.Copy).then_inc(f_xTs, 1)
                late = at(pair, -FF0_LAG[1], FF0_RING)
                n, u = num(late, FF0_RING), late[1]
                if active(late, FF0_RING):
                    e.wait_ge(f_mm, n + 1)
                    wait_some(e, f_sq, n - 1)
                    nc.scalar.activation(junk[:, u % 2, :], bank[4 + u][:, 0:T], ACT.Square,
                                         accum_out=sumsq[:, bass.ds(n, 1)]).then_inc(f_sq, 1)

            ff0_steps(e, ff0)
            e.wait_ge(f_sq, PAIRS)
            nc.scalar.activation(tmp[:, 0, :], sumsq[:, :], ACT.Sqrt).then_inc(f_root, 1)
            e.wait_ge(f_norm, 1)
            nc.scalar.activation(tmp[:, 2, :], tmp[:, 1, :], ACT.Tanh).then_inc(f_tanh, 1)
            e.wait_ge(ln_var, 4)
            scalar_sqrt(0, PAIRS)
            scalar_attention(e, 1)
            e.wait_ge(ln_var, 5)
            scalar_sqrt(0, PAIRS)

            def turn_out(c, cu):
                e.wait_ge(g_xT, CHUNK * c + CHUNK)
                wait_some(e, g_up, HB * c - HB)
                for blk in range(2):
                    nc.scalar.activation(xT[:, cu, blk, :], bank[blk][:, :], ACT.Copy).then_inc(g_xTs, 1)

            def relu_chunk(c, cu):
                wait_some(e, g_down, CHUNK * c - CHUNK)
                for hb in range(HB):
                    e.wait_ge(g_up, HB * c + hb + 1)
                    nc.scalar.activation(hidden[cu][:, hb, :], bank[2 + hb % 2][:, :], ACT.Relu,
                                         bias=up_b[:, hb:hb + 1]).then_inc(g_relu, 1)

            turn_out(0, 0)
            relu_chunk(0, 0)
            turn_out(1, 1)
            relu_chunk(1, 1)
            with e.Fori(1, PAIRS // CHUNK // 2) as i:
                turn_out(i * 2, 0)
                relu_chunk(i * 2, 0)
                turn_out(i * 2 + 1, 1)
                relu_chunk(i * 2 + 1, 1)

        def dequantise(e, engine, dst, raw, scale, blocks, signal):
            e.wait_ge(ffn_in, FFN_LOADS * 16)
            engine.tensor_scalar(dst, raw, 7.5, None, ALU.subtract).then_inc(signal, 1)
            e.wait_ge(signal, 1)
            flat = dst.rearrange("p a b -> p (a b)").rearrange("p (s q) -> p s q", q=QBLOCK)
            engine.tensor_tensor(flat, flat, scale[:, :, :].rearrange("p a s -> p (a s)").unsqueeze(2)
                                 .broadcast_to([P, blocks, QBLOCK]), ALU.mult).then_inc(signal, 1)

        def split_max(e, engine, s, l, pair, half):
            if not active(pair):
                return
            src = row_max[:, pair[1], half * HEADS:(half + 1) * HEADS, :].rearrange("p h b -> p (h b)")
            step, done = s[f"max_step{half}"], num(pair) * PARTS
            parts, rest = max_parts[:, half, :, :], max_rest[:, half, :]
            wait_apart(e, (s["maxed"], num(pair) * HPP + HEADS * (half + 1)),
                       job_wait(s, l, *(("A", "max0"), ("B", "max1"))[half], at(pair, -1), "filled"))
            engine.tensor_scalar(parts[:, 0, :], src, 1.0, None, ALU.mult).then_inc(step, 1)
            e.wait_ge(step, done + 1)
            engine.tensor_tensor(rest, src, parts[:, 0, :], ALU.subtract).then_inc(step, 1)
            wait_apart(e, (step, done + 2))
            engine.tensor_scalar(parts[:, 1, :], rest, 1.0, None, ALU.mult).then_inc(step, 1)
            e.wait_ge(step, done + 3)
            engine.tensor_tensor(parts[:, 2, :], rest, parts[:, 1, :],
                                 ALU.subtract).then_inc(s[f"max_parts{half}"], 1)

        def vector_stats(e, pair_value, signal=None):
            nc.vector.bn_stats(stats[:, pair_value, :], X[:, pair_value, :]).then_inc(signal or ln_vec, 1)

        def vector_norm(e, round_, first, end, vec, base):
            c = slice(first, end)
            e.wait_ge(vec, base)
            me, mo = stats[:, c, 1], stats[:, c, 4]
            nc.vector.tensor_tensor(tmp[:, 0, c], me, mo, ALU.add).then_inc(vec, 1)
            nc.vector.tensor_tensor(tmp[:, 1, c], me, mo, ALU.subtract).then_inc(vec, 1)
            nc.vector.tensor_tensor(tmp[:, 2, c], stats[:, c, 2], stats[:, c, 5], ALU.add).then_inc(vec, 1)
            e.wait_ge(vec, base + 3)
            nc.vector.tensor_scalar(mean[:, c], tmp[:, 0, c], 0.5, None, ALU.mult).then_inc(vec, 1)
            nc.vector.scalar_tensor_tensor(out=tmp[:, 3, c], in0=tmp[:, 1, c], scalar=0.25, in1=tmp[:, 1, c],
                                           op0=ALU.mult, op1=ALU.mult).then_inc(vec, 1)
            nc.vector.tensor_scalar(tmp[:, 2, c], tmp[:, 2, c], 1.0 / T, LN_EPS, ALU.mult,
                                    ALU.add).then_inc(vec, 1)
            e.wait_ge(vec, base + NORM_STEPS)
            nc.vector.tensor_tensor(var[:, c], tmp[:, 2, c], tmp[:, 3, c], ALU.add).then_inc(ln_var, 1)
            e.wait_ge(ln_std, round_)
            nc.vector.reciprocal(rstd[:, c], rstd[:, c]).then_inc(ln_ready, 1)
            e.wait_ge(ln_ready, round_)

        def vector_prepare(e, n):
            c = n + AHEAD + 1
            if c < X_CHUNKS:
                e.wait_ge(x_in[c], 16)
                for pair in range(c * X_PAIRS, (c + 1) * X_PAIRS):
                    vector_stats(e, pair, x_vec)
            if n == -2:
                dequantise(e, nc.vector, down_f, down_raw, down_scale, 2 * FF // QBLOCK, dequant_down)
            if n == 0:
                vector_norm(e, 2, X_PAIRS, PAIRS, x_vec, PAIRS + NORM_STEPS)

        def vector_apply(pair_value, dst, signal):
            nc.vector.tensor_scalar(dst, X[:, pair_value, :], mean[:, bass.ds(pair_value, 1)],
                                    rstd[:, bass.ds(pair_value, 1)], ALU.subtract, ALU.mult).then_inc(signal, 1)

        def vector_attention(e, l, extra=None):
            s = L[l]
            b = att_b[l]
            win = win_of[l]

            def apply(pair):
                if not active(pair):
                    return
                if l == 0:
                    wait_job(e, s, l, "A", "v", at(pair, -RING), "filled")
                else:
                    wait_job(e, s, l, "A", "q", at(pair, -RING), "filled")
                vector_apply(num(pair), xn[:, pair[1], :], s["xn_ready"])

            def maximum(pair, h):
                if not active(pair):
                    return
                if h % HEADS == 0:
                    wait_job(e, s, l, *(("A", "max0"), ("B", "max1"))[h // HEADS], at(pair, -RING), "filled")
                e.wait_ge(s["scored"], num(pair) * HPP + h + 1)
                nc.vector.tensor_reduce(row_max[:, pair[1], h, :],
                                        bank_of(pair, h)[:, 0:2 * win].rearrange("p (b k) -> p b k", b=2),
                                        AX.X, ALU.max).then_inc(s["maxed"], 1)

            def rest_of(bk, name, pair, parts, rest, column):
                if not active(pair):
                    return
                e.wait_ge(s[f"{name}_high"], num(pair) + 1)
                wait_some(e, s[f"{name}_parts"], num(pair) - RING + 1)
                nc.vector.scalar_tensor_tensor(out=rest[:, pair[1], :], in0=job_bank[bk][:, 0:T],
                                               scalar=b[:, column:column + 1], in1=parts[:, pair[1], 0, :],
                                               op0=ALU.add, op1=ALU.subtract).then_inc(s[f"{bk}_read"], 1)

            def rotate(bk, name, pair, n, column):
                if not active(pair):
                    return
                wait_job(e, s, l, bk, name, pair, "filled")
                wait_some(e, s["rot_sum"], num(pair) * 2 - 1 + n)
                nc.vector.scalar_tensor_tensor(out=rot[:, 2 * n, :], in0=job_bank[bk][:, 0:T],
                                               scalar=b[:, column:column + 1], in1=rope[:, 0, :],
                                               op0=ALU.add, op1=ALU.mult).then_inc(s["rot_mul"], 1)
                nc.vector.scalar_tensor_tensor(out=rot[:, 2 * n + 1, :], in0=job_bank[bk][:, T:2 * T],
                                               scalar=b[:, column + 1:column + 2], in1=rope[:, 1, :],
                                               op0=ALU.add, op1=ALU.mult).then_inc(s[f"{bk}_read"], 1)

            def normalise(pair, half):
                if not active(pair):
                    return
                wait_job(e, s, l, "A", f"heads{half}", pair, "filled")
                turned = job_bank["A"][:, :].rearrange("p (n c) -> p n c", c=32)
                nc.vector.reciprocal(rcp[:, half, :], turned[:, :, HD]).then_inc(s["rcp_done"], 1)
                e.wait_ge(s["rcp_done"], num(pair) * 2 + half + 1)
                wait_job(e, s, l, "B", "back", at(pair, -RING), "filled")
                nc.vector.tensor_tensor(
                    normed[:, pair[1], :, half * CH:(half + 1) * CH].rearrange("p b (h d) -> p b h d", d=HD),
                    turned[:, :, 0:HD].rearrange("p (b h) d -> p b h d", b=2),
                    rcp[:, half, :].rearrange("p (b h) -> p b h", b=2).unsqueeze(3)
                    .broadcast_to([P, 2, HEADS, HD]),
                    ALU.mult).then_inc(s["A_read"], 1)

            def update(pair):
                if not active(pair):
                    return
                last = "mix" if l == 0 else "out"
                wait_job(e, s, l, "B", last, pair, "filled")
                bias = b[:, 4:5] if l == 0 else out_bias[:, 1:2]
                nc.vector.scalar_tensor_tensor(out=X[:, num(pair), :], in0=job_bank["B"][:, 0:T], scalar=bias,
                                               in1=X[:, num(pair), :], op0=ALU.add,
                                               op1=ALU.add).then_inc(s["B_read"], 1)
                wait_job(e, s, l, "B", last, pair, "read")
                vector_stats(e, num(pair))

            def iteration(r):
                p1, p3, m1 = at(r, 1), at(r, AHEAD), at(r, -1)
                for h in range(HPP):
                    if h == 2 and l == 1:
                        rotate("A", "q", p3, 0, 0)
                    if h == 4 and l == 1:
                        rotate("B", "k", p3, 1, 2)
                    if h == 5:
                        normalise(m1, 1)
                    if h == 6:
                        apply(at(r, AHEAD + 1))
                    if h == (13, 10)[l]:
                        update(m1)
                    if h == 14:
                        normalise(r, 0)
                    maximum(p1, h)
                    if h == 2 and l == 0:
                        rest_of("A", "q", p3, Qp, q_rest, 0)
                    if h == 4 and l == 0:
                        rest_of("B", "k", p3, Kp, k_rest, 1)
                    if l == 0 and h in (0, HEADS):
                        split_max(e, nc.vector, s, l, p1 if h else r, 1 - h // HEADS)

            apply((0, 0))
            iterations(e, iteration, extra and (lambda n: extra(e, n)))

        @block.vector
        def _(e):
            nc.vector.memset(Ks[:, :, :, :].rearrange("p a h t -> p (a h t)").bitcast(i32), 0).then_inc(cleared_k, 1)
            e.wait_ge(cleared_k, 1)
            nc.vector.memset(Ks[SHIFT_ROW:SHIFT_ROW + PARTS, :, :, :].rearrange("p a h t -> p (a h t)")
                             .bitcast(fp32), MINUS_ONES).then_inc(cleared_k, 1)
            e.wait_ge(x_in[0], 16)
            for pair in range(X_PAIRS):
                vector_stats(e, pair, x_vec)
            vector_norm(e, 1, 0, X_PAIRS, x_vec, X_PAIRS)
            e.wait_ge(weights0_in, 2 * 16)
            vector_attention(e, 0, vector_prepare)
            vector_norm(e, 3, 0, PAIRS, ln_vec, PAIRS)

            def ff0(pair):
                n, u = num(pair, FF0_RING), pair[1]
                if active(pair, FF0_RING):
                    wait_some(e, f_xT, n - FF0_RING + 1)
                    vector_apply(n, ff0_xn[:, u, :], f_xn)
                late = at(pair, -FF0_LAG[2], FF0_RING)
                n, u = num(late, FF0_RING), late[1]
                if active(late, FF0_RING):
                    e.wait_ge(f_sq, n + 1)
                    nc.vector.tensor_copy(ff[:, n, :], bank[4 + u][:, 0:T]).then_inc(f_keep, 1)

            ff0_steps(e, ff0)
            e.wait_ge(f_root, 1)
            nc.vector.tensor_scalar(tmp[:, 1, :], tmp[:, 0, :], FFN_EPS, None, ALU.max).then_inc(f_norm, 1)
            e.wait_ge(f_norm, 1)
            nc.vector.tensor_scalar(tmp[:, 3, :], tmp[:, 1, :], FFN_EPS, None, ALU.add).then_inc(f_step, 1)
            e.wait_ge(f_step, 1)
            nc.vector.reciprocal(tmp[:, 3, :], tmp[:, 3, :]).then_inc(f_step, 1)
            e.wait_ge(f_step, 2)
            e.wait_ge(f_tanh, 1)
            nc.vector.tensor_tensor(gain[:, :], tmp[:, 2, :], tmp[:, 3, :], ALU.mult).then_inc(f_step, 1)
            e.wait_ge(f_step, 3)
            nc.vector.tensor_tensor(tmp[:, 1, :], gain[:, :], tmp[:, 0, :], ALU.mult).then_inc(f_step, 1)
            e.wait_ge(f_step, 4)
            nc.vector.tensor_scalar(tmp[:, 1, :], tmp[:, 1, :], FFN_EPS, None, ALU.max).then_inc(f_step, 1)
            e.wait_ge(f_step, 5)
            nc.vector.reciprocal(tmp[:, 3, :], tmp[:, 1, :]).then_inc(f_step, 1)
            e.wait_ge(f_step, 6)
            nc.vector.tensor_scalar(tmp[:, 3, :], tmp[:, 3, :], MAX_NORM, 1.0, ALU.mult, ALU.min).then_inc(f_step, 1)
            e.wait_ge(f_step, 7)
            nc.vector.tensor_tensor(gain[:, :], gain[:, :], tmp[:, 3, :], ALU.mult).then_inc(f_step, 1)
            e.wait_ge(f_step, 8)
            e.wait_ge(f_keep, PAIRS)
            with e.Fori(0, PAIRS // FF0_RING) as i:
                for u in range(FF0_RING):
                    n = FF0_RING * i + u
                    nc.vector.scalar_tensor_tensor(out=X[:, n, :], in0=ff[:, n, :], scalar=gain[:, bass.ds(n, 1)],
                                                   in1=X[:, n, :], op0=ALU.mult, op1=ALU.add).then_inc(f_upd, 1)
                for u in range(FF0_RING):
                    n = FF0_RING * i + u
                    e.wait_ge(f_upd, n + 1)
                    vector_stats(e, n)
            vector_norm(e, 4, 0, PAIRS, ln_vec, 2 * PAIRS + NORM_STEPS)
            vector_attention(e, 1)
            vector_norm(e, 5, 0, PAIRS, ln_vec, 3 * PAIRS + 2 * NORM_STEPS)

            def norm_chunk(c):
                for j in range(CHUNK):
                    wait_some(e, g_xT, c * CHUNK + j - 1)
                    vector_apply(c * CHUNK + j, xn[:, j % 2, :], g_xn)

            def update_chunk(c):
                for j in range(CHUNK):
                    e.wait_ge(g_down, c * CHUNK + j + 1)
                    e.wait_ge(g_bias, c * CHUNK + j + 1)
                    nc.vector.tensor_tensor(X[:, c * CHUNK + j, :], bank[4 + j % 2][:, 0:T],
                                            X[:, c * CHUNK + j, :], ALU.add).then_inc(g_upd, 1)

            norm_chunk(0)
            norm_chunk(1)
            with e.Fori(0, PAIRS // CHUNK - 2) as c:
                update_chunk(c)
                norm_chunk(c + 2)
            update_chunk(PAIRS // CHUNK - 2)
            update_chunk(PAIRS // CHUNK - 1)

        def pool_attention(e, l, extra=None):
            s = L[l]

            def split(name, pair, parts, rest, mid, done):
                if not active(pair):
                    return
                u = pair[1]
                bk = "A" if name == "q" else "B"
                if l == 0:
                    wait_apart(e, job_wait(s, l, bk, name, pair, "read"))
                    n, total = num(pair), 1
                else:
                    e.wait_ge(s[f"{name}_high"], num(pair) + 1)
                    nc.gpsimd.tensor_tensor(rest[:, u, :], rest[:, u, :], parts[:, u, 0, :],
                                            ALU.subtract).then_inc(s[mid], 1)
                    wait_apart(e, (s[mid], num(pair) * 2 + 1))
                    n, total = num(pair), 2
                nc.gpsimd.tensor_scalar(parts[:, u, 1, :], rest[:, u, :], 1.0, None,
                                        ALU.mult).then_inc(s[mid], 1)
                e.wait_ge(s[mid], (n + 1) * total)
                nc.gpsimd.tensor_tensor(parts[:, u, 2, :], rest[:, u, :], parts[:, u, 1, :],
                                        ALU.subtract).then_inc(s[done], 1)

            def rot_sum(bk, name, pair, n, rest):
                if not active(pair):
                    return
                wait_job(e, s, l, bk, name, pair, "read")
                e.wait_ge(s["rot_mul"], num(pair) * 2 + n + 1)
                wait_some(e, s[f"{name}_parts"], num(pair) - RING + 1)
                nc.gpsimd.tensor_tensor(rest[:, pair[1], :], rot[:, 2 * n, :], rot[:, 2 * n + 1, :],
                                        ALU.add).then_inc(s["rot_sum"], 1)

            def mask_group(pair, g):
                if not active(pair):
                    return
                wait_apart(e, (s["exped"], num(pair) * HPP + 4 * g + 4))
                first = (g % 2) * 4
                half = P // 2

                def keep(blk, lo, width, base, sign):
                    part = probs[:, first:first + 4, blk * WIN + lo:blk * WIN + lo + width]
                    return nc.gpsimd.affine_select(out=part, in_=part, compare_op=ALU.is_ge, fill=0.0, base=base,
                                                   pattern=[[0, 4], [-sign, width]], channel_multiplier=sign)

                keep(0, 0, half, BAND, -1).then_inc(s["mask_step"], 1)
                keep(0, half, P, BAND - half, 1).then_inc(s["mask_step"], 1)
                keep(1, 0, P, BAND - (P - BAND), -1).then_inc(s["mask_step"], 1)
                wait_apart(e, (s["mask_step"], (num(pair) * 4 + g + 1) * 3))
                keep(1, P, half, P + BAND - BAND - P + 0, 1).then_inc(s["masked"], 1)

            def gate(pair):
                if not active(pair):
                    return
                wait_job(e, s, l, "B", "out", pair, "read")
                e.wait_ge(s[f"side_in{pair[1]}"], (pair[0] + 1) * 16)
                wait_job(e, s, l, "B", "mix", at(pair, -1), "filled")
                nc.gpsimd.tensor_tensor(gated, relu_out, side[:, pair[1], :],
                                        ALU.mult).then_inc(s["gated"], 1)

            def iteration(r):
                p1, p3, m1 = at(r, 1), at(r, AHEAD), at(r, -1)
                if l == 0:
                    mask_group(m1, 3)
                    mask_group(r, 0)
                    split("q", p3, Qp, q_rest, "q_mid", "q_parts")
                    mask_group(r, 1)
                    split("k", p3, Kp, k_rest, "k_mid", "k_parts")
                    gate(m1)
                    mask_group(r, 2)
                else:
                    rot_sum("A", "q", p3, 0, q_rest)
                    rot_sum("B", "k", p3, 1, k_rest)
                    split("q", p3, Qp, q_rest, "q_mid", "q_parts")
                    split_max(e, nc.gpsimd, s, l, p1, 0)
                    split("k", p3, Kp, k_rest, "k_mid", "k_parts")
                    split_max(e, nc.gpsimd, s, l, p1, 1)

            iterations(e, iteration, extra and (lambda n: extra(e, n)))

        def pool_prepare(e, n):
            if n != -2:
                return
            dequantise(e, nc.gpsimd, up_f, up_raw, up_scale, HB * T // QBLOCK, dequant_up)
            for blk in range(2):
                nc.gpsimd.tensor_tensor(ff0_w[:, blk, :], ff0_w[:, blk, :], ff0_scale[:, :],
                                        ALU.mult).then_inc(ff0_scaled, 1)

        @block.gpsimd
        def _(e):
            nc.gpsimd.memset(Qs[:, :, :, :].rearrange("p a h t -> p (a h t)").bitcast(i32), 0).then_inc(cleared_q, 1)
            nc.gpsimd.memset(V[:, :, :, :, :], 0.0).then_inc(cleared_q, 1)
            e.wait_ge(cleared_q, 2)
            nc.gpsimd.memset(V[:, :, :, :, HD:HD + 1], 1.0).then_inc(cleared_q, 1)
            pool_attention(e, 0, pool_prepare)
            pool_attention(e, 1)

            def add_bias(c):
                for j in range(CHUNK):
                    e.wait_ge(g_xn, c * CHUNK + j + 1)
                    nc.gpsimd.tensor_tensor(X[:, c * CHUNK + j, :], X[:, c * CHUNK + j, :], down_b[:, :],
                                            ALU.add).then_inc(g_bias, 1)

            with e.Fori(0, PAIRS // CHUNK) as c:
                add_bias(c)


def _bd(m):
    import numpy as np
    z = np.zeros_like(m)
    return np.block([[m, z], [z, m]])


def _layouts(i):
    import numpy as np
    f = {k: np.asarray(v) for k, v in i.items()}
    dh = np.arange(CH).reshape(HEADS, HD).T.reshape(-1)
    turned = np.roll(dh.reshape(HD, HEADS), HD // 2, axis=0).reshape(-1)
    w_in, b_in = f["L0_xattn_w_in"], f["L0_xattn_b_in"]
    wq, wk, wv = w_in[0:CH], w_in[CH:2 * CH], w_in[2 * CH:3 * CH]
    bq, bk, bv = b_in[0:CH], b_in[CH:2 * CH], b_in[2 * CH:3 * CH]
    w0 = [wq[dh].T, wk[dh].T, wv.T, f["L0_xattn_w_out"].T, f["L0_xattn_w_ct"]]
    b0 = [bq[dh], bk[dh], bv, f["L0_xattn_b_out"], f["L0_xattn_b_ct"]]
    wq, wk, bq, bk = f["L1_xattn_Wq"], f["L1_xattn_Wk"], f["L1_xattn_bq"], f["L1_xattn_bk"]
    w1 = [wq[dh].T, wq[turned].T, wk[dh].T, wk[turned].T, f["L1_xattn_Wv"].T, f["L1_xattn_Wo"].T]
    b1 = [bq[dh], bq[turned], bk[dh], bk[turned], f["L1_xattn_bv"], f["L1_xattn_bo"]]
    inv = (1.0 / 10000.0 ** (np.arange(0, HD, 2, dtype=np.float32) / HD)).astype(np.float32)
    ang = np.arange(T, dtype=np.float32)[None, :] * np.concatenate([inv, inv])[:, None]
    sign = np.where(np.arange(HD) < HD // 2, -1.0, 1.0)[:, None]
    cs = np.stack([np.cos(ang), np.sin(ang) * sign], 1).astype(np.float32)
    rope = np.tile(np.repeat(cs, HEADS, axis=0), (2, 1, 1))
    q = np.arange(P)[:, None]
    k = np.arange(WIN)[None, :]
    band = np.concatenate([np.where(abs((q + b * P) - (k + b * BAND)) <= BAND, 0.0, OUTSIDE) for b in range(2)], 1)
    c = np.ascontiguousarray

    def spread(per_sequence):
        m = per_sequence.reshape(2, HD, HEADS, *per_sequence.shape[1:])
        return m.swapaxes(0, 1).reshape(P, *per_sequence.shape[1:])

    w0 = [spread(_bd(w).T).T if n < 2 else _bd(w) for n, w in enumerate(w0)]
    w1 = [spread(_bd(w).T).T if n < 4 else _bd(w) for n, w in enumerate(w1)]
    b0 = [spread(np.tile(b, 2)) if n < 2 else np.tile(b, 2) for n, b in enumerate(b0)]
    b1 = [spread(np.tile(b, 2)) if n < 4 else np.tile(b, 2) for n, b in enumerate(b1)]
    rope = spread(rope)
    return {
        "x": f["x"], "ctx": f["ctx_2048"],
        "ident": np.eye(P, dtype=np.float32), "band": band.astype(np.float32),
        "rope": rope,
        "att_w0": c(np.stack(w0, 1)), "att_w1": c(np.stack(w1, 1)),
        "att_b0": c(np.stack(b0, 1)), "att_b1": c(np.stack(b1, 1)),
        "ff0_w": f["L0_ffn_weight"], "ff0_scale": f["L0_ffn_scale"],
        "down_b": f["L1_ffn_b_down"], "up_b": c(f["L1_ffn_b_up"].reshape(FF // P, P).T),
        "up_q": f["L1_ffn_w_up_q"], "up_scale": f["L1_ffn_w_up_scale"],
        "down_q": f["L1_ffn_w_down_q"], "down_scale": f["L1_ffn_w_down_scale"],
        "lora_in": c(np.concatenate([f["L1_ffn_w_up_lora_a"].T, f["L1_ffn_w_down_lora_a"].T], 1)),
        "lora_out": c(np.concatenate([f["L1_ffn_w_up_lora_b"], f["L1_ffn_w_down_lora_b"]], 1)),
    }


def kernel(**inputs):
    import numpy as np
    import concourse.bacc as bacc
    from concourse.bass_utils import run_bass_kernel_spmd

    nc = bacc.Bacc("TRN2", target_bir_lowering=False, num_devices=1)
    arrays, aps = {}, {}
    for name, value in _layouts(inputs).items():
        value = np.ascontiguousarray(value)
        arrays[f"in_{name}"] = value
        aps[name] = nc.dram_tensor(f"in_{name}", value.shape, mybir.dt.from_np(value.dtype),
                                   kind="ExternalInput").ap()
    out = nc.dram_tensor("out", (BATCH, CH, T), mybir.dt.float32, kind="ExternalOutput").ap()
    build(nc, aps, out)
    result = run_bass_kernel_spmd(nc, [arrays], core_ids=[0])
    return result.results[0]["out"]
```

```python
import concourse.bass as bass
from concourse import mybir
from contextlib import ExitStack

BATCH = 64
CH = 64
T = 256
HEADS = 8
HD = CH // HEADS
BAND = 64
FF = 1024
RANK = 16
QBLOCK = 64
P = 128
PAIRS = BATCH // 2
HPP = 2 * HEADS
PARTS = 3
SPLIT_ROWS = PARTS * PARTS * HD
SHIFT_ROW = 96
LN_EPS = 1e-5
FFN_EPS = 1e-7
MAX_NORM = 0.99
OUTSIDE = -1.0e30
WIN = T // 2 + BAND
RING = 3
VALUES_AT = (3, 2)
X_CHUNKS = 4
EARLY = PAIRS // X_CHUNKS
FF0_RING = 4
FF0_LAG = (2, 2, 4)
SCORE_BANKS = 3
AHEAD = 3
MINUS_ONES = -(1.0 + 383 / 2 ** 16)
COPY_ROW = 72


def at(r, k, ring=RING):
    i, u = r
    t = u + k
    return (i + t // ring, t % ring)


def num(r, ring=RING):
    return r[0] * ring + r[1]


def active(r, ring=RING):
    return not isinstance(r[0], int) or 0 <= num(r, ring) < PAIRS


JOBS = {
    "A": [("q", AHEAD), ("heads1", -1), ("v", 2), ("max0", 1), ("heads0", 0)],
    "B": [("max1", 0), ("k", AHEAD), ("back", -1), ("out", -1), ("mix", -1)],
}
FIRST_FULL, LAST_FULL = 1, PAIRS - 1 - AHEAD


def job_order(layer, bank, name, pair):
    jobs = [j for j in JOBS[bank] if layer == 0 or j[0] != "mix"]
    place = [j[0] for j in jobs].index(name)
    r = at(pair, -jobs[place][1])
    if isinstance(r[0], int):
        if not active(pair):
            return None
        n = sum(0 <= q + d < PAIRS for q in range(-AHEAD, num(r)) for _, d in jobs)
        return n + sum(0 <= num(r) + d < PAIRS for _, d in jobs[:place])
    before = sum(0 <= q + d < PAIRS for q in range(-AHEAD, FIRST_FULL) for _, d in jobs)
    return num(r) * len(jobs) + (before - FIRST_FULL * len(jobs) + place)


def build(nc, a, out):
    fp32 = mybir.dt.float32
    bf16 = mybir.dt.bfloat16
    i32 = mybir.dt.int32
    ALU = mybir.AluOpType
    ACT = mybir.ActivationFunctionType
    AX = mybir.AxisListType

    x_dram = a["x"].rearrange("(n b) c t -> (b c) n t", b=2)
    ctx_dram = a["ctx"].rearrange("(n b) c t -> n (b c) t", b=2)
    out_dram = out.rearrange("(n b) c t -> (b c) n t", b=2)

    stack = ExitStack()
    with stack:
        def sb(name, shape, dt=fp32):
            return stack.enter_context(nc.sbuf_tensor(name, shape, dt))

        def sem(name):
            return stack.enter_context(nc.semaphore(name))

        X = sb("X", [P, PAIRS, T])
        ident = sb("ident", [P, P])
        ident16 = sb("ident16", [P, P], bf16)
        band16 = sb("band16", [P, 2 * WIN], bf16)
        rope = sb("rope", [P, 2, T])
        att_w = [sb("att_w0", [P, 5, P]), sb("att_w1", [P, 4, P])]
        att_b = [sb("att_b0", [P, 5]), sb("att_b1", [P, 4])]
        out_bias = sb("out_bias", [P, 2])
        ff0_w = sb("ff0_w", [P, 2, T])
        ff0_scale = sb("ff0_scale", [P, T])
        up_w = sb("up_w", [P, 2, FF])
        down_w = sb("down_w", [P, FF // P, T])
        up_b = sb("up_b", [P, FF // P])
        down_b = sb("down_b", [P, T])
        up_scale = sb("up_scale", [P, FF // P, T // QBLOCK])
        down_scale = sb("down_scale", [P, 2, FF // QBLOCK])
        stats = sb("stats", [P, PAIRS, 6])
        mean = sb("mean", [P, PAIRS])
        var = sb("var", [P, PAIRS])
        rstd = sb("rstd", [P, PAIRS])
        tmp = sb("tmp", [P, 4, PAIRS])
        sumsq = sb("sumsq", [P, PAIRS])
        gain = sb("gain", [P, PAIRS])
        Qs = sb("Qs", [P, RING, HPP, T], bf16)
        Ks = sb("Ks", [P, RING, HPP, T], bf16)
        probs = sb("probs", [P, 8, 2 * T])
        V = sb("V", [P, RING, 2, HPP, 32])
        xn = sb("xn", [P, RING, T])
        side = sb("side", [P, RING, T])
        Qp = sb("Qp", [P, RING, PARTS, T], bf16)
        Kp = sb("Kp", [P, RING, PARTS, T], bf16)
        q_rest = sb("q_rest", [P, RING, T])
        k_rest = sb("k_rest", [P, RING, T])
        rot = sb("rot", [P, 4, T])
        row_max = sb("row_max", [P, RING, HPP, 2])
        max_parts = sb("max_parts", [P, 2, PARTS, HPP], bf16)
        max_rest = sb("max_rest", [P, 2, HPP])
        max_rows = sb("max_rows", [PARTS * HPP, 2, P], bf16)
        heads_sb = sb("heads_sb", [P, 2, 2 * T])
        rcp = sb("rcp", [P, 2, HPP])
        normed = sb("normed", [P, RING, 2, P])
        mixed_in = sb("mixed_in", [P, T])
        relu_out = rot[:, 0, :]
        gated = rot[:, 1, :]
        band_raw = rot[:, :, :].rearrange("p a t -> p (a t)")[:, 0:2 * WIN]
        ff = sb("ff", [P, PAIRS, T])
        ff0_xT = [xn[:, 0, :], xn[:, 1, :], xn[:, 2, :], normed[:, 0, :, :].rearrange("p a b -> p (a b)")]
        ff0_xn = [q_rest[:, 0, :], q_rest[:, 1, :], q_rest[:, 2, :], k_rest[:, 0, :]]
        junk = k_rest[:, 1:3, :]
        xT = (Ks[:, 0:2, :, :].rearrange("p a h t -> p (a h t)").bitcast(fp32)[:, 0:4 * T * 2]
              .rearrange("p (a b t) -> p a b t", a=2, b=2))
        up_raw = ff[:, 0:FF // P, :].bitcast(i32)
        down_raw = ff[:, FF // P:2 * FF // P, :].rearrange("p (a b) t -> p a (b t)", a=2).bitcast(i32)
        lora = probs[0:RANK, :, :].rearrange("p h t -> p (h t)")
        lora_in = lora[:, 0:T + FF]
        lora_out = lora[:, T + FF:2 * (T + FF)]
        up_f = ff[:, 2 * FF // P:3 * FF // P, :]
        down_f = ff[:, 3 * FF // P:4 * FF // P, :].rearrange("p (a b) t -> p a (b t)", a=2)
        hidden = [Qs[:, 0:2, :, :].rearrange("p a h t -> p (a h t)").bitcast(fp32)
                  .rearrange("p (h t) -> p h t", h=FF // P), probs]

        bank = [stack.enter_context(nc.psum_tensor(f"bank{n}", [P, 512], fp32)) for n in range(8)]
        exp_bank, pv_bank = bank[2:4], bank[4]
        score_bank = [bank[0], bank[1], bank[5]]
        job_bank = {"A": bank[6], "B": bank[7]}
        max_bank = {b: job_bank[b][0:PARTS * HPP, 0:P // 2].bitcast(bf16) for b in "AB"}

        passed = sem("passed")
        weights0_in = sem("weights0_in")
        consts_in = sem("consts_in")
        rounded = sem("rounded")
        x_in = [sem(f"x_in{c}") for c in range(X_CHUNKS)]
        ffn_in = sem("ffn_in")
        stored = sem("stored")
        cleared_q = sem("cleared_q")
        cleared_k = sem("cleared_k")
        x_vec = sem("x_vec")
        prep_ps = sem("prep_ps")
        prep_read = sem("prep_read")
        dequant_up = sem("dequant_up")
        dequant_down = sem("dequant_down")
        ff0_scaled = sem("ff0_scaled")
        ln_vec = sem("ln_vec")
        ln_var = sem("ln_var")
        ln_std = sem("ln_std")
        ln_ready = sem("ln_ready")
        L = []
        for l in range(2):
            L.append({n: sem(f"L{l}_{n}") for n in (
                "xn_ready", "side_in0", "side_in1", "side_in2", "A_filled", "A_read", "B_filled", "B_read", "q_high", "k_high",
                "q_mid", "k_mid", "q_parts", "k_parts", "turned", "rot_mul", "rot_sum", "q_in0", "q_in1", "q_in2", "k_in0", "k_in1", "k_in2",
                "stack_in0", "stack_in1", "stack_in2", "scored", "maxed", "max_step0", "max_step1", "max_parts0", "max_parts1", "max_in0", "max_in1", "shifted", "exped",
                "masked", "mask_step", "pv_done", "heads_out", "rcp_done", "mixed", "relued", "gated")})
        f_xn = sem("f_xn")
        f_xT = sem("f_xT")
        f_xTs = sem("f_xTs")
        f_mm = sem("f_mm")
        f_sq = sem("f_sq")
        f_keep = sem("f_keep")
        f_norm = sem("f_norm")
        f_root = sem("f_root")
        f_tanh = sem("f_tanh")
        f_step = sem("f_step")
        f_upd = sem("f_upd")
        g_xn = sem("g_xn")
        g_xT = sem("g_xT")
        g_xTs = sem("g_xTs")
        g_bias = sem("g_bias")
        g_up = sem("g_up")
        g_relu = sem("g_relu")
        g_down = sem("g_down")
        g_upd = sem("g_upd")

        SCALE = float(HD) ** -0.5
        win_of = [WIN, T]
        start_of = [lambda blk: blk * BAND, lambda blk: 0]
        STACK_IN = PARTS * 16
        HB = FF // P
        CONSTS = 5
        PREP_JOBS = {-2: range(0, HB), -1: range(HB, 4 * HB)}
        PREP_READS = FF // P + 2
        PREP_BANKS = bank[2:5]
        JOBS_B = len(JOBS["B"]) * PAIRS
        FFN_LOADS = 10
        NORM_STEPS = 6
        CHUNK = 4
        chunk_xn = [xn[:, 0, :], xn[:, 1, :], side[:, 0, :], side[:, 1, :]]

        def bank_of(pair, h):
            return score_bank[(HPP * pair[1] + h) % SCORE_BANKS]

        def iterations(e, body, extra=None, last=True):
            for n in range(-AHEAD, RING):
                body((n // RING, n % RING))
                if extra:
                    extra(n)
            with e.Fori(1, (LAST_FULL + 1) // RING) as i:
                for u in range(RING):
                    body((i, u))
            for n in range((LAST_FULL + 1) // RING * RING, PAIRS + (1 if last else 0)):
                body((n // RING, n % RING))
                if extra:
                    extra(n)

        def ff0_steps(e, step, tail, norm=None):
            for n in range(2 * FF0_RING):
                if n in tail:
                    tail[n]()
                step((n // FF0_RING, n % FF0_RING))
            if 2 * FF0_RING in tail:
                tail[2 * FF0_RING]()
            with e.Fori(2, PAIRS // FF0_RING - 1) as i:
                for u in range(FF0_RING):
                    step((i, u))
            if norm:
                norm()
            for n in range(PAIRS - FF0_RING, PAIRS + max(FF0_LAG)):
                step((n // FF0_RING, n % FF0_RING))

        def ff0_early(pair):
            return isinstance(pair[0], int) and num(pair, FF0_RING) < 2 * FF0_RING - FF0_LAG[0]

        def ff0_bank(pair):
            return bank[2 + (pair[1] % 2 if ff0_early(pair) else pair[1])]

        TAIL = ((PAIRS - 1) // RING, (PAIRS - 1) % RING)
        TAIL_NORM = PAIRS - CHUNK

        def wait_job(e, s, l, b, name, pair, what):
            n = job_order(l, b, name, pair)
            if n is not None:
                e.wait_ge(s[f"{b}_{what}"], n + 1)

        def wait_bank(e, s, l, b, name, pair):
            n = job_order(l, b, name, pair)
            if not (isinstance(n, int) and n == 0):
                e.wait_ge(s[f"{b}_read"], n)

        def wait_some(e, s, value):
            if not (isinstance(value, int) and value <= 0):
                e.wait_ge(s, value)

        def wait_apart(e, *waits):
            for w, v in waits:
                if v is not None and not (isinstance(v, int) and v <= 0):
                    e.wait_ge(w, v)
                    if not isinstance(v, int):
                        e.sem_inc(passed, 1)

        def job_wait(s, l, b, name, pair, what):
            n = job_order(l, b, name, pair)
            return s[f"{b}_{what}"], None if n is None else n + 1

        block = stack.enter_context(nc.Block())

        def sync_attention(e, l):
            s = L[l]
            q_stack, k_stack = Qs[:, :, :, :].tensor, Ks[:, :, :, :].tensor

            def load_side(pair):
                if not active(pair):
                    return
                if l == 0:
                    wait_apart(e, (s["gated"], num(pair) - RING + 1))
                else:
                    wait_apart(e, job_wait(s, l, "A", "v", at(pair, -RING), "filled"))
                e.dma_start(side[:, pair[1], :], ctx_dram[num(pair)]).then_inc(s[f"side_in{pair[1]}"], 16)

            n, slot = PARTS * HD, HPP * T
            row = RING * slot

            def lay_out(pair):
                if not active(pair):
                    return
                u = pair[1]
                first = u * slot
                wait_apart(e, (s["q_parts"], num(pair) + 1), (s["shifted"], (num(pair) - RING + 1) * HPP))
                for j in range(PARTS):
                    dst = bass.AP(q_stack, first + j * row, [[PARTS * row, HD], [T, HPP], [1, T]])
                    e.dma_start(dst, Qp[:, u, j, :]).then_inc(s[f"q_in{u}"], 16)
                e.wait_ge(s["k_parts"], num(pair) + 1)
                for i in range(PARTS):
                    e.dma_start(Ks[COPY_ROW + i * HD:COPY_ROW + (i + 1) * HD, u, :, :],
                                Kp[:, u, i, :]).then_inc(s[f"k_in{u}"], 16)

            def replicate(pair):
                if not active(pair):
                    return
                u = pair[1]
                first = u * slot
                e.wait_ge(s[f"q_in{u}"], (pair[0] + 1) * PARTS * 16)
                for i in range(1, PARTS):
                    e.dma_start(Qs[i * n:(i + 1) * n, u, :, :], Qs[0:n, u, :, :]).then_inc(s[f"stack_in{u}"], 16)
                e.wait_ge(s[f"k_in{u}"], (pair[0] + 1) * PARTS * 16)
                e.dma_start(bass.AP(k_stack, first, [[row, SPLIT_ROWS], [1, slot]]),
                            bass.AP(k_stack, first + COPY_ROW * row, [[row, n], [0, PARTS], [1, slot]])
                            ).then_inc(s[f"stack_in{u}"], 16)

            def shift_rows(pair, half):
                if not active(pair):
                    return
                wait_job(e, s, l, *(("A", "max0"), ("B", "max1"))[half], pair, "read")
                e.dma_start(Qs[SHIFT_ROW:SHIFT_ROW + PARTS, pair[1], half * HEADS:(half + 1) * HEADS, :],
                            max_rows[:, half, :]).then_inc(s[f"max_in{half}"], 16)

            def iteration(r):
                load_side(at(r, AHEAD + 1 if l else 0))
                lay_out(at(r, 2))
                shift_rows(r, 1)
                replicate(at(r, 2))
                shift_rows(at(r, 1), 0)

            if l:
                load_side((0, 0))
            iterations(e, iteration)

        @block.sync
        def _(e):
            e.dma_start(att_w[0][:, :, :], a["att_w0"]).then_inc(weights0_in, 16)
            e.dma_start(att_b[0][:, :], a["att_b0"]).then_inc(weights0_in, 16)
            e.dma_start(ident[:, :], a["ident"]).then_inc(consts_in, 16)
            e.dma_start(band_raw, a["band"]).then_inc(consts_in, 16)
            e.dma_start(att_w[1][:, :, :], a["att_w1"]).then_inc(consts_in, 16)
            e.dma_start(att_b[1][:, :], a["att_b1"]).then_inc(consts_in, 16)
            e.dma_start(rope[:, :, :], a["rope"]).then_inc(consts_in, 16)
            e.wait_ge(cleared_q, 3)
            e.wait_ge(cleared_k, 2)
            sync_attention(e, 0)
            e.wait_ge(L[0]["B_read"], JOBS_B)
            sync_attention(e, 1)
            with e.Fori(0, PAIRS // CHUNK) as c:
                e.wait_ge(g_upd, c * CHUNK + CHUNK)
                e.dma_start(out_dram[:, bass.ds(c * CHUNK, CHUNK), :],
                            X[:, bass.ds(c * CHUNK, CHUNK), :]).then_inc(stored, 16)
            e.wait_ge(stored, PAIRS // CHUNK * 16)

        def tensor_attention(e, l, extra=None):
            s = L[l]
            w = att_w[l]
            WQ, WK, WV, WO = 0, 1, 2, 3
            win, start = win_of[l], start_of[l]

            def score_head(pair, h):
                if not active(pair):
                    return
                n = num(pair) * HPP + h
                if h == 0:
                    e.wait_ge(s[f"stack_in{pair[1]}"], (pair[0] + 1) * STACK_IN)
                wait_some(e, s["maxed"], n - SCORE_BANKS + 1)
                dst = bank_of(pair, h)
                if l == 0:
                    nc.tensor.matmul(dst[:, 0:2 * win], ident16[:, :], band16[:, :], start=True, stop=False)
                for blk in range(2):
                    last = nc.tensor.matmul(dst[:, blk * win:(blk + 1) * win],
                                            Qs[0:SHIFT_ROW, pair[1], h, blk * P:(blk + 1) * P],
                                            Ks[0:SHIFT_ROW, pair[1], h, start(blk):start(blk) + win],
                                            start=(l == 1), stop=(l == 1 or blk == 1))
                last.then_inc(s["scored"], 1)

            def shifted_head(pair, h):
                if not active(pair):
                    return
                n = num(pair) * HPP + h
                if h % HEADS == 0:
                    e.wait_ge(s[f"max_in{h // HEADS}"], (num(pair) + 1) * 16)
                wait_some(e, s["exped"], n - 1)
                dst = exp_bank[h % 2]
                for blk in range(2):
                    last = nc.tensor.matmul(dst[:, blk * win:(blk + 1) * win],
                                            Ks[:, pair[1], h, blk * P:(blk + 1) * P],
                                            Qs[:, pair[1], h, start(blk):start(blk) + win],
                                            start=True, stop=True)
                last.then_inc(s["shifted"], 1)

            def values_group(pair, g):
                if not active(pair):
                    return
                if l == 0:
                    e.wait_ge(s["masked"], num(pair) * 4 + g + 1)
                else:
                    e.wait_ge(s["exped"], num(pair) * HPP + 4 * g + 4)
                if g == 0:
                    wait_job(e, s, l, "A", "v", pair, "read")
                if g % 2 == 0:
                    wait_some(e, s["heads_out"], num(pair) * 2 + g // 2)
                dst = pv_bank
                for blk in range(2):
                    for j in range(4):
                        head = 4 * g + j
                        first = (g % 2) * T + start(blk)
                        last = nc.tensor.matmul(dst[32 * j:32 * j + 32, first:first + win],
                                                V[:, pair[1], blk, head, :],
                                                probs[:, head % 8, blk * win:(blk + 1) * win],
                                                start=(blk == 0), stop=(blk == 1), skip_group_check=True)
                last.then_inc(s["pv_done"], 1)

            def project(b, name, pair, weight, source, wait):
                if not active(pair):
                    return
                wait()
                wait_bank(e, s, l, b, name, pair)
                nc.tensor.matmul(job_bank[b][:, 0:T], w[:, weight, :], source,
                                 start=True, stop=True).then_inc(s[f"{b}_filled"], 1)

            def project_v(pair):
                if not active(pair):
                    return
                src = side if l else xn
                wait_bank(e, s, l, "A", "v", pair)
                for blk in range(2):
                    last = nc.tensor.matmul(job_bank["A"][:, blk * P:(blk + 1) * P],
                                            src[:, pair[1], blk * P:(blk + 1) * P], w[:, WV, :],
                                            start=True, stop=True)
                last.then_inc(s["A_filled"], 1)

            def turn_max(b, pair, half):
                if not active(pair):
                    return
                wait_apart(e, (s[f"{b}_read"], job_order(l, b, f"max{half}", pair)),
                        (s[f"max_parts{half}"], num(pair) + 1))
                nc.tensor.transpose(max_bank[b], max_parts[:, half, :, :].rearrange("p n h -> p (n h)"),
                                    ident16[:, :]).then_inc(s[f"{b}_filled"], 1)

            def turn_heads(pair, half):
                if not active(pair):
                    return
                wait_bank(e, s, l, "A", f"heads{half}", pair)
                e.wait_ge(s["heads_out"], num(pair) * 2 + half + 1)
                for blk in range(2):
                    for g in range(2):
                        last = nc.tensor.transpose(job_bank["A"][:, (blk * 2 + g) * P:(blk * 2 + g + 1) * P],
                                                   heads_sb[:, half, g * T + blk * P:g * T + (blk + 1) * P],
                                                   ident[:, :])
                last.then_inc(s["A_filled"], 1)

            def turn_back(pair):
                if not active(pair):
                    return
                wait_bank(e, s, l, "B", "back", pair)
                wait_job(e, s, l, "A", "heads1", pair, "read")
                for blk in range(2):
                    last = nc.tensor.transpose(job_bank["B"][:, blk * P:(blk + 1) * P],
                                               normed[:, pair[1], blk, :], ident[:, :])
                last.then_inc(s["B_filled"], 1)

            tail = {0: lambda: values_group(TAIL, 3), 2: lambda: turn_heads(TAIL, 1), 4: lambda: turn_back(TAIL),
                    5: lambda: project("B", "out", TAIL, WO, mixed_in[:, :],
                                       lambda: wait_job(e, s, l, "B", "back", TAIL, "read"))}
            if l == 0:
                tail[8] = lambda: project("B", "mix", TAIL, 4, gated, lambda: e.wait_ge(s["gated"], PAIRS))

            def iteration(r):
                p1, p2, p3, m1 = at(r, 1), at(r, 2), at(r, AHEAD), at(r, -1)
                for h in range(HPP):
                    if h == 3:
                        turn_max("B", r, 1)
                    if h == 1:
                        project("A", "q", p3, WQ, xn[:, p3[1], :],
                                lambda: e.wait_ge(s["xn_ready"], num(p3) + 1))
                    if h == 4 + l:
                        project("B", "k", p3, WK,
                                (side if l else xn)[:, p3[1], :],
                                lambda: l and e.wait_ge(s[f"side_in{p3[1]}"], (p3[0] + 1) * 16))
                    if h == 5:
                        turn_heads(m1, 1)
                    if h == 8:
                        turn_back(m1)
                    if h == 8:
                        project_v(p2)
                    if h == 10:
                        project("B", "out", m1, WO, mixed_in[:, :],
                                lambda: wait_job(e, s, l, "B", "back", m1, "read"))
                    if h == 12:
                        turn_max("A", p1, 0)
                    if h == 14 and l == 0:
                        project("B", "mix", m1, 4, gated,
                                lambda: e.wait_ge(s["gated"], num(m1) + 1))
                    if h == 14:
                        turn_heads(r, 0)
                    score_head(p1, h)
                    shifted_head(r, h)
                    if h % 4 == VALUES_AT[l]:
                        values_group(m1 if h < 4 else r, (h // 4 - 1) % 4)

            iterations(e, iteration, extra and (lambda n: extra(e, n)), last=False)
            return tail

        def tensor_prepare(e, n):
            if n not in PREP_JOBS:
                return
            if n == -2:
                e.wait_ge(consts_in, CONSTS * 16)
                e.wait_ge(rounded, 2)
                e.wait_ge(ffn_in, FFN_LOADS * 16)
                e.wait_ge(dequant_down, 2)
            blocks = ([("down", hb, blk) for hb in range(HB) for blk in range(2)] +
                      [("up", hb, blk) for blk in range(2) for hb in range(HB)])
            for job in PREP_JOBS[n]:
                which, hb, blk = blocks[job]
                if job == 2 * HB:
                    e.wait_ge(dequant_up, 2)
                if job % 4 == 0:
                    wait_some(e, prep_read, job // 4 - 2)
                dst = PREP_BANKS[job // 4 % 3][:, job % 4 * P:(job % 4 + 1) * P]
                if which == "down":
                    nc.tensor.matmul(dst, down_f[:, blk, hb * P:(hb + 1) * P], ident[:, :], start=True, stop=False)
                    nc.tensor.matmul(dst, lora_in[:, T + hb * P:T + (hb + 1) * P],
                                     lora_out[:, FF + blk * P:FF + (blk + 1) * P],
                                     start=False, stop=True).then_inc(prep_ps, 1)
                else:
                    nc.tensor.matmul(dst, up_f[:, hb, blk * P:(blk + 1) * P], ident[:, :], start=True, stop=False)
                    nc.tensor.matmul(dst, lora_in[:, blk * P:(blk + 1) * P], lora_out[:, hb * P:(hb + 1) * P],
                                     start=False, stop=True).then_inc(prep_ps, 1)
            if n == -1:
                wait_some(e, prep_read, HB - 2)
                for l in range(2):
                    nc.tensor.matmul(PREP_BANKS[HB % 3][:, l:l + 1], att_w[l][:, 3, :], att_b[l][:, 2:3],
                                     start=True, stop=True).then_inc(prep_ps, 1)
                e.wait_ge(prep_read, PREP_READS)

        @block.tensor
        def _(e):
            e.wait_ge(weights0_in, 2 * 16)
            tail = tensor_attention(e, 0, tensor_prepare)

            def ff0(pair):
                n, u = num(pair, FF0_RING), pair[1]
                if active(pair, FF0_RING):
                    e.wait_ge(f_xn, n + 1)
                    wait_some(e, f_xTs, n - 1)
                    for blk in range(2):
                        last = nc.tensor.transpose(bank[u % 2][:, blk * P:(blk + 1) * P],
                                                   ff0_xn[u][:, blk * P:(blk + 1) * P], ident[:, :])
                    last.then_inc(f_xT, 1)
                late = at(pair, -FF0_LAG[0], FF0_RING)
                n, u = num(late, FF0_RING), late[1]
                if active(late, FF0_RING):
                    e.wait_ge(f_xTs, n + 1)
                    wait_some(e, f_keep, n - 1 if ff0_early(late) else n - FF0_RING + 1)
                    for blk in range(2):
                        last = nc.tensor.matmul(ff0_bank(late)[:, 0:T], ff0_xT[u][:, blk * P:(blk + 1) * P],
                                                ff0_w[:, blk, :], start=(blk == 0), stop=(blk == 1))
                    last.then_inc(f_mm, 1)

            e.wait_ge(L[0]["maxed"], PAIRS * HPP)
            e.wait_ge(L[0]["exped"], PAIRS * HPP)
            e.wait_ge(ff0_scaled, 2)
            ff0_steps(e, ff0, tail)
            e.wait_ge(f_keep, PAIRS)
            tail = tensor_attention(e, 1)

            def turn_chunk(c, cu):
                for j in range(CHUNK):
                    e.wait_ge(g_xn, c * CHUNK + j + 1)
                    if j == 0:
                        wait_some(e, g_xTs, 2 * c)
                    for blk in range(2):
                        last = nc.tensor.transpose(bank[blk][:, j * P:(j + 1) * P],
                                                   chunk_xn[j][:, blk * P:(blk + 1) * P], ident[:, :])
                    last.then_inc(g_xT, 1)

            def up_chunk(c, cu, beside={}):
                e.wait_ge(g_xTs, 2 * c + 2)
                for hb in range(HB):
                    if hb in beside:
                        beside[hb]()
                    wait_some(e, g_relu, HB * c + hb - 1)
                    for blk in range(2):
                        last = nc.tensor.matmul(bank[2 + hb % 2][:, :], up_w[:, blk, hb * P:(hb + 1) * P],
                                                xT[:, cu, blk, :], start=(blk == 0), stop=(blk == 1))
                    last.then_inc(g_up, 1)

            def down_chunk(c, cu):
                e.wait_ge(g_relu, HB * c + HB)
                for j in range(CHUNK):
                    wait_some(e, g_upd, CHUNK * c + j - 1)
                    for hb in range(HB):
                        last = nc.tensor.matmul(bank[4 + j % 2][:, 0:T],
                                                hidden[cu][:, hb, j * P:(j + 1) * P], down_w[:, hb, :],
                                                start=(hb == 0), stop=(hb == HB - 1))
                    last.then_inc(g_down, 1)

            e.wait_ge(L[1]["maxed"], PAIRS * HPP)
            e.wait_ge(L[1]["exped"], PAIRS * HPP)
            turn_chunk(0, 0)
            up_chunk(0, 0, tail)
            turn_chunk(1, 1)
            down_chunk(0, 0)
            up_chunk(1, 1)
            with e.Fori(1, PAIRS // CHUNK // 2) as i:
                turn_chunk(i * 2, 0)
                down_chunk(i * 2 - 1, 1)
                up_chunk(i * 2, 0)
                turn_chunk(i * 2 + 1, 1)
                down_chunk(i * 2, 0)
                up_chunk(i * 2 + 1, 1)
            down_chunk(PAIRS // CHUNK - 1, 1)

        def scalar_attention(e, l, extra=None):
            s = L[l]
            b = att_b[l]
            win, start = win_of[l], start_of[l]

            def exp_head(pair, h):
                if not active(pair):
                    return
                n = num(pair) * HPP + h
                e.wait_ge(s["shifted"], n + 1)
                if h % 4 == 0:
                    wait_some(e, s["pv_done"], num(pair) * 4 + h // 4 - 1)
                nc.scalar.activation(probs[:, h % 8, 0:2 * win], exp_bank[h % 2][:, 0:2 * win], ACT.Exp,
                                     scale=SCALE).then_inc(s["exped"], 1)

            def high_part(bk, name, pair, parts, column):
                if not active(pair):
                    return
                u = pair[1]
                wait_some(e, s[f"{name}_in{u}"], pair[0] * PARTS * 16)
                if l == 0:
                    wait_job(e, s, l, bk, name, pair, "filled")
                    nc.scalar.activation(parts[:, u, 0, :], job_bank[bk][:, 0:T], ACT.Identity,
                                         bias=b[:, column:column + 1]).then_inc(s[f"{name}_high"], 1)
                else:
                    e.wait_ge(s["rot_sum"], num(pair) * 2 + (1 if name == "q" else 2))
                    rest = q_rest if name == "q" else k_rest
                    nc.scalar.activation(parts[:, u, 0, :], rest[:, u, :],
                                         ACT.Copy).then_inc(s[f"{name}_high"], 1)

            def turn_rows(bk, name, pair, n, column):
                if not active(pair):
                    return
                wait_job(e, s, l, bk, name, pair, "filled")
                wait_some(e, s["rot_sum"], num(pair) * 2 - 1 + n)
                half = P // 2
                for here, there in ((slice(0, half), slice(half, P)), (slice(half, P), slice(0, half))):
                    nc.scalar.activation(rot[here, 2 * n + 1, :], job_bank[bk][there, 0:T], ACT.Identity,
                                         bias=b[there, column:column + 1]).then_inc(s["turned"], 1)

            def values_out(pair):
                if not active(pair):
                    return
                wait_job(e, s, l, "A", "v", pair, "filled")
                wait_some(e, s["pv_done"], (num(pair) - RING + 1) * 4)
                nc.scalar.activation(V[:, pair[1], :, :, 0:HD].rearrange("p b h d -> p (b h) d"),
                                     job_bank["A"][:, 0:2 * P].rearrange("p (n d) -> p n d", d=HD),
                                     ACT.Copy).then_inc(s["A_read"], 1)

            def heads_out(pair, half):
                if not active(pair):
                    return
                e.wait_ge(s["pv_done"], num(pair) * 4 + 2 * half + 2)
                wait_job(e, s, l, "A", f"heads{half}", at(pair, -1), "filled")
                nc.scalar.activation(heads_sb[:, half, :], pv_bank[:, :],
                                     ACT.Copy).then_inc(s["heads_out"], 1)

            def max_out(bk, pair, half):
                if not active(pair):
                    return
                wait_job(e, s, l, bk, f"max{half}", pair, "filled")
                wait_some(e, s[f"max_in{half}"], num(pair) * 16)
                nc.scalar.activation(max_rows[:, half, :], max_bank[bk], ACT.Copy).then_inc(s[f"{bk}_read"], 1)

            def back_out(pair):
                if not active(pair):
                    return
                wait_job(e, s, l, "B", "back", pair, "filled")
                nc.scalar.activation(mixed_in[:, :], job_bank["B"][:, 0:T], ACT.Copy).then_inc(s["B_read"], 1)

            def relu(pair):
                if not active(pair):
                    return
                wait_job(e, s, l, "B", "out", pair, "filled")
                wait_some(e, s["gated"], num(pair))
                nc.scalar.activation(relu_out, job_bank["B"][:, 0:T], ACT.Relu,
                                     bias=out_bias[:, 0:1]).then_inc(s["B_read"], 1)

            tail = {1: lambda: heads_out(TAIL, 1), 4: lambda: back_out(TAIL)}
            if l == 0:
                tail[6] = lambda: relu(TAIL)

            def iteration(r):
                p1, p2, p3, m1 = at(r, 1), at(r, 2), at(r, AHEAD), at(r, -1)
                for h in range(HPP):
                    if h == 2 and l == 0:
                        high_part("A", "q", p3, Qp, 0)
                    if h == 2 and l == 1:
                        turn_rows("A", "q", p3, 0, 0)
                    if h == 3:
                        max_out("B", r, 1)
                    if h == VALUES_AT[l] + 1:
                        heads_out(m1, 1)
                    if h == 4 and l == 0:
                        high_part("B", "k", p3, Kp, 1)
                    if h == 5 and l == 1:
                        turn_rows("B", "k", p3, 1, 1)
                    if h == 6 and l == 1:
                        high_part("A", "q", p3, Qp, 0)
                    if h == 8:
                        back_out(m1)
                    if h == 9 and l == 1:
                        high_part("B", "k", p3, Kp, 1)
                    if h == 8:
                        values_out(p2)
                    if h == 10 and l == 0:
                        relu(m1)
                    if h == 12:
                        max_out("A", p1, 0)
                    if h == VALUES_AT[l] + 9:
                        heads_out(r, 0)
                    exp_head(r, h)

            iterations(e, iteration, extra and (lambda n: extra(e, n)), last=False)
            return tail

        def scalar_sqrt(first, end):
            nc.scalar.activation(rstd[:, first:end], var[:, first:end], ACT.Sqrt).then_inc(ln_std, 1)

        def scalar_edges(e, n):
            if n == 0:
                e.wait_ge(ln_var, 6)
                scalar_sqrt(EARLY, PAIRS)
            if n == TAIL_NORM + 1:
                e.wait_ge(ln_var, 7)
                scalar_sqrt(0, TAIL_NORM)

        def scalar_loads(e):
            e.dma_start(ff0_w[:, :, :], a["ff0_w"].rearrange("(b p) n -> p b n", p=P)).then_inc(ffn_in, 16)
            e.dma_start(ff0_scale[:, :], a["ff0_scale"].partition_broadcast(P)).then_inc(ffn_in, 16)
            e.dma_start(down_b[:, :], a["down_b"].partition_broadcast(P)).then_inc(ffn_in, 16)
            e.dma_start(up_b[:, :], a["up_b"]).then_inc(ffn_in, 16)
            e.dma_start(up_raw, a["up_q"].rearrange("(b p) n -> p b n", p=P)).then_inc(ffn_in, 16)
            e.dma_start(up_scale[:, :, :], a["up_scale"].rearrange("(b p) n -> p b n", p=P)).then_inc(ffn_in, 16)
            e.dma_start(down_raw, a["down_q"].rearrange("(b p) n -> p b n", p=P)).then_inc(ffn_in, 16)
            e.dma_start(down_scale[:, :, :],
                        a["down_scale"].rearrange("(b p) n -> p b n", p=P)).then_inc(ffn_in, 16)
            e.dma_start(lora_in, a["lora_in"]).then_inc(ffn_in, 16)
            e.dma_start(lora_out, a["lora_out"]).then_inc(ffn_in, 16)

        def scalar_prepare(e, n):
            if n == -AHEAD:
                e.wait_ge(consts_in, CONSTS * 16)
                nc.scalar.activation(ident16[:, :], ident[:, :], ACT.Copy).then_inc(rounded, 1)
                nc.scalar.activation(band16[:, :], band_raw, ACT.Copy).then_inc(rounded, 1)
            if n in PREP_JOBS:
                for b in range(PREP_JOBS[n].start // 4, PREP_JOBS[n].stop // 4):
                    e.wait_ge(prep_ps, 4 * b + 4)
                    if b < HB // 2:
                        dst = down_w[:, 2 * b:2 * b + 2, :].rearrange("p h t -> p (h t)")
                    else:
                        dst = up_w[:, (b - HB // 2) // 2, b % 2 * 4 * P:(b % 2 + 1) * 4 * P]
                    nc.scalar.activation(dst, PREP_BANKS[b % 3][:, :], ACT.Copy).then_inc(prep_read, 1)
            if n == -1:
                e.wait_ge(prep_ps, 4 * HB + 2)
                for l in range(2):
                    nc.scalar.activation(out_bias[:, l:l + 1], PREP_BANKS[HB % 3][:, l:l + 1], ACT.Identity,
                                         bias=att_b[l][:, 3:4]).then_inc(prep_read, 1)
            if n == 0:
                e.wait_ge(ln_var, 2)
                scalar_sqrt(EARLY, PAIRS)
            if n == TAIL_NORM + 1:
                e.wait_ge(ln_var, 3)
                scalar_sqrt(0, TAIL_NORM)

        @block.scalar
        def _(e):
            for c in range(X_CHUNKS):
                e.dma_start(X[:, c * EARLY:(c + 1) * EARLY, :],
                            x_dram[:, c * EARLY:(c + 1) * EARLY, :]).then_inc(x_in[c], 16)
                if c == 0:
                    scalar_loads(e)
            e.wait_ge(ln_var, 1)
            scalar_sqrt(0, EARLY)
            e.wait_ge(weights0_in, 2 * 16)
            e.wait_ge(cleared_q, 3)
            tail = scalar_attention(e, 0, scalar_prepare)

            def ff0(pair):
                n, u = num(pair, FF0_RING), pair[1]
                if active(pair, FF0_RING):
                    e.wait_ge(f_xT, n + 1)
                    wait_some(e, f_mm, n - FF0_RING + 1)
                    nc.scalar.activation(ff0_xT[u], bank[u % 2][:, 0:T], ACT.Copy).then_inc(f_xTs, 1)
                late = at(pair, -FF0_LAG[1], FF0_RING)
                n, u = num(late, FF0_RING), late[1]
                if active(late, FF0_RING):
                    e.wait_ge(f_mm, n + 1)
                    wait_some(e, f_sq, n - 1)
                    nc.scalar.activation(junk[:, u % 2, :], ff0_bank(late)[:, 0:T], ACT.Square,
                                         accum_out=sumsq[:, bass.ds(n, 1)]).then_inc(f_sq, 1)

            def norm():
                e.wait_ge(ln_var, 4)
                scalar_sqrt(TAIL_NORM, PAIRS)

            ff0_steps(e, ff0, tail, norm)
            e.wait_ge(f_sq, PAIRS)
            nc.scalar.activation(tmp[:, 0, :], sumsq[:, :], ACT.Sqrt).then_inc(f_root, 1)
            e.wait_ge(f_norm, 1)
            nc.scalar.activation(tmp[:, 2, :], tmp[:, 1, :], ACT.Tanh).then_inc(f_tanh, 1)
            e.wait_ge(ln_var, 5)
            scalar_sqrt(0, EARLY)
            tail = scalar_attention(e, 1, scalar_edges)

            def turn_out(c, cu):
                e.wait_ge(g_xT, CHUNK * c + CHUNK)
                wait_some(e, g_up, HB * c - HB)
                for blk in range(2):
                    nc.scalar.activation(xT[:, cu, blk, :], bank[blk][:, :], ACT.Copy).then_inc(g_xTs, 1)

            def relu_chunk(c, cu, beside={}):
                wait_some(e, g_down, CHUNK * c - CHUNK)
                for hb in range(HB):
                    if hb in beside:
                        beside[hb]()
                    e.wait_ge(g_up, HB * c + hb + 1)
                    nc.scalar.activation(hidden[cu][:, hb, :], bank[2 + hb % 2][:, :], ACT.Relu,
                                         bias=up_b[:, hb:hb + 1]).then_inc(g_relu, 1)

            turn_out(0, 0)
            relu_chunk(0, 0, tail)
            turn_out(1, 1)
            e.wait_ge(ln_var, 8)
            scalar_sqrt(TAIL_NORM, PAIRS)
            relu_chunk(1, 1)
            with e.Fori(1, PAIRS // CHUNK // 2) as i:
                turn_out(i * 2, 0)
                relu_chunk(i * 2, 0)
                turn_out(i * 2 + 1, 1)
                relu_chunk(i * 2 + 1, 1)

        def dequantise(e, engine, dst, raw, scale, blocks, signal):
            e.wait_ge(ffn_in, FFN_LOADS * 16)
            engine.tensor_scalar(dst, raw, 7.5, None, ALU.subtract).then_inc(signal, 1)
            e.wait_ge(signal, 1)
            flat = dst.rearrange("p a b -> p (a b)").rearrange("p (s q) -> p s q", q=QBLOCK)
            engine.tensor_tensor(flat, flat, scale[:, :, :].rearrange("p a s -> p (a s)").unsqueeze(2)
                                 .broadcast_to([P, blocks, QBLOCK]), ALU.mult).then_inc(signal, 1)

        def split_max(e, engine, s, l, pair, half):
            if not active(pair):
                return
            src = row_max[:, pair[1], half * HEADS:(half + 1) * HEADS, :].rearrange("p h b -> p (h b)")
            step, done = s[f"max_step{half}"], num(pair) * PARTS
            parts, rest = max_parts[:, half, :, :], max_rest[:, half, :]
            wait_apart(e, (s["maxed"], num(pair) * HPP + HEADS * (half + 1)),
                       job_wait(s, l, *(("A", "max0"), ("B", "max1"))[half], at(pair, -1), "filled"))
            engine.tensor_scalar(parts[:, 0, :], src, 1.0, None, ALU.mult).then_inc(step, 1)
            e.wait_ge(step, done + 1)
            engine.tensor_tensor(rest, src, parts[:, 0, :], ALU.subtract).then_inc(step, 1)
            wait_apart(e, (step, done + 2))
            engine.tensor_scalar(parts[:, 1, :], rest, 1.0, None, ALU.mult).then_inc(step, 1)
            e.wait_ge(step, done + 3)
            engine.tensor_tensor(parts[:, 2, :], rest, parts[:, 1, :],
                                 ALU.subtract).then_inc(s[f"max_parts{half}"], 1)

        def vector_stats(e, pair_value, signal=None):
            nc.vector.bn_stats(stats[:, pair_value, :], X[:, pair_value, :]).then_inc(signal or ln_vec, 1)

        def vector_norm(e, round_, first, end, vec, base):
            c = slice(first, end)
            e.wait_ge(vec, base)
            me, mo = stats[:, c, 1], stats[:, c, 4]
            nc.vector.tensor_tensor(tmp[:, 0, c], me, mo, ALU.add).then_inc(vec, 1)
            nc.vector.tensor_tensor(tmp[:, 1, c], me, mo, ALU.subtract).then_inc(vec, 1)
            nc.vector.tensor_tensor(tmp[:, 2, c], stats[:, c, 2], stats[:, c, 5], ALU.add).then_inc(vec, 1)
            e.wait_ge(vec, base + 3)
            nc.vector.tensor_scalar(mean[:, c], tmp[:, 0, c], 0.5, None, ALU.mult).then_inc(vec, 1)
            nc.vector.scalar_tensor_tensor(out=tmp[:, 3, c], in0=tmp[:, 1, c], scalar=0.25, in1=tmp[:, 1, c],
                                           op0=ALU.mult, op1=ALU.mult).then_inc(vec, 1)
            nc.vector.tensor_scalar(tmp[:, 2, c], tmp[:, 2, c], 1.0 / T, LN_EPS, ALU.mult,
                                    ALU.add).then_inc(vec, 1)
            e.wait_ge(vec, base + NORM_STEPS)
            nc.vector.tensor_tensor(var[:, c], tmp[:, 2, c], tmp[:, 3, c], ALU.add).then_inc(ln_var, 1)
            e.wait_ge(ln_std, round_)
            nc.vector.reciprocal(rstd[:, c], rstd[:, c]).then_inc(ln_ready, 1)
            e.wait_ge(ln_ready, round_)

        def vector_prepare(e, n):
            if n == -AHEAD:
                dequantise(e, nc.vector, down_f, down_raw, down_scale, 2 * FF // QBLOCK, dequant_down)
            c = n + AHEAD + 1
            if c < X_CHUNKS:
                e.wait_ge(x_in[c], 16)
                for pair in range(c * EARLY, (c + 1) * EARLY):
                    vector_stats(e, pair, x_vec)
            if n == TAIL_NORM + 1:
                vector_norm(e, 3, 0, TAIL_NORM, ln_vec, n)
            if n == 0:
                vector_norm(e, 2, EARLY, PAIRS, x_vec, PAIRS + NORM_STEPS)

        def ff0_update(e, part):
            pairs = range(part * EARLY, (part + 1) * EARLY)
            for n in pairs:
                nc.vector.scalar_tensor_tensor(out=X[:, n, :], in0=ff[:, n, :], scalar=gain[:, n:n + 1],
                                               in1=X[:, n, :], op0=ALU.mult, op1=ALU.add).then_inc(f_upd, 1)
            for n in pairs:
                e.wait_ge(f_upd, n + 1)
                vector_stats(e, n)

        def vector_edges(e, n):
            if n == TAIL_NORM + 1:
                vector_norm(e, 7, 0, TAIL_NORM, ln_vec, 2 * PAIRS + 4 * NORM_STEPS + n)
            if n > 0:
                return
            part = n + AHEAD + 1
            if part < PAIRS // EARLY:
                ff0_update(e, part)
            if n == 0:
                vector_norm(e, 6, EARLY, PAIRS, ln_vec, 2 * PAIRS + 3 * NORM_STEPS)

        def vector_apply(pair_value, dst, signal):
            nc.vector.tensor_scalar(dst, X[:, pair_value, :], mean[:, bass.ds(pair_value, 1)],
                                    rstd[:, bass.ds(pair_value, 1)], ALU.subtract, ALU.mult).then_inc(signal, 1)

        def vector_attention(e, l, extra=None):
            s = L[l]
            b = att_b[l]
            win = win_of[l]

            def apply(pair):
                if not active(pair):
                    return
                if l == 0:
                    wait_job(e, s, l, "A", "v", at(pair, -RING), "filled")
                else:
                    wait_job(e, s, l, "A", "q", at(pair, -RING), "filled")
                vector_apply(num(pair), xn[:, pair[1], :], s["xn_ready"])

            def maximum(pair, h):
                if not active(pair):
                    return
                if h % HEADS == 0:
                    wait_job(e, s, l, *(("A", "max0"), ("B", "max1"))[h // HEADS], at(pair, -RING), "filled")
                e.wait_ge(s["scored"], num(pair) * HPP + h + 1)
                nc.vector.tensor_reduce(row_max[:, pair[1], h, :],
                                        bank_of(pair, h)[:, 0:2 * win].rearrange("p (b k) -> p b k", b=2),
                                        AX.X, ALU.max).then_inc(s["maxed"], 1)

            def rest_of(bk, name, pair, parts, rest, column):
                if not active(pair):
                    return
                e.wait_ge(s[f"{name}_high"], num(pair) + 1)
                wait_some(e, s[f"{name}_parts"], num(pair) - RING + 1)
                nc.vector.scalar_tensor_tensor(out=rest[:, pair[1], :], in0=job_bank[bk][:, 0:T],
                                               scalar=b[:, column:column + 1], in1=parts[:, pair[1], 0, :],
                                               op0=ALU.add, op1=ALU.subtract).then_inc(s[f"{bk}_read"], 1)

            def rotate(bk, name, pair, n, column):
                if not active(pair):
                    return
                e.wait_ge(s["turned"], num(pair) * 4 + 2 * n + 2)
                wait_some(e, s["rot_sum"], num(pair) * 2 - 1 + n)
                nc.vector.scalar_tensor_tensor(out=rot[:, 2 * n, :], in0=job_bank[bk][:, 0:T],
                                               scalar=b[:, column:column + 1], in1=rope[:, 0, :],
                                               op0=ALU.add, op1=ALU.mult).then_inc(s[f"{bk}_read"], 1)

            def normalise(pair, half):
                if not active(pair):
                    return
                wait_job(e, s, l, "A", f"heads{half}", pair, "filled")
                turned = job_bank["A"][:, :].rearrange("p (n c) -> p n c", c=32)
                nc.vector.reciprocal(rcp[:, half, :], turned[:, :, HD]).then_inc(s["rcp_done"], 1)
                e.wait_ge(s["rcp_done"], num(pair) * 2 + half + 1)
                wait_job(e, s, l, "B", "back", at(pair, -RING), "filled")
                nc.vector.tensor_tensor(
                    normed[:, pair[1], :, half * CH:(half + 1) * CH].rearrange("p b (h d) -> p b h d", d=HD),
                    turned[:, :, 0:HD].rearrange("p (b h) d -> p b h d", b=2),
                    rcp[:, half, :].rearrange("p (b h) -> p b h", b=2).unsqueeze(3)
                    .broadcast_to([P, 2, HEADS, HD]),
                    ALU.mult).then_inc(s["A_read"], 1)

            def update(pair):
                if not active(pair):
                    return
                last = "mix" if l == 0 else "out"
                wait_job(e, s, l, "B", last, pair, "filled")
                bias = b[:, 4:5] if l == 0 else out_bias[:, 1:2]
                nc.vector.scalar_tensor_tensor(out=X[:, num(pair), :], in0=job_bank["B"][:, 0:T], scalar=bias,
                                               in1=X[:, num(pair), :], op0=ALU.add,
                                               op1=ALU.add).then_inc(s["B_read"], 1)
                wait_job(e, s, l, "B", last, pair, "read")
                vector_stats(e, num(pair))

            tail = {3: lambda: normalise(TAIL, 1), 8: lambda: update(TAIL)}

            def iteration(r):
                p1, p3, m1 = at(r, 1), at(r, AHEAD), at(r, -1)
                for h in range(HPP):
                    if h == 5:
                        normalise(m1, 1)
                    if h == 6:
                        apply(at(r, AHEAD + 1))
                    if h == (14, 10)[l]:
                        update(m1)
                    if h == 14:
                        normalise(r, 0)
                    maximum(p1, h)
                    if h == 2 and l == 1:
                        rotate("A", "q", p3, 0, 0)
                    if h == 5 and l == 1:
                        rotate("B", "k", p3, 1, 1)
                    if h == 2 and l == 0:
                        rest_of("A", "q", p3, Qp, q_rest, 0)
                    if h == 4 and l == 0:
                        rest_of("B", "k", p3, Kp, k_rest, 1)
                    if l == 0 and h in (0, HEADS):
                        split_max(e, nc.vector, s, l, p1 if h else r, 1 - h // HEADS)

            apply((0, 0))
            iterations(e, iteration, extra and (lambda n: extra(e, n)), last=False)
            return tail

        @block.vector
        def _(e):
            nc.vector.memset(Ks[:, :, :, :].rearrange("p a h t -> p (a h t)").bitcast(i32), 0).then_inc(cleared_k, 1)
            e.wait_ge(x_in[0], 16)
            for pair in range(EARLY):
                vector_stats(e, pair, x_vec)
            vector_norm(e, 1, 0, EARLY, x_vec, EARLY)
            e.wait_ge(weights0_in, 2 * 16)
            tail = vector_attention(e, 0, vector_prepare)

            def ff0(pair):
                n, u = num(pair, FF0_RING), pair[1]
                if active(pair, FF0_RING):
                    wait_some(e, f_xT, n - FF0_RING + 1)
                    vector_apply(n, ff0_xn[u], f_xn)
                late = at(pair, -FF0_LAG[2], FF0_RING)
                n, u = num(late, FF0_RING), late[1]
                if active(late, FF0_RING):
                    e.wait_ge(f_sq, n + 1)
                    nc.vector.tensor_copy(ff[:, n, :], ff0_bank(late)[:, 0:T]).then_inc(f_keep, 1)

            ff0_steps(e, ff0, tail, lambda: vector_norm(e, 4, TAIL_NORM, PAIRS, ln_vec, PAIRS + NORM_STEPS))
            e.wait_ge(f_root, 1)
            nc.vector.tensor_scalar(tmp[:, 1, :], tmp[:, 0, :], FFN_EPS, None, ALU.max).then_inc(f_norm, 1)
            e.wait_ge(f_norm, 1)
            nc.vector.tensor_scalar(tmp[:, 3, :], tmp[:, 1, :], FFN_EPS, None, ALU.add).then_inc(f_step, 1)
            e.wait_ge(f_step, 1)
            nc.vector.reciprocal(tmp[:, 3, :], tmp[:, 3, :]).then_inc(f_step, 1)
            e.wait_ge(f_step, 2)
            e.wait_ge(f_tanh, 1)
            nc.vector.tensor_tensor(gain[:, :], tmp[:, 2, :], tmp[:, 3, :], ALU.mult).then_inc(f_step, 1)
            e.wait_ge(f_step, 3)
            nc.vector.tensor_tensor(tmp[:, 1, :], gain[:, :], tmp[:, 0, :], ALU.mult).then_inc(f_step, 1)
            e.wait_ge(f_step, 4)
            nc.vector.tensor_scalar(tmp[:, 1, :], tmp[:, 1, :], FFN_EPS, None, ALU.max).then_inc(f_step, 1)
            e.wait_ge(f_step, 5)
            nc.vector.reciprocal(tmp[:, 3, :], tmp[:, 1, :]).then_inc(f_step, 1)
            e.wait_ge(f_step, 6)
            nc.vector.tensor_scalar(tmp[:, 3, :], tmp[:, 3, :], MAX_NORM, 1.0, ALU.mult, ALU.min).then_inc(f_step, 1)
            e.wait_ge(f_step, 7)
            nc.vector.tensor_tensor(gain[:, :], gain[:, :], tmp[:, 3, :], ALU.mult).then_inc(f_step, 1)
            e.wait_ge(f_step, 8)
            e.wait_ge(f_keep, PAIRS)
            ff0_update(e, 0)
            vector_norm(e, 5, 0, EARLY, ln_vec, PAIRS + 2 * NORM_STEPS + EARLY)
            tail = vector_attention(e, 1, vector_edges)

            def norm_chunk(c):
                for j in range(CHUNK):
                    wait_some(e, g_xT, (c - 1) * CHUNK + j + 1)
                    vector_apply(c * CHUNK + j, chunk_xn[j], g_xn)

            def update_chunk(c):
                for j in range(CHUNK):
                    e.wait_ge(g_down, c * CHUNK + j + 1)
                    e.wait_ge(g_bias, c * CHUNK + j + 1)
                    nc.vector.tensor_tensor(X[:, c * CHUNK + j, :], bank[4 + j % 2][:, 0:T],
                                            X[:, c * CHUNK + j, :], ALU.add).then_inc(g_upd, 1)

            norm_chunk(0)
            for step in tail.values():
                step()
            norm_chunk(1)
            vector_norm(e, 8, TAIL_NORM, PAIRS, ln_vec, 3 * PAIRS + 5 * NORM_STEPS)
            with e.Fori(0, PAIRS // CHUNK - 2) as c:
                update_chunk(c)
                norm_chunk(c + 2)
            update_chunk(PAIRS // CHUNK - 2)
            update_chunk(PAIRS // CHUNK - 1)

        def pool_attention(e, l, extra=None):
            s = L[l]

            def split(name, pair, parts, rest, mid, done):
                if not active(pair):
                    return
                u = pair[1]
                bk = "A" if name == "q" else "B"
                if l == 0:
                    wait_apart(e, job_wait(s, l, bk, name, pair, "read"))
                    n, total = num(pair), 1
                else:
                    e.wait_ge(s[f"{name}_high"], num(pair) + 1)
                    nc.gpsimd.tensor_tensor(rest[:, u, :], rest[:, u, :], parts[:, u, 0, :],
                                            ALU.subtract).then_inc(s[mid], 1)
                    wait_apart(e, (s[mid], num(pair) * 2 + 1))
                    n, total = num(pair), 2
                nc.gpsimd.tensor_scalar(parts[:, u, 1, :], rest[:, u, :], 1.0, None,
                                        ALU.mult).then_inc(s[mid], 1)
                e.wait_ge(s[mid], (n + 1) * total)
                nc.gpsimd.tensor_tensor(parts[:, u, 2, :], rest[:, u, :], parts[:, u, 1, :],
                                        ALU.subtract).then_inc(s[done], 1)

            def rot_sum(bk, name, pair, n, rest):
                if not active(pair):
                    return
                e.wait_ge(s["turned"], num(pair) * 4 + 2 * n + 2)
                nc.gpsimd.tensor_tensor(rot[:, 2 * n + 1, :], rot[:, 2 * n + 1, :], rope[:, 1, :],
                                        ALU.mult).then_inc(s["rot_mul"], 1)
                wait_job(e, s, l, bk, name, pair, "read")
                e.wait_ge(s["rot_mul"], num(pair) * 2 + n + 1)
                wait_some(e, s[f"{name}_parts"], num(pair) - RING + 1)
                nc.gpsimd.tensor_tensor(rest[:, pair[1], :], rot[:, 2 * n, :], rot[:, 2 * n + 1, :],
                                        ALU.add).then_inc(s["rot_sum"], 1)

            def mask_group(pair, g):
                if not active(pair):
                    return
                wait_apart(e, (s["exped"], num(pair) * HPP + 4 * g + 4))
                first = (g % 2) * 4
                half = P // 2

                def keep(blk, lo, width, base, sign):
                    part = probs[:, first:first + 4, blk * WIN + lo:blk * WIN + lo + width]
                    return nc.gpsimd.affine_select(out=part, in_=part, compare_op=ALU.is_ge, fill=0.0, base=base,
                                                   pattern=[[0, 4], [-sign, width]], channel_multiplier=sign)

                keep(0, 0, half, BAND, -1).then_inc(s["mask_step"], 1)
                keep(0, half, P, BAND - half, 1).then_inc(s["mask_step"], 1)
                keep(1, 0, P, BAND - (P - BAND), -1).then_inc(s["mask_step"], 1)
                wait_apart(e, (s["mask_step"], (num(pair) * 4 + g + 1) * 3))
                keep(1, P, half, P + BAND - BAND - P + 0, 1).then_inc(s["masked"], 1)

            def gate(pair):
                if not active(pair):
                    return
                wait_job(e, s, l, "B", "out", pair, "read")
                e.wait_ge(s[f"side_in{pair[1]}"], (pair[0] + 1) * 16)
                wait_job(e, s, l, "B", "mix", at(pair, -1), "filled")
                nc.gpsimd.tensor_tensor(gated, relu_out, side[:, pair[1], :],
                                        ALU.mult).then_inc(s["gated"], 1)

            def iteration(r):
                p1, p3, m1 = at(r, 1), at(r, AHEAD), at(r, -1)
                if l == 0:
                    mask_group(m1, 3)
                    mask_group(r, 0)
                    split("q", p3, Qp, q_rest, "q_mid", "q_parts")
                    mask_group(r, 1)
                    split("k", p3, Kp, k_rest, "k_mid", "k_parts")
                    gate(m1)
                    mask_group(r, 2)
                else:
                    rot_sum("A", "q", p3, 0, q_rest)
                    rot_sum("B", "k", p3, 1, k_rest)
                    split("q", p3, Qp, q_rest, "q_mid", "q_parts")
                    split_max(e, nc.gpsimd, s, l, p1, 0)
                    split("k", p3, Kp, k_rest, "k_mid", "k_parts")
                    split_max(e, nc.gpsimd, s, l, p1, 1)

            iterations(e, iteration, extra and (lambda n: extra(e, n)), last=(l == 0))

        def pool_prepare(e, n):
            if n != -AHEAD:
                return
            dequantise(e, nc.gpsimd, up_f, up_raw, up_scale, HB * T // QBLOCK, dequant_up)
            for blk in range(2):
                nc.gpsimd.tensor_tensor(ff0_w[:, blk, :], ff0_w[:, blk, :], ff0_scale[:, :],
                                        ALU.mult).then_inc(ff0_scaled, 1)

        @block.gpsimd
        def _(e):
            nc.gpsimd.memset(Qs[:, :, :, :].rearrange("p a h t -> p (a h t)").bitcast(i32), 0).then_inc(cleared_q, 1)
            nc.gpsimd.memset(V[:, :, :, :, :], 0.0).then_inc(cleared_q, 1)
            e.wait_ge(cleared_q, 2)
            nc.gpsimd.memset(V[:, :, :, :, HD:HD + 1], 1.0).then_inc(cleared_q, 1)
            e.wait_ge(cleared_q, 3)
            e.wait_ge(cleared_k, 1)
            nc.gpsimd.memset(Ks[SHIFT_ROW:SHIFT_ROW + PARTS, :, :, :].rearrange("p a h t -> p (a h t)")
                             .bitcast(fp32), MINUS_ONES).then_inc(cleared_k, 1)
            e.wait_ge(cleared_k, 2)
            pool_attention(e, 0, pool_prepare)
            pool_attention(e, 1)

            def add_bias(c):
                for j in range(CHUNK):
                    e.wait_ge(g_xn, c * CHUNK + j + 1)
                    nc.gpsimd.tensor_tensor(X[:, c * CHUNK + j, :], X[:, c * CHUNK + j, :], down_b[:, :],
                                            ALU.add).then_inc(g_bias, 1)

            with e.Fori(0, PAIRS // CHUNK) as c:
                add_bias(c)


def _bd(m):
    import numpy as np
    z = np.zeros_like(m)
    return np.block([[m, z], [z, m]])


def _layouts(i):
    import numpy as np
    f = {k: np.asarray(v) for k, v in i.items()}
    dh = np.arange(CH).reshape(HEADS, HD).T.reshape(-1)
    w_in, b_in = f["L0_xattn_w_in"], f["L0_xattn_b_in"]
    wq, wk, wv = w_in[0:CH], w_in[CH:2 * CH], w_in[2 * CH:3 * CH]
    bq, bk, bv = b_in[0:CH], b_in[CH:2 * CH], b_in[2 * CH:3 * CH]
    w0 = [wq[dh].T, wk[dh].T, wv.T, f["L0_xattn_w_out"].T, f["L0_xattn_w_ct"]]
    b0 = [bq[dh], bk[dh], bv, f["L0_xattn_b_out"], f["L0_xattn_b_ct"]]
    wq, wk, bq, bk = f["L1_xattn_Wq"], f["L1_xattn_Wk"], f["L1_xattn_bq"], f["L1_xattn_bk"]
    w1 = [wq[dh].T, wk[dh].T, f["L1_xattn_Wv"].T, f["L1_xattn_Wo"].T]
    b1 = [bq[dh], bk[dh], f["L1_xattn_bv"], f["L1_xattn_bo"]]
    inv = (1.0 / 10000.0 ** (np.arange(0, HD, 2, dtype=np.float32) / HD)).astype(np.float32)
    ang = np.arange(T, dtype=np.float32)[None, :] * np.concatenate([inv, inv])[:, None]
    sign = np.where(np.arange(HD) < HD // 2, -1.0, 1.0)[:, None]
    cs = np.stack([np.cos(ang), np.sin(ang) * sign], 1).astype(np.float32)
    rope = np.tile(np.repeat(cs, HEADS, axis=0), (2, 1, 1))
    q = np.arange(P)[:, None]
    k = np.arange(WIN)[None, :]
    band = np.concatenate([np.where(abs((q + b * P) - (k + b * BAND)) <= BAND, 0.0, OUTSIDE) for b in range(2)], 1)
    c = np.ascontiguousarray

    def spread(per_sequence):
        m = per_sequence.reshape(2, HD, HEADS, *per_sequence.shape[1:])
        return m.swapaxes(0, 1).reshape(P, *per_sequence.shape[1:])

    w0 = [spread(_bd(w).T).T if n < 2 else _bd(w) for n, w in enumerate(w0)]
    w1 = [spread(_bd(w).T).T if n < 2 else _bd(w) for n, w in enumerate(w1)]
    b0 = [spread(np.tile(b, 2)) if n < 2 else np.tile(b, 2) for n, b in enumerate(b0)]
    b1 = [spread(np.tile(b, 2)) if n < 2 else np.tile(b, 2) for n, b in enumerate(b1)]
    rope = spread(rope)
    return {
        "x": f["x"], "ctx": f["ctx_2048"],
        "ident": np.eye(P, dtype=np.float32), "band": band.astype(np.float32),
        "rope": rope,
        "att_w0": c(np.stack(w0, 1)), "att_w1": c(np.stack(w1, 1)),
        "att_b0": c(np.stack(b0, 1)), "att_b1": c(np.stack(b1, 1)),
        "ff0_w": f["L0_ffn_weight"], "ff0_scale": f["L0_ffn_scale"],
        "down_b": f["L1_ffn_b_down"], "up_b": c(f["L1_ffn_b_up"].reshape(FF // P, P).T),
        "up_q": f["L1_ffn_w_up_q"], "up_scale": f["L1_ffn_w_up_scale"],
        "down_q": f["L1_ffn_w_down_q"], "down_scale": f["L1_ffn_w_down_scale"],
        "lora_in": c(np.concatenate([f["L1_ffn_w_up_lora_a"].T, f["L1_ffn_w_down_lora_a"].T], 1)),
        "lora_out": c(np.concatenate([f["L1_ffn_w_up_lora_b"], f["L1_ffn_w_down_lora_b"]], 1)),
    }


def kernel(**inputs):
    import numpy as np
    import concourse.bacc as bacc
    from concourse.bass_utils import run_bass_kernel_spmd

    nc = bacc.Bacc("TRN2", target_bir_lowering=False, num_devices=1)
    arrays, aps = {}, {}
    for name, value in _layouts(inputs).items():
        value = np.ascontiguousarray(value)
        arrays[f"in_{name}"] = value
        aps[name] = nc.dram_tensor(f"in_{name}", value.shape, mybir.dt.from_np(value.dtype),
                                   kind="ExternalInput").ap()
    out = nc.dram_tensor("out", (BATCH, CH, T), mybir.dt.float32, kind="ExternalOutput").ap()
    build(nc, aps, out)
    result = run_bass_kernel_spmd(nc, [arrays], core_ids=[0])
    return result.results[0]["out"]
```
